# Optimizing a Trainium2 kernel written in Bass

```python
import numpy as np
import jax
import jax.numpy as jnp

def _softmax(x, axis=-1):
    return jax.nn.softmax(x, axis=axis)

def _gelu(x):
    return jax.nn.gelu(x, approximate=True)

def _silu(x):
    return jax.nn.silu(x)

def _sigmoid(x):
    return jax.nn.sigmoid(x)

def _layernorm(x, axis=-1, eps=1e-05):
    m = jnp.mean(x, axis=axis, keepdims=True)
    v = jnp.var(x, axis=axis, keepdims=True)
    return (x - m) / jnp.sqrt(v + eps)

def _scatter_add(tgt, idx, src, axis=0):
    return tgt.at[idx].add(src)

def _segment_sum(src, seg, n):
    return jax.ops.segment_sum(src, seg, n)
kernel_name = 'mk_adj_preln_d4_adj_r2_1ae990'

def setup_inputs(seed: int=0):
    np.random.seed(seed)
    _w = jnp.asarray

    def _rec_inputs():
        import jax
        import jax.numpy as jnp
        _gk = jax.random.key(seed)
        x = -0.0002928 + 1 * jax.random.normal(jax.random.fold_in(_gk, 1), (1354, 256), jnp.float32)
        _a = jax.random.bernoulli(jax.random.fold_in(_gk, 2), 0.0014771, (1354, 1354))
        _a = jnp.logical_or(_a, jnp.swapaxes(_a, -1, -2))
        _a = jnp.logical_or(_a, jnp.eye(1354, dtype=bool))
        adj = _a.astype(jnp.int32)
        return (x, adj)
    x, adj = _rec_inputs()

    def _L0_gnn_setup():
        import jax, jax.numpy as jnp
        import numpy as np
        EPS = 1e-08
        key = jax.random.key(seed)
        k1, k2, k3 = jax.random.split(key, 3)
        N, IN_DIM, OUT_DIM = (4096, 256, 256)
        h = jax.random.normal(k1, (N, IN_DIM), dtype=jnp.float32)
        adj = jax.random.randint(k2, (N, N), 0, 2, dtype=jnp.int32)
        W = jax.random.normal(k3, (OUT_DIM, IN_DIM), dtype=jnp.float32) * (1.0 / np.sqrt(IN_DIM))
        return {'h': h, 'adj': adj, 'W': W}
    _L0_gnn_all = _L0_gnn_setup()
    _L0_gnn_in = {k: v for k, v in _L0_gnn_all.items() if k in ('W',)}
    del _L0_gnn_all

    def _L1_gnn_setup():
        import jax, jax.numpy as jnp
        import numpy as np
        N, NFEAT, NHID, NHEADS, OUT_DIM = (2048, 256, 64, 8, 256)
        ALPHA = 0.2
        NEG = -9000000000000000.0

        def _gat_heads(x, adj_mask, W, a):
            O = W.shape[-1]
            Wh = jnp.einsum('nf,hfo->hno', x, W)
            src = jnp.einsum('hno,ho->hn', Wh, a[:, :O])
            dst = jnp.einsum('hno,ho->hn', Wh, a[:, O:])
            e = jax.nn.leaky_relu(src[:, :, None] + dst[:, None, :], ALPHA)
            e = jnp.where(adj_mask[None, :, :], e, NEG)
            attn = jax.nn.softmax(e, axis=-1)
            return jnp.einsum('hnm,hmo->hno', attn, Wh)
        key = jax.random.key(seed)
        ks = jax.random.split(key, 10)
        s = 0.1
        x = jax.random.normal(ks[0], (N, NFEAT), jnp.float32)
        adj = jax.random.randint(ks[1], (N, N), 0, 2, jnp.int32)
        W1 = jax.random.normal(ks[2], (NHEADS, NFEAT, NHID), jnp.float32) * s
        a1 = jax.random.normal(ks[3], (NHEADS, 2 * NHID), jnp.float32) * s
        Wo = jax.random.normal(ks[4], (NHEADS * NHID, OUT_DIM), jnp.float32) * s
        ao = jax.random.normal(ks[5], (2 * OUT_DIM,), jnp.float32) * s
        lin1_w = jax.random.normal(ks[6], (OUT_DIM, 512), jnp.float32) * s
        lin1_b = jnp.zeros((512,), jnp.float32)
        lin2_w = jax.random.normal(ks[7], (512, 256), jnp.float32) * s
        lin2_b = jnp.zeros((256,), jnp.float32)
        return dict(x=x, adj=adj, W1=W1, a1=a1, Wo=Wo, ao=ao, lin1_w=lin1_w, lin1_b=lin1_b, lin2_w=lin2_w, lin2_b=lin2_b)
    _L1_gnn_all = _L1_gnn_setup()
    _L1_gnn_in = {k: v for k, v in _L1_gnn_all.items() if k in ('W1', 'a1', 'Wo', 'ao', 'lin1_w', 'lin1_b', 'lin2_w', 'lin2_b')}
    del _L1_gnn_all

    def _L2_gnn_setup():
        import jax, jax.numpy as jnp
        import numpy as np
        N = 2048
        STATE_DIM = 256
        OUTPUT_DIM = 256
        N_STEPS = 5
        W_STD = 0.02

        def _lin_params(key, out_dim, in_dim):
            W = jax.random.normal(key, (out_dim, in_dim), dtype=jnp.float32) * W_STD
            b = jnp.zeros((out_dim,), dtype=jnp.float32)
            return (W, b)
        key = jax.random.key(seed)
        ks = jax.random.split(key, 10)
        prop_state = jax.random.normal(ks[0], (N, STATE_DIM), dtype=jnp.float32)
        A = jax.random.randint(ks[1], (N, N), 0, 2, dtype=jnp.int64)
        in_W, in_b = _lin_params(ks[2], STATE_DIM, STATE_DIM)
        out_W, out_b = _lin_params(ks[3], STATE_DIM, STATE_DIM)
        r_W, r_b = _lin_params(ks[4], STATE_DIM, 3 * STATE_DIM)
        z_W, z_b = _lin_params(ks[5], STATE_DIM, 3 * STATE_DIM)
        h_W, h_b = _lin_params(ks[6], STATE_DIM, 3 * STATE_DIM)
        o1_W, o1_b = _lin_params(ks[7], STATE_DIM, STATE_DIM)
        o2_W, o2_b = _lin_params(ks[8], OUTPUT_DIM, STATE_DIM)
        return {'prop_state': prop_state, 'A': A, 'in_W': in_W, 'in_b': in_b, 'out_W': out_W, 'out_b': out_b, 'r_W': r_W, 'r_b': r_b, 'z_W': z_W, 'z_b': z_b, 'h_W': h_W, 'h_b': h_b, 'o1_W': o1_W, 'o1_b': o1_b, 'o2_W': o2_W, 'o2_b': o2_b}
    _L2_gnn_all = _L2_gnn_setup()
    _L2_gnn_in = {k: v for k, v in _L2_gnn_all.items() if k in ('in_W', 'in_b', 'out_W', 'out_b', 'r_W', 'r_b', 'z_W', 'z_b', 'h_W', 'h_b', 'o1_W', 'o1_b', 'o2_W', 'o2_b')}
    del _L2_gnn_all

    def _L3_gnn_setup():
        import jax, jax.numpy as jnp
        import numpy as np
        N, IN_DIM, OUT_DIM = (2048, 256, 256)
        H, D = (8, OUT_DIM // 8)
        ALPHA = 0.2
        NEG = -9000000000000000.0
        EPS = 1e-05
        key = jax.random.key(seed)
        k1, k2, k3, k4 = jax.random.split(key, 4)
        x = jax.random.normal(k1, (N, IN_DIM), dtype=jnp.float32)
        adj = jax.random.randint(k2, (N, N), 0, 2, dtype=jnp.int32)
        W = jax.random.normal(k3, (OUT_DIM, IN_DIM), dtype=jnp.float32) / np.sqrt(IN_DIM)
        a = jax.random.normal(k4, (2 * D,), dtype=jnp.float32) / np.sqrt(2 * D)
        gamma = jnp.ones((OUT_DIM,), dtype=jnp.float32)
        beta = jnp.zeros((OUT_DIM,), dtype=jnp.float32)
        return {'x': x, 'adj': adj, 'W': W, 'a': a, 'gamma': gamma, 'beta': beta}
    _L3_gnn_all = _L3_gnn_setup()
    _L3_gnn_in = {k: v for k, v in _L3_gnn_all.items() if k in ('W', 'a', 'gamma', 'beta')}
    del _L3_gnn_all
    return {'x': x, 'adj': adj, 'L0_gnn_W': _L0_gnn_in['W'], 'L1_gnn_W1': _L1_gnn_in['W1'], 'L1_gnn_a1': _L1_gnn_in['a1'], 'L1_gnn_Wo': _L1_gnn_in['Wo'], 'L1_gnn_ao': _L1_gnn_in['ao'], 'L1_gnn_lin1_w': _L1_gnn_in['lin1_w'], 'L1_gnn_lin1_b': _L1_gnn_in['lin1_b'], 'L1_gnn_lin2_w': _L1_gnn_in['lin2_w'], 'L1_gnn_lin2_b': _L1_gnn_in['lin2_b'], 'L2_gnn_in_W': _L2_gnn_in['in_W'], 'L2_gnn_in_b': _L2_gnn_in['in_b'], 'L2_gnn_out_W': _L2_gnn_in['out_W'], 'L2_gnn_out_b': _L2_gnn_in['out_b'], 'L2_gnn_r_W': _L2_gnn_in['r_W'], 'L2_gnn_r_b': _L2_gnn_in['r_b'], 'L2_gnn_z_W': _L2_gnn_in['z_W'], 'L2_gnn_z_b': _L2_gnn_in['z_b'], 'L2_gnn_h_W': _L2_gnn_in['h_W'], 'L2_gnn_h_b': _L2_gnn_in['h_b'], 'L2_gnn_o1_W': _L2_gnn_in['o1_W'], 'L2_gnn_o1_b': _L2_gnn_in['o1_b'], 'L2_gnn_o2_W': _L2_gnn_in['o2_W'], 'L2_gnn_o2_b': _L2_gnn_in['o2_b'], 'L3_gnn_W': _L3_gnn_in['W'], 'L3_gnn_a': _L3_gnn_in['a'], 'L3_gnn_gamma': _L3_gnn_in['gamma'], 'L3_gnn_beta': _L3_gnn_in['beta']}

def reference(x, adj, L0_gnn_W, L1_gnn_W1, L1_gnn_a1, L1_gnn_Wo, L1_gnn_ao, L1_gnn_lin1_w, L1_gnn_lin1_b, L1_gnn_lin2_w, L1_gnn_lin2_b, L2_gnn_in_W, L2_gnn_in_b, L2_gnn_out_W, L2_gnn_out_b, L2_gnn_r_W, L2_gnn_r_b, L2_gnn_z_W, L2_gnn_z_b, L2_gnn_h_W, L2_gnn_h_b, L2_gnn_o1_W, L2_gnn_o1_b, L2_gnn_o2_W, L2_gnn_o2_b, L3_gnn_W, L3_gnn_a, L3_gnn_gamma, L3_gnn_beta):
    import jax
    import jax.numpy as jnp

    def _L0_gnn_ref(h, adj, W):
        import jax, jax.numpy as jnp
        import numpy as np
        EPS = 1e-08
        Wh = h @ W.T
        N = Wh.shape[0]
        norms = jnp.linalg.norm(Wh, axis=1, keepdims=True)
        sim = Wh @ Wh.T / (norms * norms.T + EPS)
        mask = (adj > 0) | jnp.eye(N, dtype=bool)
        sim_masked = jnp.where(mask, sim, -jnp.inf)
        alpha = jax.nn.softmax(sim_masked, axis=1)
        return alpha @ Wh

    def _L1_gnn_ref(x, adj, W1, a1, Wo, ao, lin1_w, lin1_b, lin2_w, lin2_b):
        import jax, jax.numpy as jnp
        import numpy as np
        N, NFEAT, NHID, NHEADS, OUT_DIM = (2048, 256, 64, 8, 256)
        ALPHA = 0.2
        NEG = -9000000000000000.0

        def _gat_heads(x, adj_mask, W, a):
            O = W.shape[-1]
            Wh = jnp.einsum('nf,hfo->hno', x, W)
            src = jnp.einsum('hno,ho->hn', Wh, a[:, :O])
            dst = jnp.einsum('hno,ho->hn', Wh, a[:, O:])
            e = jax.nn.leaky_relu(src[:, :, None] + dst[:, None, :], ALPHA)
            e = jnp.where(adj_mask[None, :, :], e, NEG)
            attn = jax.nn.softmax(e, axis=-1)
            return jnp.einsum('hnm,hmo->hno', attn, Wh)
        mask = adj > 0
        h = jax.nn.elu(_gat_heads(x, mask, W1, a1))
        x1 = jnp.transpose(h, (1, 0, 2)).reshape(x.shape[0], -1)
        h2 = _gat_heads(x1, mask, Wo[None], ao[None])[0]
        out = jax.nn.elu(h2)
        out = jax.nn.relu(out @ lin1_w + lin1_b)
        return out @ lin2_w + lin2_b

    def _L2_gnn_ref(prop_state, A, in_W, in_b, out_W, out_b, r_W, r_b, z_W, z_b, h_W, h_b, o1_W, o1_b, o2_W, o2_b):
        import jax, jax.numpy as jnp
        import numpy as np
        N = 2048
        STATE_DIM = 256
        OUTPUT_DIM = 256
        N_STEPS = 5
        W_STD = 0.02

        def _lin_params(key, out_dim, in_dim):
            W = jax.random.normal(key, (out_dim, in_dim), dtype=jnp.float32) * W_STD
            b = jnp.zeros((out_dim,), dtype=jnp.float32)
            return (W, b)
        Af = A.astype(prop_state.dtype)
        AfT = Af.T
        state = prop_state
        for _ in range(N_STEPS):
            s_in = state @ in_W.T + in_b
            s_out = state @ out_W.T + out_b
            a_in = Af @ s_in
            a_out = AfT @ s_out
            a = jnp.concatenate([a_in, a_out, state], axis=-1)
            r = jax.nn.sigmoid(a @ r_W.T + r_b)
            z = jax.nn.sigmoid(a @ z_W.T + z_b)
            joined = jnp.concatenate([a_in, a_out, r * state], axis=-1)
            h_hat = jnp.tanh(joined @ h_W.T + h_b)
            state = (1.0 - z) * state + z * h_hat
        out = jnp.tanh(state @ o1_W.T + o1_b) @ o2_W.T + o2_b
        return out

    def _L3_gnn_ref(x, adj, W, a, gamma, beta):
        import jax, jax.numpy as jnp
        import numpy as np
        N, IN_DIM, OUT_DIM = (2048, 256, 256)
        H, D = (8, OUT_DIM // 8)
        ALPHA = 0.2
        NEG = -9000000000000000.0
        EPS = 1e-05
        n = x.shape[0]
        Wh = (x @ W.T).reshape(n, H, D)
        a_src, a_dst = (a[:D], a[D:])
        s_src = jnp.einsum('jhd,d->jh', Wh, a_src)
        s_dst = jnp.einsum('ihd,d->ih', Wh, a_dst)
        e = jax.nn.leaky_relu(s_dst[:, None, :] + s_src[None, :, :], negative_slope=ALPHA)
        e = jnp.where((adj > 0)[:, :, None], e, NEG)
        attn = jax.nn.softmax(e, axis=1)
        h_prime = jnp.einsum('ijh,jhd->ihd', attn, Wh).reshape(n, H * D)
        mean = jnp.mean(h_prime, axis=0)
        var = jnp.var(h_prime, axis=0)
        h_prime = gamma * (h_prime - mean) * jax.lax.rsqrt(var + EPS) + beta
        return jax.nn.relu(h_prime)
    h = jnp.maximum(_layernorm(x, axis=-1), 0.0)
    x = x + _L0_gnn_ref(h, adj, L0_gnn_W)
    h = jnp.maximum(_layernorm(x, axis=-1), 0.0)
    x = x + _L1_gnn_ref(h, adj, L1_gnn_W1, L1_gnn_a1, L1_gnn_Wo, L1_gnn_ao, L1_gnn_lin1_w, L1_gnn_lin1_b, L1_gnn_lin2_w, L1_gnn_lin2_b)
    h = jnp.maximum(_layernorm(x, axis=-1), 0.0)
    x = x + _L2_gnn_ref(h, adj, L2_gnn_in_W, L2_gnn_in_b, L2_gnn_out_W, L2_gnn_out_b, L2_gnn_r_W, L2_gnn_r_b, L2_gnn_z_W, L2_gnn_z_b, L2_gnn_h_W, L2_gnn_h_b, L2_gnn_o1_W, L2_gnn_o1_b, L2_gnn_o2_W, L2_gnn_o2_b)
    h = jnp.maximum(_layernorm(x, axis=-1), 0.0)
    x = x + _L3_gnn_ref(h, adj, L3_gnn_W, L3_gnn_a, L3_gnn_gamma, L3_gnn_beta)
    return x

_drawn_inputs = setup_inputs


def setup_inputs(seed=0):
    import zlib

    import numpy as np

    out = dict(_drawn_inputs(seed))
    spreads = {'L1_gnn_lin1_b': (0.0, 0.1),
     'L1_gnn_lin2_b': (0.0, 0.1),
     'L2_gnn_in_b': (0.0, 0.8),
     'L2_gnn_out_b': (0.0, 0.8),
     'L2_gnn_r_b': (0.0, 0.8),
     'L2_gnn_z_b': (0.0, 0.8),
     'L2_gnn_h_b': (0.0, 0.8),
     'L2_gnn_o1_b': (0.0, 0.632),
     'L2_gnn_o2_b': (0.0, 0.1),
     'L3_gnn_gamma': (1.0, 0.2),
     'L3_gnn_beta': (0.0, 0.313)}
    factors = {'L2_gnn_in_W': 8.0,
     'L2_gnn_out_W': 8.0,
     'L2_gnn_r_W': 8.0,
     'L2_gnn_z_W': 8.0,
     'L2_gnn_h_W': 5.489,
     'L2_gnn_o1_W': 5.035,
     'L2_gnn_o2_W': 3.223}
    for name, (base, spread) in spreads.items():
        noise = np.random.default_rng([zlib.crc32(name.encode()), seed]).standard_normal(out[name].shape)
        drawn = base * np.exp(spread * noise) if base else spread * noise
        out[name] = jnp.asarray(drawn.astype(out[name].dtype))
    for name, factor in factors.items():
        out[name] = (out[name] * factor).astype(out[name].dtype)
    return out
```

```python
import concourse.bass as bass
from concourse import mybir
from contextlib import ExitStack

F32 = mybir.dt.float32
F32R = mybir.dt.float32r
F16 = mybir.dt.float16
I32 = mybir.dt.int32
ALU = mybir.AluOpType
ACT = mybir.ActivationFunctionType
AX = mybir.AxisListType

N, D = 1354, 256
NT = (N + 127) // 128
NP = NT * 128
TAIL = N - (NT - 1) * 128
CH = [(0, 512), (512, 512), (1024, NP - 1024)]
CHV = [(0, 512), (512, 512), (1024, N - 1024)]


class Scope:

    def __init__(self, nc, ctx, tag):
        self.nc, self.ctx, self.tag, self.sems = nc, ctx, tag, []

    def sb(self, name, shape, dt):
        return self.ctx.enter_context(self.nc.sbuf_tensor(f"{self.tag}_{name}", shape, dt))

    def ps(self, name, shape, dt):
        return self.ctx.enter_context(self.nc.psum_tensor(f"{self.tag}_{name}", shape, dt))

    def sem(self, name):
        self.sems.append(self.nc.alloc_semaphore(f"{self.tag}_{name}"))
        return self.sems[-1]

    def block(self):
        self.ctx.callback(self.clear)
        return self.ctx.enter_context(self.nc.Block())

    def clear(self):
        self.nc.clear_and_free_semaphores(self.sems)
        self.nc.all_engine_barrier()


class Chain:

    def __init__(self, eng, sem):
        self.eng, self.sem, self.n = eng, sem, 0

    def done(self, ins):
        self.n += 1
        ins.then_inc(self.sem, 1)

    def wait(self):
        self.eng.wait_ge(self.sem, self.n)

    def step(self, ins):
        self.done(ins)
        self.wait()


def load_graph(nc, g, x_dram, adj_dram):
    with ExitStack() as ctx:
        s = Scope(nc, ctx, "load")
        NS = 3
        stage = s.sb("stage", [128, NS, N], I32)
        tp8 = [s.ps(f"tp8_{i}", [128, 8, 128], F16) for i in range(2)]
        tp3 = [s.ps(f"tp3_{i}", [128, NT - 8, 128], F16) for i in range(2)]
        arrived = [s.sem(f"arrived{i}") for i in range(NS)]
        x_in, cleared, ident_ok, even_ok, odd_ok, pad_ok = (
            s.sem(k) for k in ("x_in", "cleared", "ident_ok", "even_ok", "odd_ok", "pad_ok"))
        turned, out8, out3 = s.sem("turned"), s.sem("out8"), s.sem("out3")
        block = s.block()

        def rows(t):
            return 128 if t < NT - 1 else TAIL

        @block.sync
        def _(sp):
            for t in range(NT):
                if t >= NS:
                    u = t - NS
                    sp.wait_ge(even_ok if u % 2 == 0 else odd_ok, u // 2 + 1)
                sp.dma_start(stage[0:rows(t), t % NS, :],
                             adj_dram[t * 128:t * 128 + rows(t), :]).then_inc(arrived[t % NS], 16)

        @block.gpsimd
        def _(pool):
            fills = [(g.A[:, :, N:NP], 0.0), (g.A[64:128, NT - 1, 0:N], 0.0), (g.x[64:128, NT - 1, :], 0.0),
                     (g.ident[:, :], 0.0), (g.ident16[:, :], 0.0), (g.ones[:, :], 1.0)]
            for n, (region, value) in enumerate(fills):
                pool.memset(region, value).then_inc(cleared, 1)
                pool.wait_ge(cleared, n + 1)
            for m in (g.ident, g.ident16):
                pool.affine_select(out=m[:, :], in_=m[:, :], compare_op=ALU.not_equal, fill=1.0, base=0,
                                   pattern=[[-1, 128]], channel_multiplier=1).then_inc(ident_ok, 1)
            pool.wait_ge(ident_ok, 2)
            pool.tensor_copy(g.A[:, NT - 1, N:NP], g.ident16[:, TAIL:128]).then_inc(pad_ok, 1)

        def convert(eng, copy, t, ok):
            if t == NT - 1:
                eng.wait_ge(cleared, 6)
            eng.wait_ge(arrived[t % NS], 16 * (t // NS + 1))
            copy(g.A[0:rows(t), t, 0:N], stage[0:rows(t), t % NS, :]).then_inc(ok, 1)

        @block.scalar
        def _(act):
            act.dma_start(g.x[:, 0:NT - 1, :],
                          x_dram[0:(NT - 1) * 128, :].rearrange("(t p) f -> p t f", p=128)).then_inc(x_in, 16)
            act.wait_ge(cleared, 3)
            act.dma_start(g.x[0:TAIL, NT - 1, :], x_dram[(NT - 1) * 128:N, :]).then_inc(x_in, 16)
            for r in range(NT):
                if r % 2 == 1:
                    convert(act, lambda o, i: act.activation(o, i, ACT.Copy), r, odd_ok)
                if r >= 1:
                    act.wait_ge(turned, r)
                    act.activation(g.AT[:, 8:NT, (r - 1) * 128:r * 128], tp3[(r - 1) % 2][:, :, :],
                                   ACT.Copy).then_inc(out3, 1)
            act.wait_ge(turned, NT)
            act.activation(g.AT[:, 8:NT, (NT - 1) * 128:NP], tp3[(NT - 1) % 2][:, :, :],
                           ACT.Copy).then_inc(out3, 1)
            act.wait_ge(x_in, 32)

        @block.vector
        def _(dve):
            for r in range(NT):
                if r % 2 == 0:
                    convert(dve, dve.tensor_copy, r, even_ok)
                if r >= 1:
                    dve.wait_ge(turned, r)
                    dve.tensor_copy(g.AT[:, 0:8, (r - 1) * 128:r * 128], tp8[(r - 1) % 2][:, :, :]).then_inc(out8, 1)
            dve.wait_ge(turned, NT)
            dve.tensor_copy(g.AT[:, 0:8, (NT - 1) * 128:NP], tp8[(NT - 1) % 2][:, :, :]).then_inc(out8, 1)

        @block.tensor
        def _(pe):
            pe.wait_ge(ident_ok, 2)
            pe.wait_ge(cleared, 6)
            pe.wait_ge(pad_ok, 1)
            for r in range(NT):
                pe.wait_ge(even_ok if r % 2 == 0 else odd_ok, r // 2 + 1)
                if r >= 2:
                    pe.wait_ge(out8, r - 1)
                    pe.wait_ge(out3, r - 1)
                for c in range(NT):
                    out = tp8[r % 2][:, c, :] if c < 8 else tp3[r % 2][:, c - 8, :]
                    mm = pe.transpose(out, g.A[:, r, c * 128:(c + 1) * 128], g.ident16[:, :])
                mm.then_inc(turned, 1)


def layernorm_relu(nc, g, tag):
    with ExitStack() as ctx:
        s = Scope(nc, ctx, tag)
        stats = s.sb("stats", [128, NT, 6], F32)
        mv = s.sb("mv", [128, NT, 2], F32)
        eps = s.sb("eps", [128, 1], F32)
        std, rstd, shift = (s.sb(k, [128, NT], F32) for k in ("std", "rstd", "shift"))
        h = s.sb("h", [128, NT, D], F32)
        tp = [s.ps(f"tp{i}", [128, 2, 256], F32) for i in range(3)]
        v, std_ok, scale_ok, h_ok, turned, out = (
            s.sem(k) for k in ("v", "std_ok", "scale_ok", "h_ok", "turned", "out"))
        pairs = [(a, min(2, NT - a)) for a in range(0, NT, 2)]
        block = s.block()

        @block.vector
        def _(dve):
            c = Chain(dve, v)
            c.done(dve.memset(eps[:, :], 1e-5))
            for t in range(NT):
                c.done(dve.bn_stats(stats[:, t, :], g.x[:, t, :]))
            c.wait()
            for t in range(NT):
                c.done(dve.bn_aggr(mv[:, t, :], stats[:, t, :]))
            c.wait()
            dve.wait_ge(std_ok, 1)
            c.step(dve.reciprocal(rstd[:, :], std[:, :]))
            dve.scalar_tensor_tensor(out=shift[:, :], in0=mv[:, :, 0], scalar=-1.0, in1=rstd[:, :],
                                     op0=ALU.mult, op1=ALU.mult).then_inc(scale_ok, 1)
            for n, (a, k) in enumerate(pairs):
                dve.wait_ge(turned, n + 1)
                dve.tensor_copy(g.hT[:, :, a * 128:(a + k) * 128], tp[n % 3][:, :, 0:k * 128]).then_inc(out, 1)

        @block.scalar
        def _(act):
            act.wait_ge(v, 1 + 2 * NT)
            act.activation(std[:, :], mv[:, :, 1], ACT.Sqrt, bias=eps[:, 0:1]).then_inc(std_ok, 1)
            act.wait_ge(scale_ok, 1)
            for t in range(NT):
                act.activation(h[:, t, :], g.x[:, t, :], ACT.Relu, bias=shift[:, t:t + 1],
                               scale=rstd[:, t:t + 1]).then_inc(h_ok, 1)

        @block.tensor
        def _(pe):
            for n, (a, k) in enumerate(pairs):
                if n >= 3:
                    pe.wait_ge(out, n - 2)
                pe.wait_ge(h_ok, a + k)
                for q in range(k):
                    for f in range(2):
                        mm = pe.transpose(tp[n % 3][:, f, q * 128:(q + 1) * 128],
                                          h[:, a + q, f * 128:(f + 1) * 128], g.ident[:, :])
                mm.then_inc(turned, 1)


def cosine_attention(nc, g, wT_dram):
    with ExitStack() as ctx:
        s = Scope(nc, ctx, "cos")
        wT = s.sb("wT", [128, 2, D], F32)
        wh = s.sb("wh", [128, NT, D + 1], F32)
        whT = s.sb("whT", [128, 2, NP], F32)
        nsq = s.sb("nsq", [128, NT], F32)
        norm = s.sb("norm", [128, NT], F32)
        norm_row = s.sb("norm_row", [128, NP], F32)
        diag = s.sb("diag", [128, NT, 128], F16)
        den = s.sb("den", [128, 2, NP], F32)
        sim = s.sb("sim", [128, 2, NP], F32)
        sqT = sim
        probs = s.sb("probs", [128, NT, NP], F32)
        rsum = s.sb("rsum", [128, NT], F32)
        bank = [s.ps(f"bank{i}", [128, 512], F32) for i in range(8)]
        w_in, wh_mm, wh_out, whT_mm, whT_out, sq_ok, nb_mm, norm_ok, nsq_ok = (
            s.sem(k) for k in ("w_in", "wh_mm", "wh_out", "whT_mm", "whT_out", "sq_ok", "nb_mm", "norm_ok", "nsq_ok"))
        dot_mm, dot_used, exp_ok, probs_ok, agg_mm, agg_out, v = (
            s.sem(k) for k in ("dot_mm", "dot_used", "exp_ok", "probs_ok", "agg_mm", "agg_out", "v"))
        block = s.block()
        blocks = [(m, c) for m in range(2) for c in range(3)]

        @block.sync
        def _(sp):
            sp.dma_start(wT[:, :, :], wT_dram.rearrange("(k p) o -> p k o", p=128)).then_inc(w_in, 16)

        @block.tensor
        def _(pe):
            pe.wait_ge(w_in, 16)
            for n, (m, c) in enumerate(blocks):
                a, w = CH[c]
                if n >= 3:
                    pe.wait_ge(whT_out, n - 2)
                for k in range(2):
                    mm = pe.matmul(bank[n % 3][:, 0:w], wT[:, k, m * 128:(m + 1) * 128], g.hT[:, k, a:a + w],
                                   start=k == 0, stop=k == 1)
                mm.then_inc(whT_mm, 1)
            for t in range(NT):
                if t >= 3:
                    pe.wait_ge(wh_out, t - 2)
                    pe.wait_ge(nsq_ok, t - 2)
                for k in range(2):
                    mm = pe.matmul(bank[3 + t % 3][:, 0:D], g.hT[:, k, t * 128:(t + 1) * 128], wT[:, k, :],
                                   start=k == 0, stop=k == 1)
                mm.then_inc(wh_mm, 1)
            pe.wait_ge(whT_out, 6)
            pe.wait_ge(sq_ok, 2)
            for c, (a, w) in enumerate(CH):
                for k in range(2):
                    mm = pe.matmul(bank[c][:, 0:w], g.ones[:, :], sqT[:, k, a:a + w], start=k == 0, stop=k == 1)
                mm.then_inc(nb_mm, 1)
            pe.wait_ge(norm_ok, 4)
            pe.wait_ge(wh_out, NT)
            pe.wait_ge(nsq_ok, NT)
            for t in range(NT):
                for c, (a, w) in enumerate(CH):
                    n = 3 * t + c
                    if n >= 6:
                        pe.wait_ge(dot_used, n - 5)
                    for k in range(2):
                        mm = pe.matmul(bank[n % 6][:, 0:w], whT[:, k, t * 128:(t + 1) * 128], whT[:, k, a:a + w],
                                       start=k == 0, stop=k == 1)
                    mm.then_inc(dot_mm, 1)
            pe.wait_ge(dot_used, 3 * NT)
            for r in range(NT):
                if r >= 8:
                    pe.wait_ge(agg_out, r - 7)
                for t in range(NT):
                    pe.wait_ge(probs_ok, t + 1)
                    mm = pe.matmul(bank[r % 8][:, 0:D + 1], probs[:, t, r * 128:(r + 1) * 128], wh[:, t, :],
                                   start=t == 0, stop=t == NT - 1)
                mm.then_inc(agg_mm, 1)

        @block.scalar
        def _(act):
            for n, (m, c) in enumerate(blocks):
                a, w = CH[c]
                act.wait_ge(whT_mm, n + 1)
                act.activation(whT[:, m, a:a + w], bank[n % 3][:, 0:w], ACT.Copy).then_inc(whT_out, 1)
            for t in range(NT):
                act.wait_ge(wh_out, t + 1)
                act.activation(probs[:, t, 0:D], bank[3 + t % 3][:, 0:D], ACT.Square,
                               accum_out=nsq[:, t:t + 1]).then_inc(nsq_ok, 1)
            act.wait_ge(nsq_ok, NT)
            act.activation(norm[:, :], nsq[:, :], ACT.Sqrt).then_inc(norm_ok, 1)
            for c, (a, w) in enumerate(CH):
                act.wait_ge(nb_mm, c + 1)
                act.activation(norm_row[:, a:a + w], bank[c][:, 0:w], ACT.Sqrt).then_inc(norm_ok, 1)
            for t in range(NT):
                act.wait_ge(dot_used, 3 * t + 3)
                act.activation(sim[:, t % 2, :], sim[:, t % 2, :], ACT.Exp).then_inc(exp_ok, 1)

        @block.gpsimd
        def _(pool):
            for m in range(2):
                pool.wait_ge(whT_out, 3 * m + 3)
                pool.tensor_tensor(sqT[:, m, :], whT[:, m, :], whT[:, m, :], ALU.mult).then_inc(sq_ok, 1)

        @block.vector
        def _(dve):
            c_ = Chain(dve, v)
            c_.done(dve.memset(wh[:, :, D:D + 1], 1.0))
            for t in range(NT):
                dve.wait_ge(wh_mm, t + 1)
                dve.tensor_copy(wh[:, t, 0:D], bank[3 + t % 3][:, 0:D]).then_inc(wh_out, 1)
            for t in range(NT):
                c_.done(dve.tensor_tensor(diag[:, t, :], g.AT[:, t, t * 128:(t + 1) * 128], g.ident16[:, :], ALU.max))
            dve.wait_ge(norm_ok, 4)

            def mask(t):
                dve.wait_ge(exp_ok, t + 1)
                c_.wait()
                dve.tensor_tensor(probs[:, t, :], sim[:, t % 2, :], g.AT[:, t, :], ALU.mult).then_inc(v, 1)
                c_.n += 1
                c_.wait()
                dve.tensor_tensor(probs[:, t, t * 128:(t + 1) * 128], sim[:, t % 2, t * 128:(t + 1) * 128],
                                  diag[:, t, :], ALU.mult).then_inc(probs_ok, 1)

            for t in range(NT):
                if t >= 2:
                    dve.wait_ge(dot_used, 3 * (t - 1))
                c_.step(dve.tensor_scalar(den[:, t % 2, :], norm_row[:, :], norm[:, t:t + 1], 1e-8, ALU.mult, ALU.add))
                c_.step(dve.reciprocal(den[:, t % 2, :], den[:, t % 2, :]))
                if t >= 2:
                    dve.wait_ge(probs_ok, t - 1)
                for c, (a, w) in enumerate(CH):
                    n = 3 * t + c
                    dve.wait_ge(dot_mm, n + 1)
                    ins = dve.tensor_tensor(sim[:, t % 2, a:a + w], bank[n % 6][:, 0:w], den[:, t % 2, a:a + w],
                                            ALU.mult)
                    ins.then_inc(dot_used, 1)
                if t >= 1:
                    mask(t - 1)
            mask(NT - 1)
            for r in range(NT):
                dve.wait_ge(agg_mm, r + 1)
                c_.step(dve.reciprocal(rsum[:, r:r + 1], bank[r % 8][:, D:D + 1]))
                dve.scalar_tensor_tensor(out=g.x[:, r, :], in0=bank[r % 8][:, 0:D], scalar=rsum[:, r:r + 1],
                                         in1=g.x[:, r, :], op0=ALU.mult, op1=ALU.add).then_inc(agg_out, 1)


def gat(nc, g, tag, inT, KT, w_dram, ai_dram, aj_dram, H, O, raw, val=None):
    HO, V1 = H * O, O + 1
    G = 4 if V1 <= 128 else 1
    groups = [(a, min(G, NT - a)) for a in range(0, NT, G)]
    per_chunk = 4 // G
    NB = 3 if G == 4 else 4
    with ExitStack() as ctx:
        s = Scope(nc, ctx, tag)
        w = s.sb("w", [128, KT, HO], F32)
        ab = s.sb("ab", [128, 2, HO], F32)
        prod = s.sb("prod", [128, HO], F32)
        wa = s.sb("wa", [128, KT, 2 * H], F32)
        wab = s.sb("wab", [128, KT, 128], F32)
        top = s.sb("top", [2 * H, 1], F32)
        dtop = s.sb("dtop", [2 * H, 2 * H], F32)
        topb = s.sb("topb", [128, 2 * H], F32)
        dn = s.sb("dn", [128, NT, H], F32)
        f2 = s.sb("f2", [128, NT, H], F32)
        hj = s.sb("hj", [128, NT, H], F32)
        if val is None:
            val = s.sb("val", [128, NT, H * V1], F32)
        row = s.sb("row", [128, 3, 512], F32)
        pt = [s.sb(f"pt{c}", [128, NT, CH[c][1]], F32) for c in range(3)]
        sb_ = [s.ps(f"sb{i}", [128, 512], F32) for i in range(3)]
        ag = [s.ps(f"ag{i}", [128, 512], F32) for i in range(NB)]
        v, w_in, wa_ok, sd_mm, top_ok, topb_mm, dn_mm, dn_ok, f_ok, wh_mm, val_ok = (
            s.sem(k) for k in ("v", "w_in", "wa_ok", "sd_mm", "top_ok", "topb_mm", "dn_mm", "dn_ok", "f_ok",
                               "wh_mm", "val_ok"))
        wab_ok, s_mm, relu_ok, row_ok, pt_ok, agg_mm, agg_out = (
            s.sem(k) for k in ("wab_ok", "s_mm", "relu_ok", "row_ok", "pt_ok", "agg_mm", "agg_out"))
        act_passed, pool_passed = s.sem("act_passed"), s.sem("pool_passed")
        block = s.block()

        def hold(eng, sem, value, passed):
            eng.wait_ge(sem, value)
            eng.sem_inc(passed, 1)

        def heads(eng, body):
            if H > 1:
                with eng.Fori(0, H - 1) as h:
                    body(h, False)
            body(H - 1, True)

        @block.sync
        def _(sp):
            sp.dma_start(w[:, :, :], w_dram.rearrange("(k p) o -> p k o", p=128)).then_inc(w_in, 16)
            for n, a in enumerate((ai_dram, aj_dram)):
                k = a.shape[0]
                for r in range(HO // k):
                    sp.dma_start(ab[:, n, r * k:(r + 1) * k], a.partition_broadcast(128)).then_inc(w_in, 16)

        n_in = 16 * (1 + HO // ai_dram.shape[0] + HO // aj_dram.shape[0])

        @block.tensor
        def _(pe):
            pe.wait_ge(wa_ok, 2 * KT)
            for c, (a, wd) in enumerate(CH):
                for k in range(KT):
                    mm = pe.matmul(sb_[c][0:2 * H, 0:wd], wa[:, k, :], inT[:, k, a:a + wd],
                                   start=k == 0, stop=k == KT - 1)
                mm.then_inc(sd_mm, 1)
            for t in range(NT):
                for k in range(KT):
                    mm = pe.matmul(ag[0][:, t * 2 * H:(t + 1) * 2 * H], inT[:, k, t * 128:(t + 1) * 128], wa[:, k, :],
                                   start=k == 0, stop=k == KT - 1)
            mm.then_inc(dn_mm, 1)
            pe.wait_ge(top_ok, 1)
            pe.matmul(ag[1][:, 0:2 * H], g.ones[0:2 * H, :], dtop[:, :], start=True, stop=True).then_inc(topb_mm, 1)
            for t in range(NT):
                if t < 2:
                    pe.wait_ge(dn_ok, 1)
                else:
                    pe.wait_ge(val_ok, t - 1)
                for k in range(KT):
                    mm = pe.matmul(ag[1 + t % 2][:, 0:HO], inT[:, k, t * 128:(t + 1) * 128], w[:, k, :],
                                   start=k == 0, stop=k == KT - 1)
                mm.then_inc(wh_mm, 1)

            def s_rows(h, c):
                a, wd = CH[c]
                pe.wait_ge(wab_ok, h + 1)
                if not (isinstance(h, int) and h == 0):
                    pe.wait_ge(row_ok, 3 * (h - 1) + c + 1)
                for k in range(KT):
                    mm = pe.matmul(sb_[c][:, 0:wd], wab[:, k, :], inT[:, k, a:a + wd], start=k == 0, stop=k == KT - 1)
                mm.then_inc(s_mm, 1)

            for c in range(3):
                s_rows(0, c)
            pe.wait_ge(val_ok, NT)

            def head(h, last):
                for c in range(3):
                    if not last:
                        s_rows(h + 1, c)
                    first = True
                    for q in range(per_chunk):
                        gi = c * per_chunk + q
                        if gi >= len(groups):
                            continue
                        a, k4 = groups[gi]
                        if H > 1 or gi >= NB:
                            pe.wait_ge(agg_out, len(groups) * h + gi + 1)
                        for e in range(k4):
                            off = (a + e) * 128 - CH[c][0]
                            for t in range(NT):
                                if first:
                                    pe.wait_ge(pt_ok, 3 * NT * h + NT * c + t + 1)
                                vals = val[:, t, bass.ds(h * V1, V1)] if H > 1 else val[:, t, :]
                                mm = pe.matmul(ag[gi % NB][:, e * V1:(e + 1) * V1], pt[c][:, t, off:off + 128],
                                               vals, start=t == 0, stop=t == NT - 1)
                            first = False
                        mm.then_inc(agg_mm, 1)

            heads(pe, head)

        @block.gpsimd
        def _(pool):
            pool.sem_inc(agg_out, NB)
            pool.wait_ge(wa_ok, 2 * KT)

            def copy(h):
                src = wa[:, :, bass.ds(h, 1)] if not isinstance(h, int) else wa[:, :, h:h + 1]
                pool.tensor_copy(wab[:, :, :], src.broadcast_to([128, KT, 128])).then_inc(wab_ok, 1)

            copy(0)

            def head(h, last):
                if not last:
                    hold(pool, s_mm, 3 * h + 3, pool_passed)
                    copy(h + 1)

            heads(pool, head)

        @block.scalar
        def _(act):
            act.wait_ge(dn_ok, 2)
            act.activation(f2[:, :, :], dn[:, :, :], ACT.Exp, scale=0.2).then_inc(f_ok, 1)
            act.activation(hj[:, :, :], dn[:, :, :], ACT.Exp, scale=0.8).then_inc(f_ok, 1)

            def rows(h, c):
                wd = CH[c][1]
                if isinstance(h, int):
                    bias = topb[:, H + h:H + h + 1]
                else:
                    bias = topb[:, bass.ds(h + H, 1)]
                hold(act, s_mm, 3 * h + c + 1, act_passed)
                act.activation(sb_[c][:, 0:wd], sb_[c][:, 0:wd], ACT.Relu, bias=bias).then_inc(relu_ok, 1)
                act.wait_ge(relu_ok, 3 * h + c + 1)
                if not (isinstance(h, int) and h == 0):
                    act.wait_ge(pt_ok, 3 * NT * (h - 1) + NT * (c + 1))
                act.activation(row[:, c, 0:wd], sb_[c][:, 0:wd], ACT.Exp, scale=-0.8).then_inc(row_ok, 1)

            for c in range(3):
                rows(0, c)

            def head(h, last):
                for c in range(3):
                    if not last:
                        rows(h + 1, c)
                    for q in range(per_chunk):
                        gi = c * per_chunk + q
                        if gi >= len(groups):
                            continue
                        a, k4 = groups[gi]
                        hold(act, agg_mm, len(groups) * h + gi + 1, act_passed)
                        dst = raw[:, a:a + k4, bass.ds(h * V1, V1)] if H > 1 else raw[:, a:a + k4, :]
                        act.activation(dst, ag[gi % NB][:, 0:k4 * V1].rearrange("p (e o) -> p e o", o=V1),
                                       ACT.Copy).then_inc(agg_out, 1)

            heads(act, head)

        @block.vector
        def _(dve):
            c_ = Chain(dve, v)
            dve.wait_ge(w_in, n_in)
            for n in range(2):
                for k in range(KT):
                    if n + k > 0:
                        dve.wait_ge(wa_ok, n * KT + k)
                    c_.step(dve.tensor_tensor(prod[:, :], w[:, k, :], ab[:, n, :], ALU.mult))
                    dve.tensor_reduce(wa[:, k, n * H:(n + 1) * H], prod[:, :].rearrange("p (h o) -> p h o", h=H),
                                      axis=AX.X, op=ALU.add).then_inc(wa_ok, 1)
            tops = prod[0:2 * H, 0:3]
            dve.wait_ge(wa_ok, 2 * KT)
            for c, (a, wd) in enumerate(CHV):
                dve.wait_ge(sd_mm, c + 1)
                c_.done(dve.reduce_max(tops[:, c:c + 1], sb_[c][0:2 * H, 0:wd], AX.X))
            c_.wait()
            c_.step(dve.reduce_max(top[:, :], tops, AX.X))
            dve.tensor_scalar(dtop[:, :], g.ident[0:2 * H, 0:2 * H], top[:, 0:1], None, ALU.mult).then_inc(top_ok, 1)
            dve.wait_ge(topb_mm, 1)
            dve.wait_ge(dn_mm, 1)
            c_.step(dve.tensor_copy(topb[:, :], ag[1][:, 0:2 * H]))
            dview = ag[0][:, 0:NT * 2 * H].rearrange("p (t h) -> p t h", h=2 * H)[:, :, H:2 * H]
            tb = topb[:, H:2 * H].unsqueeze(1).broadcast_to([128, NT, H])
            dve.tensor_tensor(dn[:, :, :], dview, tb, ALU.subtract).then_inc(dn_ok, 2)
            dve.wait_ge(f_ok, 2)
            for t in range(NT):
                dve.wait_ge(wh_mm, t + 1)
                vv = val[:, t, :].rearrange("p (h o) -> p h o", o=V1)
                fb = f2[:, t, :].unsqueeze(2)
                c_.done(dve.tensor_copy(vv[:, :, O:V1], fb))
                dve.wait_ge(v, c_.n)
                dve.tensor_tensor(vv[:, :, 0:O], ag[1 + t % 2][:, 0:HO].rearrange("p (h o) -> p h o", o=O),
                                  fb.broadcast_to([128, H, O]), ALU.mult).then_inc(val_ok, 1)

            def head(h, last):
                for c in range(3):
                    a, wd = CH[c]
                    dve.wait_ge(row_ok, 3 * h + c + 1)
                    if H > 1:
                        dve.wait_ge(agg_out, len(groups) * h + c + 1)
                    for t in range(NT):
                        sc = hj[:, t, bass.ds(h, 1)] if not isinstance(h, int) else hj[:, t, h:h + 1]
                        dve.scalar_tensor_tensor(out=pt[c][:, t, :], in0=row[:, c, 0:wd], scalar=sc,
                                                 in1=g.AT[:, t, a:a + wd], op0=ALU.max,
                                                 op1=ALU.mult).then_inc(pt_ok, 1)

            heads(dve, head)


def normalise_elu(nc, g, tag, raw, H, O, outT):
    HO, V1 = H * O, O + 1
    F = HO // 128
    with ExitStack() as ctx:
        s = Scope(nc, ctx, tag)
        inv = s.sb("inv", [128, NT, H], F32)
        xn, e, y = (s.sb(k, [128, 2, HO], F32) for k in ("xn", "e", "y"))
        tp = [s.ps(f"tp{i}", [128, F, 128], F32) for i in range(3)]
        v, neg_ok, exp_ok, y_ok, turned, out = (s.sem(k) for k in ("v", "neg_ok", "exp_ok", "y_ok", "turned", "out"))
        block = s.block()

        @block.vector
        def _(dve):
            c = Chain(dve, v)
            r4 = raw[:, :, :].rearrange("p t (h o) -> p t h o", o=V1)
            c.step(dve.reciprocal(inv[:, :, :], r4[:, :, :, O]))

            def finish(t):
                b = t % 2
                dve.wait_ge(exp_ok, t + 1)
                c.step(dve.tensor_scalar(e[:, b, :], e[:, b, :], -1.0, None, ALU.add))
                if t >= 2:
                    dve.wait_ge(turned, t - 1)
                dve.scalar_tensor_tensor(out=y[:, b, :], in0=xn[:, b, :], scalar=0.0, in1=e[:, b, :],
                                         op0=ALU.max, op1=ALU.add).then_inc(y_ok, 1)

            for t in range(NT):
                b = t % 2
                if t >= 2:
                    dve.wait_ge(y_ok, t - 1)
                c.step(dve.tensor_tensor(xn[:, b, :].rearrange("p (h o) -> p h o", o=O), r4[:, t, :, 0:O],
                                         inv[:, t, :].unsqueeze(2).broadcast_to([128, H, O]), ALU.mult))
                dve.tensor_scalar(e[:, b, :], xn[:, b, :], 0.0, None, ALU.min).then_inc(neg_ok, 1)
                if t >= 1:
                    finish(t - 1)
            finish(NT - 1)

        @block.scalar
        def _(act):
            for t in range(NT + 1):
                if t < NT:
                    act.wait_ge(neg_ok, t + 1)
                    act.activation(e[:, t % 2, :], e[:, t % 2, :], ACT.Exp).then_inc(exp_ok, 1)
                if t >= 1:
                    act.wait_ge(turned, t)
                    act.activation(outT[:, :, (t - 1) * 128:t * 128], tp[(t - 1) % 3][:, :, :],
                                   ACT.Copy).then_inc(out, 1)

        @block.tensor
        def _(pe):
            for t in range(NT):
                pe.wait_ge(y_ok, t + 1)
                if t >= 3:
                    pe.wait_ge(out, t - 2)
                for f in range(F):
                    mm = pe.transpose(tp[t % 3][:, f, :], y[:, t % 2, f * 128:(f + 1) * 128], g.ident[:, :])
                mm.then_inc(turned, 1)


def mlp(nc, g, tag, inT, w1T_dram, b1_dram, func, w2T_dram, b2_dram):
    M = w1T_dram.shape[1]
    F = M // 128
    with ExitStack() as ctx:
        s = Scope(nc, ctx, tag)
        w1 = s.sb("w1", [128, 2, M], F32)
        w2 = s.sb("w2", [128, F, D], F32)
        b1 = s.sb("b1", [128, F], F32)
        b2 = s.sb("b2", [1, D], F32)
        z = s.sb("z", [128, F, NP], F32)
        bank = [s.ps(f"bank{i}", [128, 512], F32) for i in range(8)]
        w_in, z_mm, z_ok, y_mm, y_ok = (s.sem(k) for k in ("w_in", "z_mm", "z_ok", "y_mm", "y_ok"))
        block = s.block()
        blocks = [(c, m) for c in range(3) for m in range(F)]

        @block.sync
        def _(sp):
            sp.dma_start(w1[:, :, :], w1T_dram.rearrange("(k p) o -> p k o", p=128)).then_inc(w_in, 16)
            sp.dma_start(b1[:, :], b1_dram).then_inc(w_in, 16)
            sp.dma_start(w2[:, :, :], w2T_dram.rearrange("(k p) o -> p k o", p=128)).then_inc(w_in, 16)
            sp.dma_start(b2[:, :], b2_dram.unsqueeze(0)).then_inc(w_in, 16)

        @block.tensor
        def _(pe):
            pe.wait_ge(w_in, 64)
            for n, (c, m) in enumerate(blocks):
                a, w = CH[c]
                if n >= 4:
                    pe.wait_ge(z_ok, n - 3)
                for k in range(2):
                    mm = pe.matmul(bank[n % 4][:, 0:w], w1[:, k, m * 128:(m + 1) * 128], inT[:, k, a:a + w],
                                   start=k == 0, stop=k == 1)
                mm.then_inc(z_mm, 1)
            for t in range(NT):
                pe.wait_ge(z_ok, F * (t // 4 + 1))
                if t >= 4:
                    pe.wait_ge(y_ok, t - 3)
                for k in range(F):
                    pe.matmul(bank[4 + t % 4][:, 0:D], z[:, k, t * 128:(t + 1) * 128], w2[:, k, :],
                              start=k == 0, stop=False)
                pe.matmul(bank[4 + t % 4][:, 0:D], g.ones[0:1, :], b2[:, :], start=False, stop=True).then_inc(y_mm, 1)

        @block.scalar
        def _(act):
            act.wait_ge(w_in, 64)
            for n, (c, m) in enumerate(blocks):
                a, w = CH[c]
                act.wait_ge(z_mm, n + 1)
                act.activation(z[:, m, a:a + w], bank[n % 4][:, 0:w], func, bias=b1[:, m:m + 1]).then_inc(z_ok, 1)

        @block.vector
        def _(dve):
            for t in range(NT):
                dve.wait_ge(y_mm, t + 1)
                dve.tensor_tensor(g.x[:, t, :], bank[4 + t % 4][:, 0:D], g.x[:, t, :], ALU.add).then_inc(y_ok, 1)


STATE_SCALE = 1024.0


def gated_graph(nc, g, d):
    with ExitStack() as ctx:
        s = Scope(nc, ctx, "ggnn")
        gw = [s.sb(f"gw{i}", [128, 6, 3 * D], F32R) for i in range(2)]
        bw = s.sb("bw", [6, 3 * D], F32R)
        deg = s.sb("deg", [6, N], F32R)
        nm = [s.sb(f"nm{i}", [128, NT, D], F16) for i in range(2)]
        gate_weights(nc, g, d, gw, bw, deg, nm)
        gated_steps(nc, g, gw, bw, deg, nm)


def gate_weights(nc, g, d, gw, bw, deg, nm):
    with ExitStack() as ctx:
        s = Scope(nc, ctx, "gate")
        win = s.sb("win", [128, 2, 2, D], F32)
        wst = s.sb("wst", [128, 6, 3 * D], F32)
        bcol = s.sb("bcol", [128, 2, 2], F32)
        brow = s.sb("brow", [1, 3 * D], F32)
        blhs = s.sb("blhs", [128, 2, 2, 6], F32)
        elhs = s.sb("elhs", [1, 6], F32)
        dlhs = s.sb("dlhs", [128, 2, 6], F16)
        dl1 = s.sb("dl1", [1, 6], F16)
        one16 = s.sb("one16", [1, 512], F16)
        first3 = s.sb("first3", [6, 1], F32)
        last3 = s.sb("last3", [6, 1], F32)
        bhi = s.sb("bhi", [6, 3 * D], F32R)
        blo = s.sb("blo", [6, 3 * D], F32)
        bank = [s.ps(f"bank{i}", [128, 512], F32) for i in range(8)]
        w_in, v, lhs_ok, g_mm, hi_ok, lo_ok, b_mm, b_ok, d_mm, d_ok, turned, nhi, nlo = (
            s.sem(k) for k in ("w_in", "v", "lhs_ok", "g_mm", "hi_ok", "lo_ok", "b_mm", "b_ok", "d_mm", "d_ok",
                               "turned", "nhi", "nlo"))
        block = s.block()
        HALF = 3 * D // 2
        prods = [(side, k, n) for side in range(2) for k in range(2) for n in range(2)]
        n_in = 16 * 10

        @block.sync
        def _(sp):
            for i, name in enumerate(("in_W", "out_W")):
                sp.dma_start(win[:, i, :, :], d[name].rearrange("(k p) o -> p k o", p=128)).then_inc(w_in, 16)
            for i, name in enumerate(("r_WT", "z_WT", "h_WT")):
                sp.dma_start(wst[:, :, i * D:(i + 1) * D],
                             d[name].rearrange("(k p) o -> p k o", p=128)).then_inc(w_in, 16)
            for i, name in enumerate(("in_b", "out_b")):
                sp.dma_start(bcol[:, i, :], d[name]).then_inc(w_in, 16)
            for i, name in enumerate(("r_b", "z_b", "h_b")):
                sp.dma_start(brow[:, i * D:(i + 1) * D], d[name].unsqueeze(0)).then_inc(w_in, 16)

        @block.gpsimd
        def _(pool):
            n = 0
            for m in (blhs, elhs, dlhs, dl1):
                ap = m[:, :, :, :] if m is blhs else m[:, :, :] if m is dlhs else m[:, :]
                n += 1
                pool.memset(ap, 0.0).then_inc(lhs_ok, 1)
                pool.wait_ge(lhs_ok, n)
            pool.memset(one16[:, :], 1.0).then_inc(lhs_ok, 1)
            pool.wait_ge(lhs_ok, 5)
            pool.wait_ge(w_in, n_in)
            for q in range(2):
                for side in range(2):
                    pool.tensor_copy(blhs[:, side, :, side + 3 * q], bcol[:, side, :]).then_inc(lhs_ok, 1)
                    pool.memset(dlhs[:, side, side + 3 * q:side + 3 * q + 1], 1.0).then_inc(lhs_ok, 1)
                pool.memset(elhs[:, 2 + 3 * q:3 + 3 * q], 1.0).then_inc(lhs_ok, 1)
                pool.memset(dl1[:, 2 + 3 * q:3 + 3 * q], 1.0).then_inc(lhs_ok, 1)

        @block.tensor
        def _(pe):
            pe.wait_ge(w_in, n_in)
            for n, (side, k, half) in enumerate(prods):
                if n >= 4:
                    pe.wait_ge(lo_ok, n - 3)
                for o in range(2):
                    mm = pe.matmul(bank[n % 4][:, 0:HALF], win[:, side, o, k * 128:(k + 1) * 128],
                                   wst[:, 2 * side + o, half * HALF:(half + 1) * HALF], start=o == 0, stop=o == 1)
                mm.then_inc(g_mm, 1)
            pe.wait_ge(lhs_ok, 17)
            for half in range(2):
                cols = slice(half * HALF, (half + 1) * HALF)
                for side in range(2):
                    for o in range(2):
                        pe.matmul(bank[4 + half][0:6, 0:HALF], blhs[:, side, o, :], wst[:, 2 * side + o, cols],
                                  start=side + o == 0, stop=False)
                pe.matmul(bank[4 + half][0:6, 0:HALF], elhs[:, :], brow[:, cols], start=False, stop=True).then_inc(b_mm, 1)
            for c, (a, w) in enumerate(CHV):
                if c == 2:
                    pe.wait_ge(d_ok, 1)
                for t in range(NT):
                    pe.matmul(bank[6 + c % 2][0:6, 0:w], dlhs[:, 0, :], g.AT[:, t, a:a + w], start=t == 0, stop=False)
                    pe.matmul(bank[6 + c % 2][0:6, 0:w], dlhs[:, 1, :], g.A[:, t, a:a + w], start=False, stop=False)
                pe.matmul(bank[6 + c % 2][0:6, 0:w], dl1[:, :], one16[:, 0:w], start=False, stop=True).then_inc(d_mm, 1)
            pe.wait_ge(b_ok, 2)
            pe.wait_ge(lo_ok, len(prods) + 4)
            for t in range(NT):
                if t >= 4:
                    pe.wait_ge(nlo, t - 3)
                for f in range(2):
                    mm = pe.transpose(bank[t % 4][:, f * 128:(f + 1) * 128], g.hT[:, f, t * 128:(t + 1) * 128],
                                      g.ident[:, :])
                mm.then_inc(turned, 1)

        @block.scalar
        def _(act):
            for n, (side, k, half) in enumerate(prods):
                act.wait_ge(g_mm, n + 1)
                act.activation(gw[0][:, 2 * side + k, half * HALF:(half + 1) * HALF], bank[n % 4][:, 0:HALF],
                               ACT.Copy).then_inc(hi_ok, 1)
            for k in range(4, 6):
                act.activation(gw[0][:, k, :], wst[:, k, :], ACT.Copy).then_inc(hi_ok, 1)
            for t in range(NT):
                act.wait_ge(turned, t + 1)
                act.activation(nm[0][:, t, :], bank[t % 4][:, 0:D], ACT.Copy, scale=STATE_SCALE).then_inc(nhi, 1)

        @block.vector
        def _(dve):
            c = Chain(dve, v)
            for n, (side, k, half) in enumerate(prods):
                dve.wait_ge(hi_ok, n + 1)
                cols = slice(half * HALF, (half + 1) * HALF)
                dve.tensor_tensor(gw[1][:, 2 * side + k, cols], bank[n % 4][:, 0:HALF],
                                  gw[0][:, 2 * side + k, cols].bitcast(F32), ALU.subtract).then_inc(lo_ok, 1)
            for k in range(4, 6):
                dve.wait_ge(hi_ok, len(prods) + k - 3)
                dve.tensor_tensor(gw[1][:, k, :], wst[:, k, :], gw[0][:, k, :].bitcast(F32),
                                  ALU.subtract).then_inc(lo_ok, 2)
            c.done(dve.reduce_sum(first3[:, :], g.ident[0:6, 0:3], AX.X))
            c.step(dve.reduce_sum(last3[:, :], g.ident[0:6, 3:6], AX.X))
            for half in range(2):
                cols = slice(half * HALF, (half + 1) * HALF)
                ps = bank[4 + half][0:6, 0:HALF]
                dve.wait_ge(b_mm, half + 1)
                c.step(dve.tensor_copy(bhi[:, cols], ps))
                c.step(dve.tensor_tensor(blo[:, cols], ps, bhi[:, cols].bitcast(F32), ALU.subtract))
                c.step(dve.tensor_scalar(blo[:, cols], blo[:, cols], last3[:, 0:1], None, ALU.mult))
                dve.scalar_tensor_tensor(out=bw[:, cols], in0=bhi[:, cols].bitcast(F32), scalar=first3[:, 0:1],
                                         in1=blo[:, cols], op0=ALU.mult, op1=ALU.add).then_inc(b_ok, 1)
            for q, (a, w) in enumerate(CHV):
                dve.wait_ge(d_mm, q + 1)
                dve.tensor_copy(deg[:, a:a + w], bank[6 + q % 2][0:6, 0:w]).then_inc(d_ok, 1)
            for t in range(NT):
                dve.wait_ge(nhi, t + 1)
                dve.scalar_tensor_tensor(out=nm[1][:, t, :], in0=bank[t % 4][:, 0:D], scalar=STATE_SCALE,
                                         in1=nm[0][:, t, :], op0=ALU.mult, op1=ALU.subtract).then_inc(nlo, 1)


def gated_steps(nc, g, gw, bw, deg, nm):
    STEPS = 5
    CW = 512
    FT = [t for c in range(3) for t in [(4 * c, min(4, NT - 4 * c))]]
    with ExitStack() as ctx:
        s = Scope(nc, ctx, "step")
        uv = [[s.sb(f"uv{b}{p}", [128, 4, CW], F32R) for p in range(2)] for b in range(2)]
        st = [s.sb(f"st{p}", [128, 2, CW], F32R) for p in range(2)]
        rs = [s.sb(f"rs{p}", [128, 2, CW], F32R) for p in range(2)]
        rsf, r, z, ht = (s.sb(k, [128, 2, CW], F32) for k in ("rsf", "r", "z", "ht"))
        sums = [s.ps(f"sums{i}", [128, 512], F32) for i in range(2)]
        gate = [s.ps(f"gate{i}", [128, 512], F32) for i in range(6)]
        sums_mm, sums_hi, sums_lo = s.sem("sums_mm"), s.sem("sums_hi"), s.sem("sums_lo")
        st_hi, st_lo, rz_mm, h_mm, gate_out = (s.sem(k) for k in ("st_hi", "st_lo", "rz_mm", "h_mm", "gate_out"))
        rs_ok, rs_hi, rs_lo, upd, new_ok, turned = (s.sem(k) for k in ("rs_ok", "rs_hi", "rs_lo", "upd", "new_ok", "turned"))
        block = s.block()

        uses = [("sum", 0, m) for m in range(4)] + [("sum", 1, m) for m in range(4)] + [("sum", 2, m) for m in range(4)]
        uses += [("turn", c, q) for c in range(3) for q in range(2)]
        U = len(uses)
        number = {u: n for n, u in enumerate(uses)}

        @block.gpsimd
        def _(pool):
            pool.sem_inc(sums_lo, 2)
            pool.sem_inc(gate_out, 6)
            pool.sem_inc(h_mm, 2)

        @block.tensor
        def _(pe):
            def add_up(step, c):
                a, w = CHV[c]
                for m in range(4):
                    n = number[("sum", c, m)]
                    adj = g.AT if m < 2 else g.A
                    f = m % 2
                    pe.wait_ge(sums_lo, U * step + n + 1)
                    for t in range(NT):
                        if n == 0 and t == NT - 1:
                            pe.wait_ge(sums_lo, U * step + 2)
                        for p in range(2):
                            mm = pe.matmul(sums[n % 2][:, 0:w], nm[p][:, t, f * 128:(f + 1) * 128],
                                           adj[:, t, a:a + w], start=t + p == 0, stop=t == NT - 1 and p == 1)
                    mm.then_inc(sums_mm, 1)

            def products(out, m, ks, parts, w, start, stop):
                n = 0
                for k, (hi, lo) in zip(ks, parts):
                    col = slice(m * 128, (m + 1) * 128)
                    for wp, x in ((gw[0], hi), (gw[0], lo), (gw[1], hi)):
                        n += 1
                        mm = pe.matmul(out[:, 0:w], wp[:, k, col], x, start=start and n == 1,
                                       stop=stop and n == 3 * len(ks))
                return mm

            def gates(step, c):
                a, w = CHV[c]
                G = 3 * step + c
                b = c % 2
                pair = [(uv[b][0][:, k, 0:w], uv[b][1][:, k, 0:w]) for k in range(4)]
                spair = [(st[0][:, k, 0:w], st[1][:, k, 0:w]) for k in range(2)]
                rpair = [(rs[0][:, k, 0:w], rs[1][:, k, 0:w]) for k in range(2)]
                pe.wait_ge(sums_lo, U * step + number[("sum", c, 3)] + 3)
                pe.wait_ge(st_lo, G + 1)
                for m in range(6):
                    pe.wait_ge(gate_out, 6 * G + m + 1)
                    pe.matmul(gate[m][:, 0:w], bw[:, m * 128:(m + 1) * 128], deg[:, a:a + w], start=True, stop=False)
                    mm = products(gate[m], m, range(4), pair, w, False, False)
                    if m < 4:
                        mm = products(gate[m], m, (4, 5), spair, w, False, True)
                        mm.then_inc(rz_mm, 1)
                pe.wait_ge(rs_lo, G + 1)
                for m in (4, 5):
                    products(gate[m], m, (4, 5), rpair, w, False, True).then_inc(h_mm, 1)

            def turn(step, c):
                t0, k = FT[c]
                pe.wait_ge(new_ok, 3 * step + c + 1)
                for q in range(2):
                    n = number[("turn", c, q)]
                    pe.wait_ge(sums_lo, U * step + n + 1)
                    for e in range(min(2, k - 2 * q)):
                        for f in range(2):
                            t = t0 + 2 * q + e
                            mm = pe.transpose(sums[n % 2][:, (2 * e + f) * 128:(2 * e + f + 1) * 128],
                                              g.hT[:, f, t * 128:(t + 1) * 128], g.ident[:, :])
                    mm.then_inc(sums_mm, 1)

            with pe.Fori(0, STEPS) as step:
                add_up(step, 0)
                add_up(step, 1)
                gates(step, 0)
                add_up(step, 2)
                gates(step, 1)
                turn(step, 0)
                gates(step, 2)
                turn(step, 1)
                turn(step, 2)

        @block.scalar
        def _(act):
            def sums_high(step, c):
                w = CHV[c][1]
                for m in range(4):
                    n = number[("sum", c, m)]
                    act.wait_ge(sums_mm, U * step + n + 1)
                    if m == 0:
                        last = {0: 3 * step * 2, 1: (3 * step) * 2, 2: (3 * step + 1) * 2}[c]
                        act.wait_ge(h_mm, last + 2)
                    act.activation(uv[c % 2][0][:, m, 0:w], sums[n % 2][:, 0:w], ACT.Copy,
                                   scale=1.0 / STATE_SCALE).then_inc(sums_hi, 1)

            def state_high(step, c):
                a, w = CHV[c]
                G = 3 * step + c
                act.wait_ge(h_mm, 2 * G + 2)
                act.activation(st[0][:, :, 0:w], g.hT[:, :, a:a + w], ACT.Copy).then_inc(st_hi, 1)

            def gates(step, c):
                w = CHV[c][1]
                G = 3 * step + c
                for m in range(4):
                    act.wait_ge(rz_mm, 4 * G + m + 1)
                    if m == 2:
                        act.wait_ge(upd, 3 * G + 1)
                    act.activation((r, z)[m // 2][:, m % 2, 0:w], gate[m][:, 0:w], ACT.Sigmoid).then_inc(gate_out, 1)
                    if m == 1:
                        act.wait_ge(rs_ok, G + 1)
                        act.activation(rs[0][:, :, 0:w], rsf[:, :, 0:w], ACT.Copy).then_inc(rs_hi, 1)
                for m in range(2):
                    act.wait_ge(h_mm, 2 * G + m + 3)
                    act.activation(ht[:, m, 0:w], gate[4 + m][:, 0:w], ACT.Tanh).then_inc(gate_out, 1)

            def turned_high(step, c):
                t0, k = FT[c]
                for q in range(2):
                    n = number[("turn", c, q)]
                    kk = min(2, k - 2 * q)
                    act.wait_ge(sums_mm, U * step + n + 1)
                    act.activation(nm[0][:, t0 + 2 * q:t0 + 2 * q + kk, :],
                                   sums[n % 2][:, 0:kk * D].rearrange("p (t f) -> p t f", f=D), ACT.Copy,
                                   scale=STATE_SCALE).then_inc(sums_hi, 1)

            with act.Fori(0, STEPS) as step:
                state_high(step, 0)
                sums_high(step, 0)
                sums_high(step, 1)
                gates(step, 0)
                state_high(step, 1)
                sums_high(step, 2)
                gates(step, 1)
                state_high(step, 2)
                turned_high(step, 0)
                gates(step, 2)
                turned_high(step, 1)
                turned_high(step, 2)

        @block.vector
        def _(dve):
            dve.sem_inc(upd, 1)

            def sums_low(step, c):
                w = CHV[c][1]
                for m in range(4):
                    n = number[("sum", c, m)]
                    dve.wait_ge(sums_hi, U * step + n + 1)
                    dve.scalar_tensor_tensor(out=uv[c % 2][1][:, m, 0:w], in0=sums[n % 2][:, 0:w],
                                             scalar=1.0 / STATE_SCALE, in1=uv[c % 2][0][:, m, 0:w].bitcast(F32),
                                             op0=ALU.mult, op1=ALU.subtract).then_inc(sums_lo, 1)

            def state_low(step, c):
                a, w = CHV[c]
                dve.wait_ge(st_hi, 3 * step + c + 1)
                dve.tensor_tensor(st[1][:, :, 0:w], g.hT[:, :, a:a + w], st[0][:, :, 0:w].bitcast(F32),
                                  ALU.subtract).then_inc(st_lo, 1)

            def reset(step, c):
                a, w = CHV[c]
                G = 3 * step + c
                dve.wait_ge(gate_out, 6 * G + 2 + 6)
                dve.tensor_tensor(rsf[:, :, 0:w], r[:, :, 0:w], g.hT[:, :, a:a + w], ALU.mult).then_inc(rs_ok, 1)
                dve.wait_ge(rs_hi, G + 1)
                dve.tensor_tensor(rs[1][:, :, 0:w], rsf[:, :, 0:w], rs[0][:, :, 0:w].bitcast(F32),
                                  ALU.subtract).then_inc(rs_lo, 1)

            def update(step, c):
                a, w = CHV[c]
                G = 3 * step + c
                dve.wait_ge(gate_out, 6 * G + 6 + 6)
                old = g.hT[:, :, a:a + w]
                dve.tensor_tensor(ht[:, :, 0:w], ht[:, :, 0:w], old, ALU.subtract).then_inc(upd, 1)
                dve.wait_ge(upd, 3 * G + 2)
                dve.tensor_tensor(ht[:, :, 0:w], ht[:, :, 0:w], z[:, :, 0:w], ALU.mult).then_inc(upd, 1)
                dve.wait_ge(upd, 3 * G + 3)
                dve.tensor_tensor(old, old, ht[:, :, 0:w], ALU.add).then_inc(new_ok, 1)
                dve.wait_ge(new_ok, G + 1)
                dve.sem_inc(upd, 1)

            def turned_low(step, c):
                t0, k = FT[c]
                for q in range(2):
                    n = number[("turn", c, q)]
                    kk = min(2, k - 2 * q)
                    tiles = slice(t0 + 2 * q, t0 + 2 * q + kk)
                    dve.wait_ge(sums_hi, U * step + n + 1)
                    dve.scalar_tensor_tensor(out=nm[1][:, tiles, :],
                                             in0=sums[n % 2][:, 0:kk * D].rearrange("p (t f) -> p t f", f=D),
                                             scalar=STATE_SCALE, in1=nm[0][:, tiles, :],
                                             op0=ALU.mult, op1=ALU.subtract).then_inc(sums_lo, 1)

            with dve.Fori(0, STEPS) as step:
                state_low(step, 0)
                sums_low(step, 0)
                sums_low(step, 1)
                reset(step, 0)
                update(step, 0)
                state_low(step, 1)
                sums_low(step, 2)
                reset(step, 1)
                update(step, 1)
                state_low(step, 2)
                turned_low(step, 0)
                reset(step, 2)
                update(step, 2)
                turned_low(step, 1)
                turned_low(step, 2)


def batchnorm_out(nc, g, raw, H, O, gamma_dram, beta_dram, out_dram):
    V1 = O + 1
    with ExitStack() as ctx:
        s = Scope(nc, ctx, "bn")
        inv = s.sb("inv", [128, NT, H], F32)
        hp = s.sb("hp", [128, NT, D], F32)
        sq = s.sb("sq", [128, NT, D], F32)
        gb = s.sb("gb", [128, 2, D], F32)
        mean, scale, tmp = (s.sb(k, [128, D], F32) for k in ("mean", "scale", "tmp"))
        eps = s.sb("eps", [128, 1], F32)
        bank = [s.ps(f"bank{i}", [128, 512], F32) for i in range(2)]
        v, w_in, hp_ok, sum_mm, sq_ok, var_ok, std_ok, cen_ok, pre_ok, relu_ok, x_ok, stored = (
            s.sem(k) for k in ("v", "w_in", "hp_ok", "sum_mm", "sq_ok", "var_ok", "std_ok", "cen_ok", "pre_ok",
                               "relu_ok", "x_ok", "stored"))
        block = s.block()

        @block.sync
        def _(sp):
            sp.dma_start(gb[:, 0, :], gamma_dram.partition_broadcast(128)).then_inc(w_in, 16)
            sp.dma_start(gb[:, 1, :], beta_dram.partition_broadcast(128)).then_inc(w_in, 16)
            for t in range(NT):
                k = 128 if t < NT - 1 else TAIL
                sp.wait_ge(x_ok, t + 1)
                sp.dma_start(out_dram[t * 128:t * 128 + k, :], g.x[0:k, t, :]).then_inc(stored, 16)
            sp.wait_ge(stored, 16 * NT)

        @block.tensor
        def _(pe):
            for b, (src, ok) in enumerate(((hp, hp_ok), (sq, sq_ok))):
                for t in range(NT):
                    k = 128 if t < NT - 1 else TAIL
                    pe.wait_ge(ok, t + 1)
                    mm = pe.matmul(bank[b][:, 0:D], g.ones[0:k, :], src[0:k, t, :], start=t == 0, stop=t == NT - 1)
                mm.then_inc(sum_mm, 1)

        @block.scalar
        def _(act):
            for t in range(NT):
                act.wait_ge(cen_ok, t + 1)
                act.activation(sq[:, t, :], hp[:, t, :], ACT.Square).then_inc(sq_ok, 1)
            act.wait_ge(var_ok, 1)
            act.activation(tmp[:, :], tmp[:, :], ACT.Sqrt, bias=eps[:, 0:1]).then_inc(std_ok, 1)

        @block.vector
        def _(dve):
            c = Chain(dve, v)
            r4 = raw[:, :, :].rearrange("p t (h o) -> p t h o", o=V1)
            c.done(dve.memset(eps[:, :], 1e-5))
            c.step(dve.reciprocal(inv[:, :, :], r4[:, :, :, O]))
            for t in range(NT):
                dve.tensor_tensor(hp[:, t, :].rearrange("p (h o) -> p h o", o=O), r4[:, t, :, 0:O],
                                  inv[:, t, :].unsqueeze(2).broadcast_to([128, H, O]), ALU.mult).then_inc(hp_ok, 1)
            dve.wait_ge(sum_mm, 1)
            c.step(dve.tensor_scalar(mean[:, :], bank[0][:, 0:D], 1.0 / N, None, ALU.mult))
            for t in range(NT):
                dve.tensor_tensor(hp[:, t, :], hp[:, t, :], mean[:, :], ALU.subtract).then_inc(cen_ok, 1)
            dve.wait_ge(sum_mm, 2)
            dve.tensor_scalar(tmp[:, :], bank[1][:, 0:D], 1.0 / N, None, ALU.mult).then_inc(var_ok, 1)
            dve.wait_ge(std_ok, 1)
            dve.wait_ge(w_in, 32)
            c.step(dve.reciprocal(scale[:, :], tmp[:, :]))
            c.step(dve.tensor_tensor(scale[:, :], scale[:, :], gb[:, 0, :], ALU.mult))
            dve.wait_ge(cen_ok, NT)
            for t in range(NT):
                c.step(dve.tensor_tensor(hp[:, t, :], hp[:, t, :], scale[:, :], ALU.mult))
                c.step(dve.tensor_tensor(hp[:, t, :], hp[:, t, :], gb[:, 1, :], ALU.add))
                dve.scalar_tensor_tensor(out=g.x[:, t, :], in0=hp[:, t, :], scalar=0.0, in1=g.x[:, t, :],
                                         op0=ALU.max, op1=ALU.add).then_inc(x_ok, 1)


class Graph:
    pass


def program(nc, d, out):
    with ExitStack() as ctx:
        s = Scope(nc, ctx, "g")
        g = Graph()
        g.A = s.sb("A", [128, NT, NP], F16)
        g.AT = s.sb("AT", [128, NT, NP], F16)
        g.x = s.sb("x", [128, NT, D], F32)
        g.hT = s.sb("hT", [128, 2, NP], F32)
        g.ident = s.sb("ident", [128, 128], F32)
        g.ident16 = s.sb("ident16", [128, 128], F16)
        g.ones = s.sb("ones", [128, 128], F32)

        load_graph(nc, g, d["x"], d["adj"])
        layernorm_relu(nc, g, "ln0")
        cosine_attention(nc, g, d["L0_WT"])
        layernorm_relu(nc, g, "ln1")
        with ExitStack() as c1:
            s1 = Scope(nc, c1, "l1")
            with ExitStack() as c2:
                raw8 = Scope(nc, c2, "l1r").sb("raw8", [128, NT, 8 * 65], F32)
                gat(nc, g, "gat8", g.hT, 2, d["L1_W1"], d["L1_ai"], d["L1_aj"], 8, 64, raw8)
                x1T = Scope(nc, c2, "l1x").sb("x1T", [128, 4, NP], F32)
                normalise_elu(nc, g, "elu8", raw8, 8, 64, x1T)
                raw1 = raw8[:, :, 0:257]
                gat(nc, g, "gat1", x1T, 4, d["L1_Wo"], d["L1_aoi"], d["L1_aoj"], 1, 256, raw1, raw8[:, :, 257:514])
                normalise_elu(nc, g, "elu1", raw1, 1, 256, g.hT)
            mlp(nc, g, "mlp1", g.hT, d["L1_lin1"], d["L1_b1"], ACT.Relu, d["L1_lin2"], d["L1_b2"])
        layernorm_relu(nc, g, "ln2")
        gated_graph(nc, g, d)
        mlp(nc, g, "mlp2", g.hT, d["o1_WT"], d["o1_b"], ACT.Tanh, d["o2_WT"], d["o2_b"])
        layernorm_relu(nc, g, "ln3")
        with ExitStack() as c3:
            raw3 = Scope(nc, c3, "l3").sb("raw3", [128, NT, 8 * 33], F32)
            gat(nc, g, "gat3", g.hT, 2, d["L3_WT"], d["L3_ai"], d["L3_aj"], 8, 32, raw3)
            batchnorm_out(nc, g, raw3, 8, 32, d["L3_gamma"], d["L3_beta"], out)


def kernel(**inputs):
    import numpy as _np
    import concourse.bacc as _bacc
    from concourse import mybir as _mybir
    from concourse.bass_utils import run_bass_kernel_spmd as _run

    i = {k: _np.asarray(v) for k, v in inputs.items()}
    laid = {
        "x": i["x"], "adj": i["adj"], "L0_WT": i["L0_gnn_W"].T,
        "L1_W1": i["L1_gnn_W1"].transpose(1, 0, 2).reshape(256, 512),
        "L1_ai": i["L1_gnn_a1"][:, :64].reshape(512), "L1_aj": i["L1_gnn_a1"][:, 64:].reshape(512),
        "L1_Wo": i["L1_gnn_Wo"], "L1_aoi": i["L1_gnn_ao"][:256], "L1_aoj": i["L1_gnn_ao"][256:],
        "L1_lin1": i["L1_gnn_lin1_w"], "L1_b1": i["L1_gnn_lin1_b"].reshape(4, 128).T,
        "L1_lin2": i["L1_gnn_lin2_w"], "L1_b2": i["L1_gnn_lin2_b"],
        "in_W": i["L2_gnn_in_W"], "out_W": i["L2_gnn_out_W"], 
        "in_b": i["L2_gnn_in_b"].reshape(2, 128).T, "out_b": i["L2_gnn_out_b"].reshape(2, 128).T,
        "r_WT": i["L2_gnn_r_W"].T, "z_WT": i["L2_gnn_z_W"].T, "h_WT": i["L2_gnn_h_W"].T,
        "r_b": i["L2_gnn_r_b"], "z_b": i["L2_gnn_z_b"], "h_b": i["L2_gnn_h_b"],
        "o1_WT": i["L2_gnn_o1_W"].T, "o1_b": i["L2_gnn_o1_b"].reshape(2, 128).T,
        "o2_WT": i["L2_gnn_o2_W"].T, "o2_b": i["L2_gnn_o2_b"],
        "L3_WT": i["L3_gnn_W"].T, "L3_ai": i["L3_gnn_a"][32:], "L3_aj": i["L3_gnn_a"][:32],
        "L3_gamma": i["L3_gnn_gamma"], "L3_beta": i["L3_gnn_beta"],
    }
    nc = _bacc.Bacc("TRN2", target_bir_lowering=False, num_devices=1)
    arrays, d = {}, {}
    for name, a in laid.items():
        a = _np.ascontiguousarray(a)
        arrays[f"in_{name}_dram"] = a
        d[name] = nc.dram_tensor(f"in_{name}_dram", a.shape, _mybir.dt.from_np(a.dtype), kind="ExternalInput").ap()
    out = nc.dram_tensor("out_dram", (1354, 256), _mybir.dt.float32, kind="ExternalOutput").ap()
    program(nc, d, out)
    r = _run(nc, [arrays], core_ids=[0])
    return r.results[0]["out_dram"]
```

```python
import concourse.bass as bass
from concourse import mybir
from contextlib import ExitStack

F32 = mybir.dt.float32
F32R = mybir.dt.float32r
F16 = mybir.dt.float16
I32 = mybir.dt.int32
ALU = mybir.AluOpType
ACT = mybir.ActivationFunctionType
AX = mybir.AxisListType
RMAX = bass.bass_isa.ReduceOp.max

N, D = 1354, 256
NT = (N + 127) // 128
NP = NT * 128
TAIL = N - (NT - 1) * 128
CH = [(0, 512), (512, 512), (1024, NP - 1024)]
CHV = [(0, 512), (512, 512), (1024, N - 1024)]


class Scope:

    def __init__(self, nc, ctx, tag):
        self.nc, self.ctx, self.tag, self.sems = nc, ctx, tag, []

    def sb(self, name, shape, dt):
        return self.ctx.enter_context(self.nc.sbuf_tensor(f"{self.tag}_{name}", shape, dt))

    def ps(self, name, shape, dt):
        return self.ctx.enter_context(self.nc.psum_tensor(f"{self.tag}_{name}", shape, dt))

    def sem(self, name):
        self.sems.append(self.nc.alloc_semaphore(f"{self.tag}_{name}"))
        return self.sems[-1]

    def block(self):
        self.ctx.callback(self.clear)
        return self.ctx.enter_context(self.nc.Block())

    def clear(self):
        self.nc.clear_and_free_semaphores(self.sems)
        self.nc.all_engine_barrier()


class Chain:

    def __init__(self, eng, sem):
        self.eng, self.sem, self.n = eng, sem, 0

    def done(self, ins):
        self.n += 1
        ins.then_inc(self.sem, 1)

    def wait(self):
        self.eng.wait_ge(self.sem, self.n)

    def step(self, ins):
        self.done(ins)
        self.wait()


def load_graph(nc, g, x_dram, adj_dram):
    with ExitStack() as ctx:
        s = Scope(nc, ctx, "load")
        NS = 3
        stage = s.sb("stage", [128, NS, N], I32)
        tp8 = [s.ps(f"tp8_{i}", [128, 8, 128], F16) for i in range(2)]
        tp3 = [s.ps(f"tp3_{i}", [128, NT - 8, 128], F16) for i in range(2)]
        arrived = [s.sem(f"arrived{i}") for i in range(NS)]
        x_in, cleared, ident_ok, even_ok, odd_ok, pad_ok = (
            s.sem(k) for k in ("x_in", "cleared", "ident_ok", "even_ok", "odd_ok", "pad_ok"))
        few = s.sb("few", [128, 3], F32)
        deg = [s.ps(f"deg{i}", [128, 512], F32) for i in range(3)]
        one16 = s.sb("one16", [128, 128], F16)
        turned, out8, out3, deg_mm, v = (s.sem(k) for k in ("turned", "out8", "out3", "deg_mm", "v"))
        block = s.block()

        def rows(t):
            return 128 if t < NT - 1 else TAIL

        @block.sync
        def _(sp):
            for t in range(NT):
                if t >= NS:
                    u = t - NS
                    sp.wait_ge(even_ok if u % 2 == 0 else odd_ok, u // 2 + 1)
                sp.dma_start(stage[0:rows(t), t % NS, :],
                             adj_dram[t * 128:t * 128 + rows(t), :]).then_inc(arrived[t % NS], 16)

        @block.gpsimd
        def _(pool):
            fills = [(g.A[:, :, N:NP], 0.0), (g.A[64:128, NT - 1, 0:N], 0.0), (g.x[64:128, NT - 1, :], 0.0),
                     (g.ident[:, :], 0.0), (g.ident16[:, :], 0.0), (g.ones[:, :], 1.0), (one16[:, :], 1.0)]
            for n, (region, value) in enumerate(fills):
                pool.memset(region, value).then_inc(cleared, 1)
                pool.wait_ge(cleared, n + 1)
            for m in (g.ident, g.ident16):
                pool.affine_select(out=m[:, :], in_=m[:, :], compare_op=ALU.not_equal, fill=1.0, base=0,
                                   pattern=[[-1, 128]], channel_multiplier=1).then_inc(ident_ok, 1)
            pool.wait_ge(ident_ok, 2)
            pool.tensor_copy(g.A[:, NT - 1, N:NP], g.ident16[:, TAIL:128]).then_inc(pad_ok, 1)

        def convert(eng, copy, t, ok):
            if t == NT - 1:
                eng.wait_ge(cleared, 7)
            eng.wait_ge(arrived[t % NS], 16 * (t // NS + 1))
            copy(g.A[0:rows(t), t, 0:N], stage[0:rows(t), t % NS, :]).then_inc(ok, 1)

        @block.scalar
        def _(act):
            act.dma_start(g.x[:, 0:NT - 1, :],
                          x_dram[0:(NT - 1) * 128, :].rearrange("(t p) f -> p t f", p=128)).then_inc(x_in, 16)
            act.wait_ge(cleared, 3)
            act.dma_start(g.x[0:TAIL, NT - 1, :], x_dram[(NT - 1) * 128:N, :]).then_inc(x_in, 16)
            for r in range(NT):
                if r % 2 == 1:
                    convert(act, lambda o, i: act.activation(o, i, ACT.Copy), r, odd_ok)
                if r >= 1:
                    act.wait_ge(turned, r)
                    act.activation(g.AT[:, 8:NT, (r - 1) * 128:r * 128], tp3[(r - 1) % 2][:, :, :],
                                   ACT.Copy).then_inc(out3, 1)
            act.wait_ge(turned, NT)
            act.activation(g.AT[:, 8:NT, (NT - 1) * 128:NP], tp3[(NT - 1) % 2][:, :, :],
                           ACT.Copy).then_inc(out3, 1)
            act.wait_ge(x_in, 32)

        @block.vector
        def _(dve):
            for r in range(NT):
                if r % 2 == 0:
                    convert(dve, dve.tensor_copy, r, even_ok)
                if r >= 1:
                    dve.wait_ge(turned, r)
                    dve.tensor_copy(g.AT[:, 0:8, (r - 1) * 128:r * 128], tp8[(r - 1) % 2][:, :, :]).then_inc(out8, 1)
            dve.wait_ge(turned, NT)
            dve.tensor_copy(g.AT[:, 0:8, (NT - 1) * 128:NP], tp8[(NT - 1) % 2][:, :, :]).then_inc(out8, 1)
            c_ = Chain(dve, v)
            for c, (a, w) in enumerate(CHV):
                dve.wait_ge(deg_mm, c + 1)
                c_.done(dve.tensor_reduce(few[:, c:c + 1], deg[c][:, 0:w], axis=AX.X, op=ALU.min))
            c_.wait()
            c_.step(dve.tensor_reduce(g.fewest[:, :], few[:, :], axis=AX.X, op=ALU.min))

        @block.tensor
        def _(pe):
            pe.wait_ge(ident_ok, 2)
            pe.wait_ge(cleared, 7)
            pe.wait_ge(pad_ok, 1)
            for r in range(NT):
                pe.wait_ge(even_ok if r % 2 == 0 else odd_ok, r // 2 + 1)
                if r >= 2:
                    pe.wait_ge(out8, r - 1)
                    pe.wait_ge(out3, r - 1)
                for c in range(NT):
                    out = tp8[r % 2][:, c, :] if c < 8 else tp3[r % 2][:, c - 8, :]
                    mm = pe.transpose(out, g.A[:, r, c * 128:(c + 1) * 128], g.ident16[:, :])
                mm.then_inc(turned, 1)
            pe.wait_ge(out8, NT)
            pe.wait_ge(out3, NT)
            for c, (a, w) in enumerate(CHV):
                for t in range(NT):
                    mm = pe.matmul(deg[c][:, 0:w], one16[:, :], g.AT[:, t, a:a + w], start=t == 0, stop=t == NT - 1)
                mm.then_inc(deg_mm, 1)


def layernorm_relu(nc, g, tag):
    with ExitStack() as ctx:
        s = Scope(nc, ctx, tag)
        stats = s.sb("stats", [128, NT, 6], F32)
        mv = s.sb("mv", [128, NT, 2], F32)
        eps = s.sb("eps", [128, 1], F32)
        std, rstd, shift = (s.sb(k, [128, NT], F32) for k in ("std", "rstd", "shift"))
        h = s.sb("h", [128, NT, D], F32)
        tp = [s.ps(f"tp{i}", [128, 2, 256], F32) for i in range(3)]
        v, std_ok, scale_ok, h_ok, turned, out = (
            s.sem(k) for k in ("v", "std_ok", "scale_ok", "h_ok", "turned", "out"))
        pairs = [(a, min(2, NT - a)) for a in range(0, NT, 2)]
        block = s.block()

        @block.vector
        def _(dve):
            c = Chain(dve, v)
            c.done(dve.memset(eps[:, :], 1e-5))
            for t in range(NT):
                c.done(dve.bn_stats(stats[:, t, :], g.x[:, t, :]))
            c.wait()
            for t in range(NT):
                c.done(dve.bn_aggr(mv[:, t, :], stats[:, t, :]))
            c.wait()
            dve.wait_ge(std_ok, 1)
            c.step(dve.reciprocal(rstd[:, :], std[:, :]))
            dve.scalar_tensor_tensor(out=shift[:, :], in0=mv[:, :, 0], scalar=-1.0, in1=rstd[:, :],
                                     op0=ALU.mult, op1=ALU.mult).then_inc(scale_ok, 1)
            for n, (a, k) in enumerate(pairs):
                dve.wait_ge(turned, n + 1)
                dve.tensor_copy(g.hT[:, :, a * 128:(a + k) * 128], tp[n % 3][:, :, 0:k * 128]).then_inc(out, 1)

        @block.scalar
        def _(act):
            act.wait_ge(v, 1 + 2 * NT)
            act.activation(std[:, :], mv[:, :, 1], ACT.Sqrt, bias=eps[:, 0:1]).then_inc(std_ok, 1)
            act.wait_ge(scale_ok, 1)
            for t in range(NT):
                act.activation(h[:, t, :], g.x[:, t, :], ACT.Relu, bias=shift[:, t:t + 1],
                               scale=rstd[:, t:t + 1]).then_inc(h_ok, 1)

        @block.tensor
        def _(pe):
            for n, (a, k) in enumerate(pairs):
                if n >= 3:
                    pe.wait_ge(out, n - 2)
                pe.wait_ge(h_ok, a + k)
                for q in range(k):
                    for f in range(2):
                        mm = pe.transpose(tp[n % 3][:, f, q * 128:(q + 1) * 128],
                                          h[:, a + q, f * 128:(f + 1) * 128], g.ident[:, :])
                mm.then_inc(turned, 1)


def cosine_attention(nc, g, wT_dram):
    with ExitStack() as ctx:
        s = Scope(nc, ctx, "cos")
        wT = s.sb("wT", [128, 2, D], F32)
        wh = s.sb("wh", [128, NT, D + 1], F32)
        whT = s.sb("whT", [128, 2, NP], F32)
        nsq = s.sb("nsq", [128, NT], F32)
        norm = s.sb("norm", [128, NT], F32)
        norm_row = s.sb("norm_row", [128, NP], F32)
        diag = s.sb("diag", [128, NT, 128], F16)
        den = s.sb("den", [128, 2, NP], F32)
        sim = s.sb("sim", [128, 2, NP], F32)
        sqT = sim
        probs = s.sb("probs", [128, NT, NP], F32)
        rsum = s.sb("rsum", [128, NT], F32)
        bank = [s.ps(f"bank{i}", [128, 512], F32) for i in range(8)]
        w_in, wh_mm, wh_out, whT_mm, whT_out, sq_ok, nb_mm, norm_ok, nsq_ok = (
            s.sem(k) for k in ("w_in", "wh_mm", "wh_out", "whT_mm", "whT_out", "sq_ok", "nb_mm", "norm_ok", "nsq_ok"))
        dot_mm, dot_used, exp_ok, probs_ok, agg_mm, agg_out, v = (
            s.sem(k) for k in ("dot_mm", "dot_used", "exp_ok", "probs_ok", "agg_mm", "agg_out", "v"))
        block = s.block()
        blocks = [(m, c) for m in range(2) for c in range(3)]

        @block.sync
        def _(sp):
            sp.dma_start(wT[:, :, :], wT_dram.rearrange("(k p) o -> p k o", p=128)).then_inc(w_in, 16)

        @block.tensor
        def _(pe):
            pe.wait_ge(w_in, 16)
            for n, (m, c) in enumerate(blocks):
                a, w = CH[c]
                if n >= 3:
                    pe.wait_ge(whT_out, n - 2)
                for k in range(2):
                    mm = pe.matmul(bank[n % 3][:, 0:w], wT[:, k, m * 128:(m + 1) * 128], g.hT[:, k, a:a + w],
                                   start=k == 0, stop=k == 1)
                mm.then_inc(whT_mm, 1)
            for t in range(NT):
                if t >= 3:
                    pe.wait_ge(wh_out, t - 2)
                    pe.wait_ge(nsq_ok, t - 2)
                for k in range(2):
                    mm = pe.matmul(bank[3 + t % 3][:, 0:D], g.hT[:, k, t * 128:(t + 1) * 128], wT[:, k, :],
                                   start=k == 0, stop=k == 1)
                mm.then_inc(wh_mm, 1)
            pe.wait_ge(whT_out, 6)
            pe.wait_ge(sq_ok, 2)
            for c, (a, w) in enumerate(CH):
                for k in range(2):
                    mm = pe.matmul(bank[c][:, 0:w], g.ones[:, :], sqT[:, k, a:a + w], start=k == 0, stop=k == 1)
                mm.then_inc(nb_mm, 1)
            pe.wait_ge(norm_ok, 4)
            pe.wait_ge(wh_out, NT)
            pe.wait_ge(nsq_ok, NT)
            for t in range(NT):
                for c, (a, w) in enumerate(CH):
                    n = 3 * t + c
                    if n >= 6:
                        pe.wait_ge(dot_used, n - 5)
                    for k in range(2):
                        mm = pe.matmul(bank[n % 6][:, 0:w], whT[:, k, t * 128:(t + 1) * 128], whT[:, k, a:a + w],
                                       start=k == 0, stop=k == 1)
                    mm.then_inc(dot_mm, 1)
            pe.wait_ge(dot_used, 3 * NT)
            for r in range(NT):
                if r >= 8:
                    pe.wait_ge(agg_out, r - 7)
                for t in range(NT):
                    pe.wait_ge(probs_ok, t + 1)
                    mm = pe.matmul(bank[r % 8][:, 0:D + 1], probs[:, t, r * 128:(r + 1) * 128], wh[:, t, :],
                                   start=t == 0, stop=t == NT - 1)
                mm.then_inc(agg_mm, 1)

        @block.scalar
        def _(act):
            for n, (m, c) in enumerate(blocks):
                a, w = CH[c]
                act.wait_ge(whT_mm, n + 1)
                act.activation(whT[:, m, a:a + w], bank[n % 3][:, 0:w], ACT.Copy).then_inc(whT_out, 1)
            for t in range(NT):
                act.wait_ge(wh_out, t + 1)
                act.activation(probs[:, t, 0:D], bank[3 + t % 3][:, 0:D], ACT.Square,
                               accum_out=nsq[:, t:t + 1]).then_inc(nsq_ok, 1)
            act.wait_ge(nsq_ok, NT)
            act.activation(norm[:, :], nsq[:, :], ACT.Sqrt).then_inc(norm_ok, 1)
            for c, (a, w) in enumerate(CH):
                act.wait_ge(nb_mm, c + 1)
                act.activation(norm_row[:, a:a + w], bank[c][:, 0:w], ACT.Sqrt).then_inc(norm_ok, 1)
            for t in range(NT):
                act.wait_ge(dot_used, 3 * t + 3)
                act.activation(sim[:, t % 2, :], sim[:, t % 2, :], ACT.Exp).then_inc(exp_ok, 1)

        @block.gpsimd
        def _(pool):
            for m in range(2):
                pool.wait_ge(whT_out, 3 * m + 3)
                pool.tensor_tensor(sqT[:, m, :], whT[:, m, :], whT[:, m, :], ALU.mult).then_inc(sq_ok, 1)

        @block.vector
        def _(dve):
            c_ = Chain(dve, v)
            c_.done(dve.memset(wh[:, :, D:D + 1], 1.0))
            for t in range(NT):
                dve.wait_ge(wh_mm, t + 1)
                dve.tensor_copy(wh[:, t, 0:D], bank[3 + t % 3][:, 0:D]).then_inc(wh_out, 1)
            for t in range(NT):
                c_.done(dve.tensor_tensor(diag[:, t, :], g.AT[:, t, t * 128:(t + 1) * 128], g.ident16[:, :], ALU.max))
            dve.wait_ge(norm_ok, 4)

            def mask(t):
                dve.wait_ge(exp_ok, t + 1)
                c_.wait()
                dve.tensor_tensor(probs[:, t, :], sim[:, t % 2, :], g.AT[:, t, :], ALU.mult).then_inc(v, 1)
                c_.n += 1
                c_.wait()
                dve.tensor_tensor(probs[:, t, t * 128:(t + 1) * 128], sim[:, t % 2, t * 128:(t + 1) * 128],
                                  diag[:, t, :], ALU.mult).then_inc(probs_ok, 1)

            for t in range(NT):
                if t >= 2:
                    dve.wait_ge(dot_used, 3 * (t - 1))
                c_.step(dve.tensor_scalar(den[:, t % 2, :], norm_row[:, :], norm[:, t:t + 1], 1e-8, ALU.mult, ALU.add))
                c_.step(dve.reciprocal(den[:, t % 2, :], den[:, t % 2, :]))
                if t >= 2:
                    dve.wait_ge(probs_ok, t - 1)
                for c, (a, w) in enumerate(CH):
                    n = 3 * t + c
                    dve.wait_ge(dot_mm, n + 1)
                    ins = dve.tensor_tensor(sim[:, t % 2, a:a + w], bank[n % 6][:, 0:w], den[:, t % 2, a:a + w],
                                            ALU.mult)
                    ins.then_inc(dot_used, 1)
                if t >= 1:
                    mask(t - 1)
            mask(NT - 1)
            for r in range(NT):
                dve.wait_ge(agg_mm, r + 1)
                c_.step(dve.reciprocal(rsum[:, r:r + 1], bank[r % 8][:, D:D + 1]))
                dve.scalar_tensor_tensor(out=g.x[:, r, :], in0=bank[r % 8][:, 0:D], scalar=rsum[:, r:r + 1],
                                         in1=g.x[:, r, :], op0=ALU.mult, op1=ALU.add).then_inc(agg_out, 1)


def gat(nc, g, tag, inT, KT, w_dram, ai_dram, aj_dram, H, O, val):
    with ExitStack() as ctx:
        s = Scope(nc, ctx, tag)
        b = Graph()
        b.wa = s.sb("wa", [128, KT, 2 * H], F32)
        b.sd = s.sb("sd", [128, NT, 2 * H], F32)
        b.hj = s.sb("hj", [128, NT, H], F32)
        b.f = s.sb("f", [128, NT, 2, H], F32)
        b.ri = s.sb("ri", [128, NT, H], F32)
        b.row = [s.sb(f"row{p}", [H, NP], F32R) for p in range(2)]
        b.val = val
        gat_prelude(nc, g, tag + "p", inT, KT, w_dram, ai_dram, aj_dram, H, O, b)
        near = nc.values_load(g.near[0:1, 0:1], min_val=0, max_val=1)
        with nc.If(near == 1):
            if H > 1:
                gat_heads(nc, g, tag + "h", H, O, b)
            else:
                gat_one_head(nc, g, tag + "h", O, b)
        with nc.Else():
            gat_rowwise(nc, g, tag + "r", inT, KT, w_dram, H, O, b)


SPREAD = 60.0
SPREAD16, WH_LOW, WH_HIGH, SCALE16 = 10.0, 0.5, 15.9, 4096.0


def gat_prelude(nc, g, tag, inT, KT, w_dram, ai_dram, aj_dram, H, O, b):
    HO, V1 = H * O, O + 1
    val, wa = b.val, b.wa
    with ExitStack() as ctx:
        s = Scope(nc, ctx, tag)
        w = s.sb("w", [128, KT, HO], F32)
        ab = s.sb("ab", [128, 2, HO], F32)
        prod = s.sb("prod", [128, 2, HO], F32)
        tops = s.sb("tops", [2 * H, 2, 3], F32)
        top = s.sb("top", [2 * H, 2], F32)
        dtop = s.sb("dtop", [2 * H, 2, 2 * H], F32)
        topb = s.sb("topb", [128, 4 * H], F32)
        dt = s.sb("dt", [H, H], F32)
        dcol = s.sb("dcol", [H, 1], F32)
        ok = s.sb("ok", [128, 2], F32)
        dn = s.sb("dn", [128, NT, H], F32)
        sn = s.sb("sn", [128, NT, H], F32)
        whmax = s.sb("whmax", [1, 3], F32)
        peaks = s.sb("peaks", [128, 2, NT], F32)
        absmax = s.sb("absmax", [128, 2], F32)
        rowf = s.sb("rowf", [H, NP], F32)
        sb_ = [s.ps(f"sb{i}", [128, 512], F32) for i in range(3)]
        ag = [s.ps(f"ag{i}", [128, 512], F32) for i in range(5)]
        v, w_in, a_in, wa_ok, sd_mm, top_ok, topb_mm, dn_mm, dn_ok, f_ok, wh_mm, val_ok, dcol_ok, relu_ok, exp_ok, hi_ok = (
            s.sem(k) for k in ("v", "w_in", "a_in", "wa_ok", "sd_mm", "top_ok", "topb_mm", "dn_mm", "dn_ok", "f_ok",
                               "wh_mm", "val_ok", "dcol_ok", "relu_ok", "exp_ok", "hi_ok"))
        peak_ok, max_ok, max_mm = (s.sem(k) for k in ("peak_ok", "max_ok", "max_mm"))
        block = s.block()

        @block.sync
        def _(sp):
            sp.dma_start(w[:, :, :], w_dram.rearrange("(k p) o -> p k o", p=128)).then_inc(w_in, 16)
            for n, a in enumerate((ai_dram, aj_dram)):
                k = a.shape[0]
                for r in range(HO // k):
                    sp.dma_start(ab[:, n, r * k:(r + 1) * k], a.partition_broadcast(128)).then_inc(a_in, 16)

        n_in = 16 * (HO // ai_dram.shape[0] + HO // aj_dram.shape[0])

        @block.tensor
        def _(pe):
            pe.wait_ge(w_in, 16)

            def wh(t):
                if t >= 3:
                    pe.wait_ge(val_ok, t - 2)
                    if H > 1:
                        pe.wait_ge(peak_ok, 2 * (t - 2))
                for k in range(KT):
                    mm = pe.matmul(ag[2 + t % 3][:, 0:HO], inT[:, k, t * 128:(t + 1) * 128], w[:, k, :],
                                   start=k == 0, stop=k == KT - 1)
                mm.then_inc(wh_mm, 1)

            for t in range(3):
                wh(t)
            pe.wait_ge(wa_ok, 2 * KT)
            for c, (a, wd) in enumerate(CH):
                for k in range(KT):
                    mm = pe.matmul(sb_[c][0:2 * H, 0:wd], wa[:, k, :], inT[:, k, a:a + wd],
                                   start=k == 0, stop=k == KT - 1)
                mm.then_inc(sd_mm, 1)
            for t in range(NT):
                for k in range(KT):
                    mm = pe.matmul(ag[0][:, t * 2 * H:(t + 1) * 2 * H], inT[:, k, t * 128:(t + 1) * 128], wa[:, k, :],
                                   start=k == 0, stop=k == KT - 1)
            mm.then_inc(dn_mm, 1)
            pe.wait_ge(top_ok, 1)
            pe.matmul(ag[1][:, 0:4 * H], g.ones[0:2 * H, :], dtop[:, :, :], start=True, stop=True).then_inc(topb_mm, 1)
            for t in range(3, NT):
                wh(t)
            if H > 1:
                pe.wait_ge(max_ok, 1)
                pe.transpose(ag[0][0:1, 0:128], absmax[:, 0:1], g.ident[:, :]).then_inc(max_mm, 1)

        @block.scalar
        def _(act):
            act.wait_ge(dn_ok, 2 if H > 1 else 1)
            act.activation(b.f[:, :, 0, :], dn[:, :, :], ACT.Exp, scale=0.2).then_inc(f_ok, 1)
            act.activation(b.hj[:, :, :], dn[:, :, :], ACT.Exp, scale=0.8).then_inc(f_ok, 1)
            if H > 1:
                act.activation(b.f[:, :, 1, :], dn[:, :, :], ACT.Exp).then_inc(f_ok, 1)
                act.activation(b.ri[:, :, :], sn[:, :, :], ACT.Exp, scale=-0.8).then_inc(f_ok, 1)
            act.wait_ge(dcol_ok, 1)
            for c, (a, wd) in enumerate(CH):
                ps = sb_[c][0:H, 0:wd]
                act.activation(ps, ps, ACT.Relu, bias=dcol[:, 0:1]).then_inc(relu_ok, 1)
                act.wait_ge(relu_ok, c + 1)
                act.activation(rowf[:, a:a + wd], ps, ACT.Exp, scale=-0.8).then_inc(exp_ok, 1)
            act.wait_ge(exp_ok, 3)
            act.activation(b.row[0][:, :], rowf[:, :], ACT.Copy).then_inc(hi_ok, 1)
            if H > 1:
                for t in range(NT):
                    act.wait_ge(wh_mm, t + 1)
                    act.activation(val[:, t, :].rearrange("p (h o) -> p h o", o=V1)[:, :, 0:O],
                                   ag[2 + t % 3][:, 0:HO].rearrange("p (h o) -> p h o", o=O),
                                   ACT.Copy).then_inc(val_ok, 1)

        @block.vector
        def _(dve):
            c_ = Chain(dve, v)
            dve.wait_ge(w_in, 16)
            dve.wait_ge(a_in, n_in)
            for n in range(2):
                for k in range(KT):
                    q = (n * KT + k) % 2
                    if n * KT + k >= 2:
                        dve.wait_ge(wa_ok, n * KT + k - 1)
                    c_.step(dve.tensor_tensor(prod[:, q, :], w[:, k, :], ab[:, n, :], ALU.mult))
                    dve.tensor_reduce(wa[:, k, n * H:(n + 1) * H], prod[:, q, :].rearrange("p (h o) -> p h o", h=H),
                                      axis=AX.X, op=ALU.add).then_inc(wa_ok, 1)
            for c, (a, wd) in enumerate(CHV):
                dve.wait_ge(sd_mm, c + 1)
                ps = sb_[c][0:2 * H, 0:wd]
                c_.done(dve.tensor_reduce(tops[:, 0, c:c + 1], ps, axis=AX.X, op=ALU.max))
                c_.done(dve.tensor_reduce(tops[:, 1, c:c + 1], ps, axis=AX.X, op=ALU.min))
            c_.wait()
            c_.done(dve.tensor_reduce(top[:, 0:1], tops[:, 0, :], axis=AX.X, op=ALU.max))
            c_.step(dve.tensor_reduce(top[:, 1:2], tops[:, 1, :], axis=AX.X, op=ALU.min))
            c_.step(dve.tensor_tensor(top[:, 1:2], top[:, 0:1], top[:, 1:2], ALU.subtract))
            c_.step(dve.tensor_scalar(dtop[:, 0, :], g.ident[0:2 * H, 0:2 * H], top[:, 0:1], None, ALU.mult))
            dve.tensor_scalar(dtop[:, 1, :], g.ident[0:2 * H, 0:2 * H], top[:, 1:2], None,
                              ALU.mult).then_inc(top_ok, 1)
            dve.wait_ge(topb_mm, 1)
            dve.wait_ge(dn_mm, 1)
            c_.step(dve.tensor_copy(topb[:, :], ag[1][:, 0:4 * H]))
            c_.step(dve.tensor_copy(b.sd[:, :, :], ag[0][:, 0:NT * 2 * H].rearrange("p (t h) -> p t h", h=2 * H)))
            tb = topb[:, H:2 * H].unsqueeze(1).broadcast_to([128, NT, H])
            if H > 1:
                c_.step(dve.tensor_tensor(sn[:, :, :], b.sd[:, :, 0:H], tb, ALU.add))
                dve.tensor_scalar(sn[:, :, :], sn[:, :, :], 0.0, None, ALU.max).then_inc(dn_ok, 1)
            dve.tensor_tensor(dn[:, :, :], b.sd[:, :, H:2 * H], tb, ALU.subtract).then_inc(dn_ok, 1)
            c_.step(dve.tensor_tensor(dt[:, :], topb[0:H, H:2 * H], g.ident[0:H, 0:H], ALU.mult))
            dve.tensor_reduce(dcol[:, :], dt[:, :], axis=AX.X, op=ALU.add).then_inc(dcol_ok, 1)
            if H == 1:
                dve.wait_ge(f_ok, 2)
                for t in range(NT):
                    dve.wait_ge(wh_mm, t + 1)
                    c_.done(dve.tensor_copy(val[:, t, O:V1], b.f[:, t, 0, :]))
                    dve.tensor_tensor(val[:, t, 0:O], ag[2 + t % 3][:, 0:O], b.f[:, t, 0, :].broadcast_to([128, O]),
                                      ALU.mult).then_inc(val_ok, 1)
            else:
                vals = val[:, :, :].rearrange("p t (h o) -> p t h o", o=V1)
                c_.done(dve.memset(vals[:, :, :, O], 1.0))
                for t in range(NT):
                    dve.wait_ge(val_ok, t + 1)
                    for n, op in enumerate((ALU.max, ALU.min)):
                        dve.tensor_reduce(peaks[:, n, t:t + 1], ag[2 + t % 3][:, 0:HO], axis=AX.X,
                                          op=op).then_inc(peak_ok, 1)
                dve.wait_ge(peak_ok, 2 * NT)
                c_.done(dve.tensor_reduce(absmax[:, 0:1], peaks[:, 0, :], axis=AX.X, op=ALU.max))
                c_.step(dve.tensor_reduce(absmax[:, 1:2], peaks[:, 1, :], axis=AX.X, op=ALU.min))
                dve.scalar_tensor_tensor(out=absmax[:, 0:1], in0=absmax[:, 1:2], scalar=-1.0, in1=absmax[:, 0:1],
                                         op0=ALU.mult, op1=ALU.max).then_inc(max_ok, 1)
                dve.wait_ge(f_ok, 4)
                c_.step(dve.tensor_scalar(b.f[:, :, :, :], b.f[:, :, :, :], SCALE16, None, ALU.mult))
                dve.wait_ge(max_mm, 1)
                c_.step(dve.tensor_reduce(whmax[:, 0:1], ag[0][0:1, 0:128], axis=AX.X, op=ALU.max))
                c_.step(dve.tensor_scalar(whmax[:, 1:2], whmax[:, 0:1], WH_LOW, None, ALU.is_ge))
                c_.step(dve.tensor_scalar(whmax[:, 2:3], whmax[:, 0:1], WH_HIGH, None, ALU.is_le))
                c_.step(dve.tensor_tensor(whmax[:, 1:2], whmax[:, 1:2], whmax[:, 2:3], ALU.mult))
            c_.step(dve.tensor_reduce(ok[:, 0:1], topb[:, 3 * H:4 * H], axis=AX.X, op=ALU.max))
            c_.step(dve.tensor_scalar(ok[:, 0:1], ok[:, 0:1], SPREAD16 if H > 1 else SPREAD, None, ALU.is_le))
            c_.step(dve.tensor_scalar(ok[:, 1:2], g.fewest[:, 0:1], 0.5, None, ALU.is_gt))
            if H > 1:
                c_.step(dve.tensor_tensor(ok[0:1, 0:1], ok[0:1, 0:1], whmax[:, 1:2], ALU.mult))
            c_.step(dve.tensor_tensor(g.near[:, :], ok[0:1, 0:1], ok[0:1, 1:2], ALU.mult))
            dve.wait_ge(hi_ok, 1)
            c_.step(dve.tensor_tensor(b.row[1][:, :], rowf[:, :], b.row[0][:, :].bitcast(F32), ALU.subtract))


def hold(eng, sem, value, passed):
    eng.wait_ge(sem, value)
    eng.sem_inc(passed, 1)


def head_pairs(eng, H, body):
    with eng.Fori(0, H // 2 - 1) as pair:
        body(pair * 2, 0, 2)
        body(pair * 2 + 1, 1, 2)
    body(H - 2, 0, 1)
    body(H - 1, 1, 0)


def gat_heads(nc, g, tag, H, O, b):
    V1 = O + 1
    G = 2 if 8 * V1 <= 512 else 1
    groups = [(a, k) for c in CH for a in range(c[0] // 128, (c[0] + c[1]) // 128, G)
              for k in (min(G, (c[0] + c[1]) // 128 - a),)]
    NG, NB = len(groups), 4
    in_chunk = [[n for n, (a, k) in enumerate(groups) if c[0] <= a * 128 < c[0] + c[1]] for c in CH]
    val, hj = b.val, b.hj
    with ExitStack() as ctx:
        s = Scope(nc, ctx, tag)
        sel = [s.sb(f"sel{e}", [H, 128], F32R) for e in range(2)]
        vf = s.sb("vf", [128, NT, 2, V1], F32)
        vv = [s.sb(f"vv{e}", [128, NT, 6, V1], F16) for e in range(2)]
        row = s.sb("row", [128, 3, 512], F32)
        neg = [s.sb(f"neg{c}", [128, NT, CH[c][1]], F16) for c in range(3)]
        parts = [s.sb(f"parts{e}", [128, NT, 4, V1], F32) for e in range(2)]
        both = s.sb("both", [128, NT, 2, V1], F32)
        sb_ = [s.ps(f"sb{i}", [128, 512], F32) for i in range(3)]
        ag = [s.ps(f"ag{i}", [128, 512], F32) for i in range(NB)]
        sel_ok, vf_ok, vhi_ok, vlo_ok, vneg_ok, s_mm, row_ok, neg_ok, agg_mm, agg_out, sum_ok, val_ok, passed = (
            s.sem(k) for k in ("sel_ok", "vf_ok", "vhi_ok", "vlo_ok", "vneg_ok", "s_mm", "row_ok", "neg_ok", "agg_mm",
                               "agg_out", "sum_ok", "val_ok", "passed"))
        block = s.block()

        @block.sync
        def _(sp):
            sp.sem_inc(passed, 1)

        @block.tensor
        def _(pe):
            def rows(h, e, c):
                a, wd = CH[c]
                pe.wait_ge(sel_ok, h + 1)
                if not (isinstance(h, int) and h == 0):
                    pe.wait_ge(row_ok, 3 * (h - 1) + c + 1)
                pe.matmul(sb_[c][:, 0:wd], sel[e][:, :], b.row[0][:, a:a + wd], start=True, stop=False)
                pe.matmul(sb_[c][:, 0:wd], sel[e][:, :], b.row[1][:, a:a + wd], start=False, stop=True).then_inc(s_mm, 1)

            for c in range(3):
                rows(0, 0, c)

            def head(h, e, follow):
                pe.wait_ge(vneg_ok, h + 1)
                for c in range(3):
                    if follow:
                        rows(h + 1, 1 - e, c)
                    for n in in_chunk[c]:
                        a, k = groups[n]
                        last = n - NB if n >= NB else max(m for m in range(NG) if m % NB == n % NB) - NG
                        pe.wait_ge(agg_out, NG * h + last + 1 + NG)
                        for i in range(k):
                            off = (a + i) * 128 - CH[c][0]
                            out = ag[n % NB][:, i * 4 * V1:(i + 1) * 4 * V1]
                            for t in range(NT):
                                if n == in_chunk[c][0] and i == 0:
                                    pe.wait_ge(neg_ok, 3 * NT * h + NT * c + t + 1)
                                pe.matmul(out, neg[c][:, t, off:off + 128], vv[e][:, t, 0:4, :],
                                          start=t == 0, stop=False)
                                mm = pe.matmul(out[:, 2 * V1:4 * V1], g.AT[:, t, (a + i) * 128:(a + i + 1) * 128],
                                               vv[e][:, t, 4:6, :], start=False, stop=t == NT - 1)
                        mm.then_inc(agg_mm, 1)

            head_pairs(pe, H, head)

        @block.gpsimd
        def _(pool):
            pool.sem_inc(agg_out, NG)
            pool.sem_inc(val_ok, 2)

            def select(h, e):
                src = g.ident[0:H, h:h + 1] if isinstance(h, int) else g.ident[0:H, bass.ds(h, 1)]
                pool.tensor_copy(sel[e][:, :], src.broadcast_to([H, 128])).then_inc(sel_ok, 1)

            def values(h, e):
                pool.tensor_tensor(vf[:, :, :, :],
                                   val[:, :, bass.ds(h * V1, V1)].unsqueeze(2).broadcast_to([128, NT, 2, V1]),
                                   b.f[:, :, :, bass.ds(h, 1)].broadcast_to([128, NT, 2, V1]),
                                   ALU.mult).then_inc(vf_ok, 1)
                pool.wait_ge(vhi_ok, h + 1)
                pool.tensor_tensor(vv[e][:, :, 1:6:4, :], vf[:, :, :, :], vv[e][:, :, 0:5:4, :],
                                   ALU.subtract).then_inc(vlo_ok, 1)

            def total(h, e):
                pool.wait_ge(val_ok, h + 2)
                pool.wait_ge(agg_out, NG * h + NG + NG)
                pool.tensor_tensor(both[:, :, :, :], parts[e][:, :, 0:4:2, :], parts[e][:, :, 1:4:2, :],
                                   ALU.add).then_inc(sum_ok, 1)
                hold(pool, sum_ok, 2 * h + 1, passed)
                pool.tensor_tensor(both[:, :, 0, :], both[:, :, 0, :],
                                   b.ri[:, :, bass.ds(h, 1)].broadcast_to([128, NT, V1]), ALU.mult).then_inc(sum_ok, 1)
                hold(pool, sum_ok, 2 * h + 2, passed)
                pool.tensor_tensor(val[:, :, bass.ds(h * V1, V1)], both[:, :, 0, :], both[:, :, 1, :],
                                   ALU.add).then_inc(val_ok, 1)

            select(0, 0)
            values(0, 0)
            select(1, 1)
            hold(pool, vlo_ok, 1, passed)
            values(1, 1)

            def head(h, e, follow):
                total(h, e)
                if follow == 2:
                    hold(pool, vlo_ok, h + 2, passed)
                    hold(pool, val_ok, h + 3, passed)
                    select(h + 2, e)
                    values(h + 2, e)

            head_pairs(pool, H, head)

        @block.scalar
        def _(act):
            def rows(h, c):
                wd = CH[c][1]
                act.wait_ge(s_mm, 3 * h + c + 1)
                if not (isinstance(h, int) and h == 0):
                    act.wait_ge(neg_ok, 3 * NT * (h - 1) + NT * (c + 1))
                act.activation(row[:, c, 0:wd], sb_[c][:, 0:wd], ACT.Copy).then_inc(row_ok, 1)

            def high(h, e):
                act.wait_ge(vf_ok, h + 1)
                act.activation(vv[e][:, :, 0:5:4, :], vf[:, :, :, :], ACT.Copy).then_inc(vhi_ok, 1)

            def negate(h, e):
                act.wait_ge(vlo_ok, h + 1)
                act.activation(vv[e][:, :, 2:4, :], vv[e][:, :, 4:6, :], ACT.Copy, scale=-1.0).then_inc(vneg_ok, 1)

            for c in range(3):
                rows(0, c)
            high(0, 0)
            negate(0, 0)

            def head(h, e, follow):
                act.wait_ge(val_ok, h + 1)
                for c in range(3):
                    if follow:
                        rows(h + 1, c)
                    for n in in_chunk[c]:
                        a, k = groups[n]
                        act.wait_ge(agg_mm, NG * h + n + 1)
                        act.activation(parts[e][:, a:a + k, :, :],
                                       ag[n % NB][:, 0:k * 4 * V1].rearrange("p (i q o) -> p i q o", q=4, o=V1),
                                       ACT.Copy).then_inc(agg_out, 1)
                    if follow and c == 0:
                        high(h + 1, 1 - e)
                    if follow and c == 1:
                        negate(h + 1, 1 - e)

            head_pairs(act, H, head)

        @block.vector
        def _(dve):
            def head(h, e, follow):
                for c in range(3):
                    a, wd = CH[c]
                    dve.wait_ge(row_ok, 3 * h + c + 1)
                    dve.wait_ge(agg_out, NG * h + in_chunk[c][-1] + 1)
                    for t in range(NT):
                        dve.scalar_tensor_tensor(out=neg[c][:, t, :], in0=row[:, c, 0:wd],
                                                 scalar=hj[:, t, bass.ds(h, 1)], in1=g.AT[:, t, a:a + wd],
                                                 op0=ALU.is_ge, op1=ALU.mult).then_inc(neg_ok, 1)

            head_pairs(dve, H, head)


def gat_one_head(nc, g, tag, O, b):
    V1 = O + 1
    NB = 4
    with ExitStack() as ctx:
        s = Scope(nc, ctx, tag)
        sel = s.sb("sel", [1, 128], F32R)
        row = s.sb("row", [128, 3, 512], F32)
        pt = [s.sb(f"pt{c}", [128, NT, CH[c][1]], F32) for c in range(3)]
        sb_ = [s.ps(f"sb{i}", [128, 512], F32) for i in range(3)]
        ag = [s.ps(f"ag{i}", [128, 512], F32) for i in range(NB)]
        sel_ok, s_mm, row_ok, pt_ok, agg_mm, agg_out, sp_passed = (
            s.sem(k) for k in ("sel_ok", "s_mm", "row_ok", "pt_ok", "agg_mm", "agg_out", "sp_passed"))
        block = s.block()

        @block.sync
        def _(sp):
            sp.sem_inc(sp_passed, 1)

        @block.gpsimd
        def _(pool):
            pool.tensor_copy(sel[:, :], g.ones[0:1, :]).then_inc(sel_ok, 1)

        @block.tensor
        def _(pe):
            pe.wait_ge(sel_ok, 1)
            for c, (a, wd) in enumerate(CH):
                pe.matmul(sb_[c][:, 0:wd], sel[:, :], b.row[0][:, a:a + wd], start=True, stop=False)
                pe.matmul(sb_[c][:, 0:wd], sel[:, :], b.row[1][:, a:a + wd], start=False, stop=True).then_inc(s_mm, 1)
            for r in range(NT):
                c = r // 4
                if r >= NB:
                    pe.wait_ge(agg_out, r - NB + 1)
                for t in range(NT):
                    if r % 4 == 0:
                        pe.wait_ge(pt_ok, NT * c + t + 1)
                    mm = pe.matmul(ag[r % NB][:, 0:V1], pt[c][:, t, (r % 4) * 128:(r % 4 + 1) * 128], b.val[:, t, :],
                                   start=t == 0, stop=t == NT - 1)
                mm.then_inc(agg_mm, 1)

        @block.scalar
        def _(act):
            for c, (a, wd) in enumerate(CH):
                act.wait_ge(s_mm, c + 1)
                act.activation(row[:, c, 0:wd], sb_[c][:, 0:wd], ACT.Copy).then_inc(row_ok, 1)
            for r in range(NT):
                act.wait_ge(agg_mm, r + 1)
                act.activation(g.sums1[:, r, :], ag[r % NB][:, 0:V1], ACT.Copy).then_inc(agg_out, 1)

        @block.vector
        def _(dve):
            for c, (a, wd) in enumerate(CH):
                dve.wait_ge(row_ok, c + 1)
                for t in range(NT):
                    dve.scalar_tensor_tensor(out=pt[c][:, t, :], in0=row[:, c, 0:wd], scalar=b.hj[:, t, 0:1],
                                             in1=g.AT[:, t, a:a + wd], op0=ALU.max, op1=ALU.mult).then_inc(pt_ok, 1)


NEG = -9e15


def gat_rowwise(nc, g, tag, inT, KT, w_dram, H, O, b):
    V1, HO = O + 1, H * O
    val = b.val
    with ExitStack() as ctx:
        s = Scope(nc, ctx, tag)
        w = s.sb("w", [128, KT, HO], F32)
        wab = s.sb("wab", [128, KT, 128], F32)
        vh = s.sb("vh", [128, NT, V1], F32)
        drow = s.sb("drow", [128, NP], F32)
        e = s.sb("e", [128, NP], F32)
        bias = s.sb("bias", [128, NP], F32)
        p = s.sb("p", [128, NP], F32)
        pT = s.sb("pT", [128, NT, 128], F32)
        neg, total, inv = (s.sb(k, [128, 1], F32) for k in ("neg", "total", "inv"))
        bank = [s.ps(f"bank{i}", [128, 512], F32) for i in range(8)]
        w_in, wh_mm, val_ok, copied, d_mm, d_ok, v, sc_ok, p_ok, pn_ok, t_mm, t_ok, a_mm, a_ok, passed = (
            s.sem(k) for k in ("w_in", "wh_mm", "val_ok", "copied", "d_mm", "d_ok", "v", "sc_ok", "p_ok", "pn_ok",
                               "t_mm", "t_ok", "a_mm", "a_ok", "passed"))
        block = s.block()

        @block.sync
        def _(sp):
            sp.dma_start(w[:, :, :], w_dram.rearrange("(k p) o -> p k o", p=128)).then_inc(w_in, 16)

        @block.gpsimd
        def _(pool):
            pool.memset(p[:, N:NP], 0.0).then_inc(copied, 1)
            pool.wait_ge(copied, 1)
            pool.wait_ge(val_ok, NT)
            pool.sem_inc(a_ok, 1)
            with pool.Fori(0, H) as h:
                pool.wait_ge(a_ok, NT * h + 1)
                pool.sem_inc(passed, 1)
                pool.tensor_copy(wab[:, :, :], b.wa[:, :, bass.ds(h + H, 1)].broadcast_to([128, KT, 128])).then_inc(copied, 1)
                pool.tensor_copy(vh[:, :, :], val[:, :, bass.ds(h * V1, V1)]).then_inc(copied, 1)

        @block.tensor
        def _(pe):
            pe.wait_ge(w_in, 16)
            for t in range(NT):
                if t >= 2:
                    pe.wait_ge(val_ok, t - 1)
                for k in range(KT):
                    mm = pe.matmul(bank[t % 2][:, 0:HO], inT[:, k, t * 128:(t + 1) * 128], w[:, k, :],
                                   start=k == 0, stop=k == KT - 1)
                mm.then_inc(wh_mm, 1)
            with pe.Fori(0, H) as h:
                pe.wait_ge(copied, 2 * h + 3)
                for c, (a, wd) in enumerate(CH):
                    for k in range(KT):
                        mm = pe.matmul(bank[2 + c][:, 0:wd], wab[:, k, :], inT[:, k, a:a + wd],
                                       start=k == 0, stop=k == KT - 1)
                    mm.then_inc(d_mm, 1)
                for r in range(NT):
                    pe.wait_ge(pn_ok, NT * h + r + 1)
                    for t in range(NT):
                        mm = pe.transpose(bank[5 + t // 4][:, (t % 4) * 128:(t % 4 + 1) * 128],
                                          p[:, t * 128:(t + 1) * 128], g.ident[:, :])
                    mm.then_inc(t_mm, 1)
                    pe.wait_ge(t_ok, 3 * (NT * h + r) + 3)
                    for t in range(NT):
                        mm = pe.matmul(bank[0][:, 0:V1], pT[:, t, :], vh[:, t, :], start=t == 0, stop=t == NT - 1)
                    mm.then_inc(a_mm, 1)

        @block.scalar
        def _(act):
            with act.Fori(0, H) as h:
                for r in range(NT):
                    act.wait_ge(sc_ok, NT * h + r + 1)
                    act.activation(p[:, 0:N], e[:, 0:N], ACT.Exp, bias=neg[:, 0:1],
                                   accum_out=total[:, 0:1]).then_inc(p_ok, 1)
                    act.wait_ge(a_mm, NT * h + r + 1)
                    act.sem_inc(passed, 1)
                    act.activation(val[:, r, bass.ds(h * V1, V1)], bank[0][:, 0:V1], ACT.Copy).then_inc(a_ok, 1)

        @block.vector
        def _(dve):
            dve.sem_inc(v, 1)
            for t in range(NT):
                dve.wait_ge(wh_mm, t + 1)
                vv = val[:, t, :].rearrange("p (h o) -> p h o", o=V1)
                dve.memset(vv[:, :, O:V1], 1.0).then_inc(v, 1)
                dve.tensor_copy(vv[:, :, 0:O], bank[t % 2][:, 0:HO].rearrange("p (h o) -> p h o", o=O)).then_inc(val_ok, 1)
            dve.wait_ge(v, 1 + NT)
            first = 1 + NT
            S = 6
            with dve.Fori(0, H) as h:
                for c, (a, wd) in enumerate(CH):
                    dve.wait_ge(d_mm, 3 * h + c + 1)
                    dve.tensor_copy(drow[:, a:a + wd], bank[2 + c][:, 0:wd]).then_inc(d_ok, 1)
                dve.wait_ge(d_ok, 3 * h + 3)
                for r in range(NT):
                    base = first + S * (NT * h + r)
                    dve.wait_ge(a_ok, NT * h + r + 1)
                    dve.tensor_scalar(e[:, 0:N], drow[:, 0:N], b.sd[:, r, bass.ds(h, 1)], None, ALU.add).then_inc(v, 1)
                    dve.tensor_scalar(bias[:, 0:N], g.A[:, r, 0:N], -1.0, -NEG, ALU.add, ALU.mult).then_inc(v, 1)
                    dve.wait_ge(v, base + 2)
                    dve.scalar_tensor_tensor(out=e[:, 0:N], in0=e[:, 0:N], scalar=0.2, in1=e[:, 0:N],
                                             op0=ALU.mult, op1=ALU.max).then_inc(v, 1)
                    dve.wait_ge(v, base + 3)
                    dve.tensor_tensor(e[:, 0:N], e[:, 0:N], bias[:, 0:N], ALU.add).then_inc(v, 1)
                    dve.wait_ge(v, base + 4)
                    dve.tensor_reduce(neg[:, :], e[:, 0:N], axis=AX.X, op=ALU.max).then_inc(v, 1)
                    dve.wait_ge(v, base + 5)
                    dve.tensor_scalar(neg[:, :], neg[:, :], -1.0, None, ALU.mult).then_inc(sc_ok, 1)
                    dve.wait_ge(p_ok, NT * h + r + 1)
                    dve.reciprocal(inv[:, :], total[:, :]).then_inc(v, 1)
                    dve.wait_ge(v, base + 6)
                    dve.tensor_scalar(p[:, 0:N], p[:, 0:N], inv[:, 0:1], None, ALU.mult).then_inc(pn_ok, 1)
                    dve.wait_ge(t_mm, NT * h + r + 1)
                    for q in range(3):
                        k = min(4, NT - 4 * q)
                        dve.tensor_copy(pT[:, 4 * q:4 * q + k, :],
                                        bank[5 + q][:, 0:k * 128].rearrange("p (t i) -> p t i", i=128)).then_inc(t_ok, 1)


def normalise_elu(nc, g, tag, raw, H, O, outT):
    HO, V1 = H * O, O + 1
    F = HO // 128
    with ExitStack() as ctx:
        s = Scope(nc, ctx, tag)
        inv = s.sb("inv", [128, NT, H], F32)
        xn, e, y = (s.sb(k, [128, 2, HO], F32) for k in ("xn", "e", "y"))
        tp = [s.ps(f"tp{i}", [128, F, 128], F32) for i in range(3)]
        v, neg_ok, exp_ok, y_ok, turned, out = (s.sem(k) for k in ("v", "neg_ok", "exp_ok", "y_ok", "turned", "out"))
        block = s.block()

        @block.vector
        def _(dve):
            c = Chain(dve, v)
            r4 = raw[:, :, :].rearrange("p t (h o) -> p t h o", o=V1)
            c.step(dve.reciprocal(inv[:, :, :], r4[:, :, :, O]))

            def finish(t):
                b = t % 2
                dve.wait_ge(exp_ok, t + 1)
                c.step(dve.tensor_scalar(e[:, b, :], e[:, b, :], -1.0, None, ALU.add))
                if t >= 2:
                    dve.wait_ge(turned, t - 1)
                dve.scalar_tensor_tensor(out=y[:, b, :], in0=xn[:, b, :], scalar=0.0, in1=e[:, b, :],
                                         op0=ALU.max, op1=ALU.add).then_inc(y_ok, 1)

            for t in range(NT):
                b = t % 2
                if t >= 2:
                    dve.wait_ge(y_ok, t - 1)
                c.step(dve.tensor_tensor(xn[:, b, :].rearrange("p (h o) -> p h o", o=O), r4[:, t, :, 0:O],
                                         inv[:, t, :].unsqueeze(2).broadcast_to([128, H, O]), ALU.mult))
                dve.tensor_scalar(e[:, b, :], xn[:, b, :], 0.0, None, ALU.min).then_inc(neg_ok, 1)
                if t >= 1:
                    finish(t - 1)
            finish(NT - 1)

        @block.scalar
        def _(act):
            for t in range(NT + 1):
                if t < NT:
                    act.wait_ge(neg_ok, t + 1)
                    act.activation(e[:, t % 2, :], e[:, t % 2, :], ACT.Exp).then_inc(exp_ok, 1)
                if t >= 1:
                    act.wait_ge(turned, t)
                    act.activation(outT[:, :, (t - 1) * 128:t * 128], tp[(t - 1) % 3][:, :, :],
                                   ACT.Copy).then_inc(out, 1)

        @block.tensor
        def _(pe):
            for t in range(NT):
                pe.wait_ge(y_ok, t + 1)
                if t >= 3:
                    pe.wait_ge(out, t - 2)
                for f in range(F):
                    mm = pe.transpose(tp[t % 3][:, f, :], y[:, t % 2, f * 128:(f + 1) * 128], g.ident[:, :])
                mm.then_inc(turned, 1)


def mlp(nc, g, tag, inT, w1T_dram, b1_dram, func, w2T_dram, b2_dram, check_symmetry=False):
    M = w1T_dram.shape[1]
    F = M // 128
    with ExitStack() as ctx:
        s = Scope(nc, ctx, tag)
        w1 = s.sb("w1", [128, 2, M], F32)
        w2 = s.sb("w2", [128, F, D], F32)
        b1 = s.sb("b1", [128, F], F32)
        b2 = s.sb("b2", [1, D], F32)
        z = s.sb("z", [128, F, NP], F32)
        bank = [s.ps(f"bank{i}", [128, 512], F32) for i in range(8)]
        w_in, z_mm, z_ok, y_mm, y_ok = (s.sem(k) for k in ("w_in", "z_mm", "z_ok", "y_mm", "y_ok"))
        block = s.block()
        blocks = [(c, m) for c in range(3) for m in range(F)]
        if check_symmetry:
            diff = s.sb("diff", [128, NT, N], F16)
            most = s.sb("most", [128, 4], F32)
            v, most_ok, all_ok = s.sem("v"), s.sem("most_ok"), s.sem("all_ok")

            @block.gpsimd
            def _(pool):
                pool.wait_ge(most_ok, 1)
                pool.partition_all_reduce(most[:, 1:2], most[:, 0:1], 128, RMAX).then_inc(all_ok, 1)

        @block.sync
        def _(sp):
            sp.dma_start(w1[:, :, :], w1T_dram.rearrange("(k p) o -> p k o", p=128)).then_inc(w_in, 16)
            sp.dma_start(b1[:, :], b1_dram).then_inc(w_in, 16)
            sp.dma_start(w2[:, :, :], w2T_dram.rearrange("(k p) o -> p k o", p=128)).then_inc(w_in, 16)
            sp.dma_start(b2[:, :], b2_dram.unsqueeze(0)).then_inc(w_in, 16)

        @block.tensor
        def _(pe):
            pe.wait_ge(w_in, 64)
            for n, (c, m) in enumerate(blocks):
                a, w = CH[c]
                if n >= 4:
                    pe.wait_ge(z_ok, n - 3)
                for k in range(2):
                    mm = pe.matmul(bank[n % 4][:, 0:w], w1[:, k, m * 128:(m + 1) * 128], inT[:, k, a:a + w],
                                   start=k == 0, stop=k == 1)
                mm.then_inc(z_mm, 1)
            for t in range(NT):
                pe.wait_ge(z_ok, F * (t // 4 + 1))
                if t >= 4:
                    pe.wait_ge(y_ok, t - 3)
                for k in range(F):
                    pe.matmul(bank[4 + t % 4][:, 0:D], z[:, k, t * 128:(t + 1) * 128], w2[:, k, :],
                              start=k == 0, stop=False)
                pe.matmul(bank[4 + t % 4][:, 0:D], g.ones[0:1, :], b2[:, :], start=False, stop=True).then_inc(y_mm, 1)

        @block.scalar
        def _(act):
            act.wait_ge(w_in, 64)
            for n, (c, m) in enumerate(blocks):
                a, w = CH[c]
                act.wait_ge(z_mm, n + 1)
                act.activation(z[:, m, a:a + w], bank[n % 4][:, 0:w], func, bias=b1[:, m:m + 1]).then_inc(z_ok, 1)

        @block.vector
        def _(dve):
            if check_symmetry:
                c = Chain(dve, v)
                c.step(dve.tensor_tensor(diff[:, :, :], g.A[:, :, 0:N], g.AT[:, :, 0:N], ALU.subtract))
                dve.tensor_reduce(most[:, 0:1], diff[:, :, :], axis=AX.XY, op=ALU.max).then_inc(most_ok, 1)
                dve.wait_ge(all_ok, 1)
                c.step(dve.tensor_scalar(g.symmetric[:, :], most[0:1, 1:2], 0.0, None, ALU.is_le))
            for t in range(NT):
                dve.wait_ge(y_mm, t + 1)
                dve.tensor_tensor(g.x[:, t, :], bank[4 + t % 4][:, 0:D], g.x[:, t, :], ALU.add).then_inc(y_ok, 1)


STATE_SCALE = 1024.0


def gated_graph(nc, g, d):
    symmetric = nc.values_load(g.symmetric[0:1, 0:1], min_val=0, max_val=1)
    with nc.If(symmetric == 1):
        gated_network(nc, g, d, "s", 1)
    with nc.Else():
        gated_network(nc, g, d, "a", 2)


def gated_network(nc, g, d, tag, sides):
    with ExitStack() as ctx:
        s = Scope(nc, ctx, "ggnn" + tag)
        gw = [s.sb(f"gw{i}", [128, 2 * sides + 2, 3 * D], F32R) for i in range(2)]
        bw = s.sb("bw", [6, 3 * D], F32R)
        deg = s.sb("deg", [6, N], F32R)
        nm = [s.sb(f"nm{i}", [128, NT, D], F16) for i in range(2)]
        gate_weights(nc, g, d, tag, sides, gw, bw, deg, nm)
        gated_steps(nc, g, tag, sides, gw, bw, deg, nm)


def gate_weights(nc, g, d, tag, sides, gw, bw, deg, nm):
    with ExitStack() as ctx:
        s = Scope(nc, ctx, "gate" + tag)
        win = s.sb("win", [128, 2, 2, D], F32)
        wst = s.sb("wst", [128, 6, 3 * D], F32)
        bcol = s.sb("bcol", [128, 2, 2], F32)
        brow = s.sb("brow", [1, 3 * D], F32)
        blhs = s.sb("blhs", [128, 2, 2, 6], F32)
        elhs = s.sb("elhs", [1, 6], F32)
        dlhs = s.sb("dlhs", [128, 2, 6], F16)
        dl1 = s.sb("dl1", [1, 6], F16)
        one16 = s.sb("one16", [1, 512], F16)
        first3 = s.sb("first3", [6, 1], F32)
        last3 = s.sb("last3", [6, 1], F32)
        bhi = s.sb("bhi", [6, 3 * D], F32R)
        blo = s.sb("blo", [6, 3 * D], F32)
        bank = [s.ps(f"bank{i}", [128, 512], F32) for i in range(8)]
        w_in, v, lhs_ok, g_mm, hi_ok, lo_ok, b_mm, b_ok, d_mm, d_ok, turned, nhi, nlo = (
            s.sem(k) for k in ("w_in", "v", "lhs_ok", "g_mm", "hi_ok", "lo_ok", "b_mm", "b_ok", "d_mm", "d_ok",
                               "turned", "nhi", "nlo"))
        block = s.block()
        HALF = 3 * D // 2
        prods = [(side, k, n) for side in range(sides) for k in range(2) for n in range(2)]
        own = 2 * sides
        n_in = 16 * 10

        @block.sync
        def _(sp):
            for i, name in enumerate(("in_W", "out_W")):
                sp.dma_start(win[:, i, :, :], d[name].rearrange("(k p) o -> p k o", p=128)).then_inc(w_in, 16)
            for i, name in enumerate(("r_WT", "z_WT", "h_WT")):
                sp.dma_start(wst[:, :, i * D:(i + 1) * D],
                             d[name].rearrange("(k p) o -> p k o", p=128)).then_inc(w_in, 16)
            for i, name in enumerate(("in_b", "out_b")):
                sp.dma_start(bcol[:, i, :], d[name]).then_inc(w_in, 16)
            for i, name in enumerate(("r_b", "z_b", "h_b")):
                sp.dma_start(brow[:, i * D:(i + 1) * D], d[name].unsqueeze(0)).then_inc(w_in, 16)

        @block.gpsimd
        def _(pool):
            n = 0
            for m in (blhs, elhs, dlhs, dl1):
                ap = m[:, :, :, :] if m is blhs else m[:, :, :] if m is dlhs else m[:, :]
                n += 1
                pool.memset(ap, 0.0).then_inc(lhs_ok, 1)
                pool.wait_ge(lhs_ok, n)
            pool.memset(one16[:, :], 1.0).then_inc(lhs_ok, 1)
            pool.wait_ge(lhs_ok, 5)
            pool.wait_ge(w_in, n_in)
            for q in range(2):
                for side in range(2):
                    pool.tensor_copy(blhs[:, side, :, side + 3 * q], bcol[:, side, :]).then_inc(lhs_ok, 1)
                    pool.memset(dlhs[:, side, side + 3 * q:side + 3 * q + 1], 1.0).then_inc(lhs_ok, 1)
                pool.memset(elhs[:, 2 + 3 * q:3 + 3 * q], 1.0).then_inc(lhs_ok, 1)
                pool.memset(dl1[:, 2 + 3 * q:3 + 3 * q], 1.0).then_inc(lhs_ok, 1)

        @block.tensor
        def _(pe):
            pe.wait_ge(w_in, n_in)
            for n, (side, k, half) in enumerate(prods):
                if n >= 4:
                    pe.wait_ge(lo_ok, n - 3)
                terms = [(sd, o) for sd in ((side,) if sides == 2 else (0, 1)) for o in range(2)]
                for i, (sd, o) in enumerate(terms):
                    mm = pe.matmul(bank[n % 4][:, 0:HALF], win[:, sd, o, k * 128:(k + 1) * 128],
                                   wst[:, 2 * sd + o, half * HALF:(half + 1) * HALF],
                                   start=i == 0, stop=i == len(terms) - 1)
                mm.then_inc(g_mm, 1)
            pe.wait_ge(lhs_ok, 17)
            for half in range(2):
                cols = slice(half * HALF, (half + 1) * HALF)
                for side in range(2):
                    for o in range(2):
                        pe.matmul(bank[4 + half][0:6, 0:HALF], blhs[:, side, o, :], wst[:, 2 * side + o, cols],
                                  start=side + o == 0, stop=False)
                pe.matmul(bank[4 + half][0:6, 0:HALF], elhs[:, :], brow[:, cols], start=False, stop=True).then_inc(b_mm, 1)
            for c, (a, w) in enumerate(CHV):
                if c == 2:
                    pe.wait_ge(d_ok, 1)
                for t in range(NT):
                    pe.matmul(bank[6 + c % 2][0:6, 0:w], dlhs[:, 0, :], g.AT[:, t, a:a + w], start=t == 0, stop=False)
                    pe.matmul(bank[6 + c % 2][0:6, 0:w], dlhs[:, 1, :], g.A[:, t, a:a + w], start=False, stop=False)
                pe.matmul(bank[6 + c % 2][0:6, 0:w], dl1[:, :], one16[:, 0:w], start=False, stop=True).then_inc(d_mm, 1)
            pe.wait_ge(b_ok, 2)
            pe.wait_ge(lo_ok, len(prods) + 4)
            for t in range(NT):
                if t >= 4:
                    pe.wait_ge(nlo, t - 3)
                for f in range(2):
                    mm = pe.transpose(bank[t % 4][:, f * 128:(f + 1) * 128], g.hT[:, f, t * 128:(t + 1) * 128],
                                      g.ident[:, :])
                mm.then_inc(turned, 1)

        @block.scalar
        def _(act):
            for n, (side, k, half) in enumerate(prods):
                act.wait_ge(g_mm, n + 1)
                act.activation(gw[0][:, 2 * side + k, half * HALF:(half + 1) * HALF], bank[n % 4][:, 0:HALF],
                               ACT.Copy).then_inc(hi_ok, 1)
            for k in range(2):
                act.activation(gw[0][:, own + k, :], wst[:, 4 + k, :], ACT.Copy).then_inc(hi_ok, 1)
            for t in range(NT):
                act.wait_ge(turned, t + 1)
                act.activation(nm[0][:, t, :], bank[t % 4][:, 0:D], ACT.Copy, scale=STATE_SCALE).then_inc(nhi, 1)

        @block.vector
        def _(dve):
            c = Chain(dve, v)
            for n, (side, k, half) in enumerate(prods):
                dve.wait_ge(hi_ok, n + 1)
                cols = slice(half * HALF, (half + 1) * HALF)
                dve.tensor_tensor(gw[1][:, 2 * side + k, cols], bank[n % 4][:, 0:HALF],
                                  gw[0][:, 2 * side + k, cols].bitcast(F32), ALU.subtract).then_inc(lo_ok, 1)
            for k in range(2):
                dve.wait_ge(hi_ok, len(prods) + k + 1)
                dve.tensor_tensor(gw[1][:, own + k, :], wst[:, 4 + k, :], gw[0][:, own + k, :].bitcast(F32),
                                  ALU.subtract).then_inc(lo_ok, 2)
            c.done(dve.reduce_sum(first3[:, :], g.ident[0:6, 0:3], AX.X))
            c.step(dve.reduce_sum(last3[:, :], g.ident[0:6, 3:6], AX.X))
            for half in range(2):
                cols = slice(half * HALF, (half + 1) * HALF)
                ps = bank[4 + half][0:6, 0:HALF]
                dve.wait_ge(b_mm, half + 1)
                c.step(dve.tensor_copy(bhi[:, cols], ps))
                c.step(dve.tensor_tensor(blo[:, cols], ps, bhi[:, cols].bitcast(F32), ALU.subtract))
                c.step(dve.tensor_scalar(blo[:, cols], blo[:, cols], last3[:, 0:1], None, ALU.mult))
                dve.scalar_tensor_tensor(out=bw[:, cols], in0=bhi[:, cols].bitcast(F32), scalar=first3[:, 0:1],
                                         in1=blo[:, cols], op0=ALU.mult, op1=ALU.add).then_inc(b_ok, 1)
            for q, (a, w) in enumerate(CHV):
                dve.wait_ge(d_mm, q + 1)
                dve.tensor_copy(deg[:, a:a + w], bank[6 + q % 2][0:6, 0:w]).then_inc(d_ok, 1)
            for t in range(NT):
                dve.wait_ge(nhi, t + 1)
                dve.scalar_tensor_tensor(out=nm[1][:, t, :], in0=bank[t % 4][:, 0:D], scalar=STATE_SCALE,
                                         in1=nm[0][:, t, :], op0=ALU.mult, op1=ALU.subtract).then_inc(nlo, 1)


def gated_steps(nc, g, tag, sides, gw, bw, deg, nm):
    M = 2 * sides
    STEPS = 5
    CW = 512
    FT = [t for c in range(3) for t in [(4 * c, min(4, NT - 4 * c))]]
    with ExitStack() as ctx:
        s = Scope(nc, ctx, "step" + tag)
        uv = [[s.sb(f"uv{b}{p}", [128, M, CW], F32R) for p in range(2)] for b in range(2)]
        st = [s.sb(f"st{p}", [128, 2, CW], F32R) for p in range(2)]
        rs = [s.sb(f"rs{p}", [128, 2, CW], F32R) for p in range(2)]
        rsf, r, z, ht = (s.sb(k, [128, 2, CW], F32) for k in ("rsf", "r", "z", "ht"))
        sums = [s.ps(f"sums{i}", [128, 512], F32) for i in range(2)]
        gate = [s.ps(f"gate{i}", [128, 512], F32) for i in range(6)]
        sums_mm, sums_hi, sums_lo = s.sem("sums_mm"), s.sem("sums_hi"), s.sem("sums_lo")
        sp_passed = s.sem("sp_passed")
        st_hi, st_lo, rz_mm, h_mm, gate_out = (s.sem(k) for k in ("st_hi", "st_lo", "rz_mm", "h_mm", "gate_out"))
        rs_ok, rs_hi, rs_lo, upd, new_ok, turned = (s.sem(k) for k in ("rs_ok", "rs_hi", "rs_lo", "upd", "new_ok", "turned"))
        block = s.block()

        uses = [("sum", c, m) for c in range(3) for m in range(M)]
        uses += [("turn", c, q) for c in range(3) for q in range(2)]
        U = len(uses)
        number = {u: n for n, u in enumerate(uses)}

        @block.gpsimd
        def _(pool):
            pool.sem_inc(sums_lo, 2)
            pool.sem_inc(gate_out, 6)
            pool.sem_inc(h_mm, 2)

        @block.tensor
        def _(pe):
            def add_up(step, c):
                a, w = CHV[c]
                for m in range(M):
                    n = number[("sum", c, m)]
                    adj = g.AT if m < 2 else g.A
                    f = m % 2
                    pe.wait_ge(sums_lo, U * step + n + 1)
                    for t in range(NT):
                        if n == 0 and t == NT - 1:
                            pe.wait_ge(sums_lo, U * step + 2)
                        for p in range(2):
                            mm = pe.matmul(sums[n % 2][:, 0:w], nm[p][:, t, f * 128:(f + 1) * 128],
                                           adj[:, t, a:a + w], start=t + p == 0, stop=t == NT - 1 and p == 1)
                    mm.then_inc(sums_mm, 1)

            def products(out, m, ks, parts, w, start, stop):
                n = 0
                for k, (hi, lo) in zip(ks, parts):
                    col = slice(m * 128, (m + 1) * 128)
                    for wp, x in ((gw[0], hi), (gw[0], lo), (gw[1], hi)):
                        n += 1
                        mm = pe.matmul(out[:, 0:w], wp[:, k, col], x, start=start and n == 1,
                                       stop=stop and n == 3 * len(ks))
                return mm

            def gates(step, c):
                a, w = CHV[c]
                G = 3 * step + c
                b = c % 2
                pair = [(uv[b][0][:, k, 0:w], uv[b][1][:, k, 0:w]) for k in range(M)]
                spair = [(st[0][:, k, 0:w], st[1][:, k, 0:w]) for k in range(2)]
                rpair = [(rs[0][:, k, 0:w], rs[1][:, k, 0:w]) for k in range(2)]
                pe.wait_ge(sums_lo, U * step + number[("sum", c, M - 1)] + 3)
                pe.wait_ge(st_lo, G + 1)
                for m in range(6):
                    pe.wait_ge(gate_out, 6 * G + m + 1)
                    pe.matmul(gate[m][:, 0:w], bw[:, m * 128:(m + 1) * 128], deg[:, a:a + w], start=True, stop=False)
                    mm = products(gate[m], m, range(M), pair, w, False, False)
                    if m < 4:
                        mm = products(gate[m], m, (M, M + 1), spair, w, False, True)
                        mm.then_inc(rz_mm, 1)
                pe.wait_ge(rs_lo, G + 1)
                for m in (4, 5):
                    products(gate[m], m, (M, M + 1), rpair, w, False, True).then_inc(h_mm, 1)

            def turn(step, c):
                t0, k = FT[c]
                pe.wait_ge(new_ok, 3 * step + c + 1)
                for q in range(2):
                    n = number[("turn", c, q)]
                    pe.wait_ge(sums_lo, U * step + n + 1)
                    for e in range(min(2, k - 2 * q)):
                        for f in range(2):
                            t = t0 + 2 * q + e
                            mm = pe.transpose(sums[n % 2][:, (2 * e + f) * 128:(2 * e + f + 1) * 128],
                                              g.hT[:, f, t * 128:(t + 1) * 128], g.ident[:, :])
                    mm.then_inc(sums_mm, 1)

            with pe.Fori(0, STEPS) as step:
                add_up(step, 0)
                add_up(step, 1)
                gates(step, 0)
                add_up(step, 2)
                gates(step, 1)
                turn(step, 0)
                gates(step, 2)
                turn(step, 1)
                turn(step, 2)

        @block.sync
        def _(sp):
            sp.sem_inc(sp_passed, 1)

        @block.scalar
        def _(act):
            def sums_high(step, c):
                w = CHV[c][1]
                for m in range(M):
                    n = number[("sum", c, m)]
                    act.wait_ge(sums_mm, U * step + n + 1)
                    if m == 0:
                        last = {0: 3 * step * 2, 1: (3 * step) * 2, 2: (3 * step + 1) * 2}[c]
                        act.wait_ge(h_mm, last + 2)
                    act.activation(uv[c % 2][0][:, m, 0:w], sums[n % 2][:, 0:w], ACT.Copy,
                                   scale=1.0 / STATE_SCALE).then_inc(sums_hi, 1)

            def state_high(step, c):
                a, w = CHV[c]
                G = 3 * step + c
                act.wait_ge(h_mm, 2 * G + 2)
                act.activation(st[0][:, :, 0:w], g.hT[:, :, a:a + w], ACT.Copy).then_inc(st_hi, 1)

            def gates(step, c):
                w = CHV[c][1]
                G = 3 * step + c
                for m in range(4):
                    act.wait_ge(rz_mm, 4 * G + m + 1)
                    if m == 2:
                        act.wait_ge(upd, 3 * G + 1)
                    act.activation((r, z)[m // 2][:, m % 2, 0:w], gate[m][:, 0:w], ACT.Sigmoid).then_inc(gate_out, 1)
                    if m == 1:
                        act.wait_ge(rs_ok, G + 1)
                        act.activation(rs[0][:, :, 0:w], rsf[:, :, 0:w], ACT.Copy).then_inc(rs_hi, 1)
                for m in range(2):
                    act.wait_ge(h_mm, 2 * G + m + 3)
                    act.activation(ht[:, m, 0:w], gate[4 + m][:, 0:w], ACT.Tanh).then_inc(gate_out, 1)

            def turned_high(step, c):
                t0, k = FT[c]
                for q in range(2):
                    n = number[("turn", c, q)]
                    kk = min(2, k - 2 * q)
                    act.wait_ge(sums_mm, U * step + n + 1)
                    act.activation(nm[0][:, t0 + 2 * q:t0 + 2 * q + kk, :],
                                   sums[n % 2][:, 0:kk * D].rearrange("p (t f) -> p t f", f=D), ACT.Copy,
                                   scale=STATE_SCALE).then_inc(sums_hi, 1)

            with act.Fori(0, STEPS) as step:
                state_high(step, 0)
                sums_high(step, 0)
                sums_high(step, 1)
                gates(step, 0)
                state_high(step, 1)
                sums_high(step, 2)
                gates(step, 1)
                state_high(step, 2)
                turned_high(step, 0)
                gates(step, 2)
                turned_high(step, 1)
                turned_high(step, 2)

        @block.vector
        def _(dve):
            dve.sem_inc(upd, 1)

            def sums_low(step, c):
                w = CHV[c][1]
                for m in range(M):
                    n = number[("sum", c, m)]
                    dve.wait_ge(sums_hi, U * step + n + 1)
                    dve.scalar_tensor_tensor(out=uv[c % 2][1][:, m, 0:w], in0=sums[n % 2][:, 0:w],
                                             scalar=1.0 / STATE_SCALE, in1=uv[c % 2][0][:, m, 0:w].bitcast(F32),
                                             op0=ALU.mult, op1=ALU.subtract).then_inc(sums_lo, 1)

            def state_low(step, c):
                a, w = CHV[c]
                dve.wait_ge(st_hi, 3 * step + c + 1)
                dve.tensor_tensor(st[1][:, :, 0:w], g.hT[:, :, a:a + w], st[0][:, :, 0:w].bitcast(F32),
                                  ALU.subtract).then_inc(st_lo, 1)

            def reset(step, c):
                a, w = CHV[c]
                G = 3 * step + c
                dve.wait_ge(gate_out, 6 * G + 2 + 6)
                dve.tensor_tensor(rsf[:, :, 0:w], r[:, :, 0:w], g.hT[:, :, a:a + w], ALU.mult).then_inc(rs_ok, 1)
                dve.wait_ge(rs_hi, G + 1)
                dve.tensor_tensor(rs[1][:, :, 0:w], rsf[:, :, 0:w], rs[0][:, :, 0:w].bitcast(F32),
                                  ALU.subtract).then_inc(rs_lo, 1)

            def update(step, c):
                a, w = CHV[c]
                G = 3 * step + c
                dve.wait_ge(gate_out, 6 * G + 6 + 6)
                old = g.hT[:, :, a:a + w]
                dve.tensor_tensor(ht[:, :, 0:w], ht[:, :, 0:w], old, ALU.subtract).then_inc(upd, 1)
                dve.wait_ge(upd, 3 * G + 2)
                dve.tensor_tensor(ht[:, :, 0:w], ht[:, :, 0:w], z[:, :, 0:w], ALU.mult).then_inc(upd, 1)
                dve.wait_ge(upd, 3 * G + 3)
                dve.tensor_tensor(old, old, ht[:, :, 0:w], ALU.add).then_inc(new_ok, 1)
                dve.wait_ge(new_ok, G + 1)
                dve.sem_inc(upd, 1)

            def turned_low(step, c):
                t0, k = FT[c]
                for q in range(2):
                    n = number[("turn", c, q)]
                    kk = min(2, k - 2 * q)
                    tiles = slice(t0 + 2 * q, t0 + 2 * q + kk)
                    dve.wait_ge(sums_hi, U * step + n + 1)
                    dve.scalar_tensor_tensor(out=nm[1][:, tiles, :],
                                             in0=sums[n % 2][:, 0:kk * D].rearrange("p (t f) -> p t f", f=D),
                                             scalar=STATE_SCALE, in1=nm[0][:, tiles, :],
                                             op0=ALU.mult, op1=ALU.subtract).then_inc(sums_lo, 1)

            with dve.Fori(0, STEPS) as step:
                state_low(step, 0)
                sums_low(step, 0)
                sums_low(step, 1)
                reset(step, 0)
                update(step, 0)
                state_low(step, 1)
                sums_low(step, 2)
                reset(step, 1)
                update(step, 1)
                state_low(step, 2)
                turned_low(step, 0)
                reset(step, 2)
                update(step, 2)
                turned_low(step, 1)
                turned_low(step, 2)


def batchnorm_out(nc, g, raw, H, O, gamma_dram, beta_dram, out_dram):
    V1 = O + 1
    with ExitStack() as ctx:
        s = Scope(nc, ctx, "bn")
        inv = s.sb("inv", [128, NT, H], F32)
        hp = s.sb("hp", [128, NT, D], F32)
        sq = s.sb("sq", [128, NT, D], F32)
        gb = s.sb("gb", [128, 2, D], F32)
        mean, scale, tmp = (s.sb(k, [128, D], F32) for k in ("mean", "scale", "tmp"))
        eps = s.sb("eps", [128, 1], F32)
        bank = [s.ps(f"bank{i}", [128, 512], F32) for i in range(2)]
        v, w_in, hp_ok, sum_mm, sq_ok, var_ok, std_ok, cen_ok, pre_ok, relu_ok, x_ok, stored = (
            s.sem(k) for k in ("v", "w_in", "hp_ok", "sum_mm", "sq_ok", "var_ok", "std_ok", "cen_ok", "pre_ok",
                               "relu_ok", "x_ok", "stored"))
        block = s.block()

        @block.sync
        def _(sp):
            sp.dma_start(gb[:, 0, :], gamma_dram.partition_broadcast(128)).then_inc(w_in, 16)
            sp.dma_start(gb[:, 1, :], beta_dram.partition_broadcast(128)).then_inc(w_in, 16)
            for t in range(NT):
                k = 128 if t < NT - 1 else TAIL
                sp.wait_ge(x_ok, t + 1)
                sp.dma_start(out_dram[t * 128:t * 128 + k, :], g.x[0:k, t, :]).then_inc(stored, 16)
            sp.wait_ge(stored, 16 * NT)

        @block.tensor
        def _(pe):
            for b, (src, ok) in enumerate(((hp, hp_ok), (sq, sq_ok))):
                for t in range(NT):
                    k = 128 if t < NT - 1 else TAIL
                    pe.wait_ge(ok, t + 1)
                    mm = pe.matmul(bank[b][:, 0:D], g.ones[0:k, :], src[0:k, t, :], start=t == 0, stop=t == NT - 1)
                mm.then_inc(sum_mm, 1)

        @block.scalar
        def _(act):
            for t in range(NT):
                act.wait_ge(cen_ok, t + 1)
                act.activation(sq[:, t, :], hp[:, t, :], ACT.Square).then_inc(sq_ok, 1)
            act.wait_ge(var_ok, 1)
            act.activation(tmp[:, :], tmp[:, :], ACT.Sqrt, bias=eps[:, 0:1]).then_inc(std_ok, 1)

        @block.vector
        def _(dve):
            c = Chain(dve, v)
            r4 = raw[:, :, :].rearrange("p t (h o) -> p t h o", o=V1)
            c.done(dve.memset(eps[:, :], 1e-5))
            c.step(dve.reciprocal(inv[:, :, :], r4[:, :, :, O]))
            for t in range(NT):
                dve.tensor_tensor(hp[:, t, :].rearrange("p (h o) -> p h o", o=O), r4[:, t, :, 0:O],
                                  inv[:, t, :].unsqueeze(2).broadcast_to([128, H, O]), ALU.mult).then_inc(hp_ok, 1)
            dve.wait_ge(sum_mm, 1)
            c.step(dve.tensor_scalar(mean[:, :], bank[0][:, 0:D], 1.0 / N, None, ALU.mult))
            for t in range(NT):
                dve.tensor_tensor(hp[:, t, :], hp[:, t, :], mean[:, :], ALU.subtract).then_inc(cen_ok, 1)
            dve.wait_ge(sum_mm, 2)
            dve.tensor_scalar(tmp[:, :], bank[1][:, 0:D], 1.0 / N, None, ALU.mult).then_inc(var_ok, 1)
            dve.wait_ge(std_ok, 1)
            dve.wait_ge(w_in, 32)
            c.step(dve.reciprocal(scale[:, :], tmp[:, :]))
            c.step(dve.tensor_tensor(scale[:, :], scale[:, :], gb[:, 0, :], ALU.mult))
            dve.wait_ge(cen_ok, NT)
            for t in range(NT):
                c.step(dve.tensor_tensor(hp[:, t, :], hp[:, t, :], scale[:, :], ALU.mult))
                c.step(dve.tensor_tensor(hp[:, t, :], hp[:, t, :], gb[:, 1, :], ALU.add))
                dve.scalar_tensor_tensor(out=g.x[:, t, :], in0=hp[:, t, :], scalar=0.0, in1=g.x[:, t, :],
                                         op0=ALU.max, op1=ALU.add).then_inc(x_ok, 1)


class Graph:
    pass


def program(nc, d, out):
    with ExitStack() as ctx:
        s = Scope(nc, ctx, "g")
        g = Graph()
        g.A = s.sb("A", [128, NT, NP], F16)
        g.AT = s.sb("AT", [128, NT, NP], F16)
        g.x = s.sb("x", [128, NT, D], F32)
        g.hT = s.sb("hT", [128, 2, NP], F32)
        g.ident = s.sb("ident", [128, 128], F32)
        g.ident16 = s.sb("ident16", [128, 128], F16)
        g.ones = s.sb("ones", [128, 128], F32)
        g.fewest = s.sb("fewest", [128, 1], F32)
        g.near = s.sb("near", [1, 1], I32)
        g.symmetric = s.sb("symmetric", [1, 1], I32)

        load_graph(nc, g, d["x"], d["adj"])
        layernorm_relu(nc, g, "ln0")
        cosine_attention(nc, g, d["L0_WT"])
        layernorm_relu(nc, g, "ln1")
        with ExitStack() as c2:
            val8 = Scope(nc, c2, "l1v").sb("val8", [128, NT, 8 * 65], F32)
            gat(nc, g, "gat8", g.hT, 2, d["L1_W1"], d["L1_ai"], d["L1_aj"], 8, 64, val8)
            x1T = Scope(nc, c2, "l1x").sb("x1T", [128, 4, NP], F32)
            normalise_elu(nc, g, "elu8", val8, 8, 64, x1T)
            g.sums1 = val8[:, :, 0:257]
            gat(nc, g, "gat1", x1T, 4, d["L1_Wo"], d["L1_aoi"], d["L1_aoj"], 1, 256, val8[:, :, 257:514])
            normalise_elu(nc, g, "elu1", g.sums1, 1, 256, g.hT)
        mlp(nc, g, "mlp1", g.hT, d["L1_lin1"], d["L1_b1"], ACT.Relu, d["L1_lin2"], d["L1_b2"], check_symmetry=True)
        layernorm_relu(nc, g, "ln2")
        gated_graph(nc, g, d)
        mlp(nc, g, "mlp2", g.hT, d["o1_WT"], d["o1_b"], ACT.Tanh, d["o2_WT"], d["o2_b"])
        layernorm_relu(nc, g, "ln3")
        with ExitStack() as c3:
            val3 = Scope(nc, c3, "l3").sb("val3", [128, NT, 8 * 33], F32)
            gat(nc, g, "gat3", g.hT, 2, d["L3_WT"], d["L3_ai"], d["L3_aj"], 8, 32, val3)
            batchnorm_out(nc, g, val3, 8, 32, d["L3_gamma"], d["L3_beta"], out)


def kernel(**inputs):
    import numpy as _np
    import concourse.bacc as _bacc
    from concourse import mybir as _mybir
    from concourse.bass_utils import run_bass_kernel_spmd as _run

    i = {k: _np.asarray(v) for k, v in inputs.items()}
    laid = {
        "x": i["x"], "adj": i["adj"], "L0_WT": i["L0_gnn_W"].T,
        "L1_W1": i["L1_gnn_W1"].transpose(1, 0, 2).reshape(256, 512),
        "L1_ai": i["L1_gnn_a1"][:, :64].reshape(512), "L1_aj": i["L1_gnn_a1"][:, 64:].reshape(512),
        "L1_Wo": i["L1_gnn_Wo"], "L1_aoi": i["L1_gnn_ao"][:256], "L1_aoj": i["L1_gnn_ao"][256:],
        "L1_lin1": i["L1_gnn_lin1_w"], "L1_b1": i["L1_gnn_lin1_b"].reshape(4, 128).T,
        "L1_lin2": i["L1_gnn_lin2_w"], "L1_b2": i["L1_gnn_lin2_b"],
        "in_W": i["L2_gnn_in_W"], "out_W": i["L2_gnn_out_W"], 
        "in_b": i["L2_gnn_in_b"].reshape(2, 128).T, "out_b": i["L2_gnn_out_b"].reshape(2, 128).T,
        "r_WT": i["L2_gnn_r_W"].T, "z_WT": i["L2_gnn_z_W"].T, "h_WT": i["L2_gnn_h_W"].T,
        "r_b": i["L2_gnn_r_b"], "z_b": i["L2_gnn_z_b"], "h_b": i["L2_gnn_h_b"],
        "o1_WT": i["L2_gnn_o1_W"].T, "o1_b": i["L2_gnn_o1_b"].reshape(2, 128).T,
        "o2_WT": i["L2_gnn_o2_W"].T, "o2_b": i["L2_gnn_o2_b"],
        "L3_WT": i["L3_gnn_W"].T, "L3_ai": i["L3_gnn_a"][32:], "L3_aj": i["L3_gnn_a"][:32],
        "L3_gamma": i["L3_gnn_gamma"], "L3_beta": i["L3_gnn_beta"],
    }
    nc = _bacc.Bacc("TRN2", target_bir_lowering=False, num_devices=1)
    arrays, d = {}, {}
    for name, a in laid.items():
        a = _np.ascontiguousarray(a)
        arrays[f"in_{name}_dram"] = a
        d[name] = nc.dram_tensor(f"in_{name}_dram", a.shape, _mybir.dt.from_np(a.dtype), kind="ExternalInput").ap()
    out = nc.dram_tensor("out_dram", (1354, 256), _mybir.dt.float32, kind="ExternalOutput").ap()
    program(nc, d, out)
    r = _run(nc, [arrays], core_ids=[0])
    return r.results[0]["out_dram"]
```

```python
import concourse.bass as bass
from concourse import mybir
from contextlib import ExitStack

F32 = mybir.dt.float32
F32R = mybir.dt.float32r
F16 = mybir.dt.float16
I32 = mybir.dt.int32
ALU = mybir.AluOpType
ACT = mybir.ActivationFunctionType
AX = mybir.AxisListType
RMAX = bass.bass_isa.ReduceOp.max

N, D = 1354, 256
NT = (N + 127) // 128
NP = NT * 128
TAIL = N - (NT - 1) * 128
CH = [(0, 512), (512, 512), (1024, NP - 1024)]
HALVES = [(0, (NT + 1) // 2 * 128), ((NT + 1) // 2 * 128, NT // 2 * 128)]
CHV = [(0, 512), (512, 512), (1024, N - 1024)]


class Scope:

    def __init__(self, nc, ctx, tag):
        self.nc, self.ctx, self.tag, self.sems = nc, ctx, tag, []

    def sb(self, name, shape, dt):
        return self.ctx.enter_context(self.nc.sbuf_tensor(f"{self.tag}_{name}", shape, dt))

    def ps(self, name, shape, dt):
        return self.ctx.enter_context(self.nc.psum_tensor(f"{self.tag}_{name}", shape, dt))

    def sem(self, name):
        self.sems.append(self.nc.alloc_semaphore(f"{self.tag}_{name}"))
        return self.sems[-1]

    def block(self):
        self.ctx.callback(self.clear)
        return self.ctx.enter_context(self.nc.Block())

    def clear(self):
        self.nc.clear_and_free_semaphores(self.sems)
        self.nc.all_engine_barrier()


class Chain:

    def __init__(self, eng, sem):
        self.eng, self.sem, self.n = eng, sem, 0

    def done(self, ins):
        self.n += 1
        ins.then_inc(self.sem, 1)

    def wait(self):
        self.eng.wait_ge(self.sem, self.n)

    def step(self, ins):
        self.done(ins)
        self.wait()


class Graph:
    pass


def load_graph(nc, g, x_dram, adj_dram, loads):
    with ExitStack() as ctx:
        s = Scope(nc, ctx, "load")
        NS = 6
        stage = s.sb("stage", [128, NS, N], I32)
        tp8 = [s.ps(f"tp8_{i}", [128, 8, 128], F16) for i in range(2)]
        tp3 = [s.ps(f"tp3_{i}", [128, NT - 8, 128], F16) for i in range(2)]
        arrived = [s.sem(f"arrived{i}") for i in range(NS)]
        x_in, cleared, ident_ok, even_ok, odd_ok, pad_ok = (
            s.sem(k) for k in ("x_in", "cleared", "ident_ok", "even_ok", "odd_ok", "pad_ok"))
        few = s.sb("few", [128, 3], F32)
        deg = [s.ps(f"deg{i}", [128, 512], F32) for i in range(3)]
        one16 = s.sb("one16", [128, 128], F16)
        turned, out8, out3, deg_mm, v = (s.sem(k) for k in ("turned", "out8", "out3", "deg_mm", "v"))
        ln = layernorm_buffers(s, deg)
        w_in = s.sem("w_in")
        block = s.block()

        def rows(t):
            return 128 if t < NT - 1 else TAIL

        @block.sync
        def _(sp):
            sp.dma_start(g.x[:, 0:NT - 1, :],
                         x_dram[0:(NT - 1) * 128, :].rearrange("(t p) f -> p t f", p=128)).then_inc(x_in, 16)
            sp.wait_ge(cleared, 1)
            sp.dma_start(g.x[0:TAIL, NT - 1, :], x_dram[(NT - 1) * 128:N, :]).then_inc(x_in, 16)
            for t in range(NT):
                if t >= NS:
                    u = t - NS
                    sp.wait_ge(even_ok if u % 2 == 0 else odd_ok, u // 2 + 1)
                sp.dma_start(stage[0:rows(t), t % NS, :],
                             adj_dram[t * 128:t * 128 + rows(t), :]).then_inc(arrived[t % NS], 16)

        @block.gpsimd
        def _(pool):
            fills = [(g.x[64:128, NT - 1, :], 0.0), (g.A[:, :, N:NP], 0.0), (g.A[64:128, NT - 1, 0:N], 0.0),
                     (g.ident[:, :], 0.0), (g.ident16[:, :], 0.0), (g.ones[:, :], 1.0), (one16[:, :], 1.0)]
            for n, (region, value) in enumerate(fills):
                pool.memset(region, value).then_inc(cleared, 1)
                pool.wait_ge(cleared, n + 1)
            for m in (g.ident, g.ident16):
                pool.affine_select(out=m[:, :], in_=m[:, :], compare_op=ALU.not_equal, fill=1.0, base=0,
                                   pattern=[[-1, 128]], channel_multiplier=1).then_inc(ident_ok, 1)
            pool.wait_ge(ident_ok, 2)
            pool.tensor_copy(g.A[:, NT - 1, N:NP], g.ident16[:, TAIL:128]).then_inc(pad_ok, 1)

        @block.scalar
        def _(act):
            for buffer, source in loads:
                act.dma_start(buffer, source).then_inc(w_in, 16)

        layernorm_programs(g, ln, block, (x_in, 32), (ident_ok, 2))

        def convert(eng, copy, t, ok):
            if t == NT - 1:
                eng.wait_ge(cleared, 7)
            eng.wait_ge(arrived[t % NS], 16 * (t // NS + 1))
            copy(g.A[0:rows(t), t, 0:N], stage[0:rows(t), t % NS, :]).then_inc(ok, 1)

        @block.scalar
        def _(act):
            for r in range(NT):
                if r % 2 == 1:
                    convert(act, lambda o, i: act.activation(o, i, ACT.Copy), r, odd_ok)
                if r >= 1:
                    act.wait_ge(turned, r)
                    act.activation(g.AT[:, 8:NT, (r - 1) * 128:r * 128], tp3[(r - 1) % 2][:, :, :],
                                   ACT.Copy).then_inc(out3, 1)
            act.wait_ge(turned, NT)
            act.activation(g.AT[:, 8:NT, (NT - 1) * 128:NP], tp3[(NT - 1) % 2][:, :, :],
                           ACT.Copy).then_inc(out3, 1)
            act.wait_ge(w_in, 16 * len(loads))

        @block.vector
        def _(dve):
            for r in range(NT):
                if r % 2 == 0:
                    convert(dve, dve.tensor_copy, r, even_ok)
                if r >= 1:
                    dve.wait_ge(turned, r)
                    dve.tensor_copy(g.AT[:, 0:8, (r - 1) * 128:r * 128], tp8[(r - 1) % 2][:, :, :]).then_inc(out8, 1)
            dve.wait_ge(turned, NT)
            dve.tensor_copy(g.AT[:, 0:8, (NT - 1) * 128:NP], tp8[(NT - 1) % 2][:, :, :]).then_inc(out8, 1)
            c_ = Chain(dve, v)
            for c, (_, w) in enumerate(CHV):
                dve.wait_ge(deg_mm, min(4 * (c + 1), NT))
                c_.done(dve.tensor_reduce(few[:, c:c + 1], deg[c][:, 0:w], axis=AX.X, op=ALU.min))
            c_.wait()
            c_.step(dve.tensor_reduce(g.fewest[:, :], few[:, :], axis=AX.X, op=ALU.min))

        @block.tensor
        def _(pe):
            pe.wait_ge(ident_ok, 2)
            pe.wait_ge(cleared, 7)
            pe.wait_ge(pad_ok, 1)
            pe.wait_ge(ln.out, len(ln.pairs))

            def count(r):
                pe.wait_ge(out8, r + 1)
                pe.wait_ge(out3, r + 1)
                for t in range(NT):
                    mm = pe.matmul(deg[r // 4][:, (r % 4) * 128:(r % 4 + 1) * 128], one16[:, :],
                                   g.AT[:, t, r * 128:(r + 1) * 128], start=t == 0, stop=t == NT - 1)
                mm.then_inc(deg_mm, 1)

            for r in range(NT):
                pe.wait_ge(even_ok if r % 2 == 0 else odd_ok, r // 2 + 1)
                if r >= 2:
                    pe.wait_ge(out8, r - 1)
                    pe.wait_ge(out3, r - 1)
                for c in range(NT):
                    out = tp8[r % 2][:, c, :] if c < 8 else tp3[r % 2][:, c - 8, :]
                    mm = pe.transpose(out, g.A[:, r, c * 128:(c + 1) * 128], g.ident16[:, :])
                mm.then_inc(turned, 1)
                if r >= 2:
                    count(r - 2)
            count(NT - 2)
            count(NT - 1)


def by_partition(dram):
    return dram.rearrange("(k p) o -> p k o", p=128)


def fetch(block, s, loads):
    @block.sync
    def _(sp):
        if loads:
            fetched = s.sem("fetched")
            for buffer, source in loads:
                sp.dma_start(buffer, source).then_inc(fetched, 16)
            sp.wait_ge(fetched, 16 * len(loads))


def layernorm_relu(nc, g, tag, loads=()):
    with ExitStack() as ctx:
        s = Scope(nc, ctx, tag)
        b = layernorm_buffers(s, [s.ps(f"tp{i}", [128, 512], F32) for i in range(3)])
        block = s.block()
        fetch(block, s, loads)
        layernorm_programs(g, b, block)


def measure(dve, g, t, x_ok, value, measured):
    dve.wait_ge(x_ok, value)
    dve.bn_stats(g.stats[:, t, :], g.x[:, t, :]).then_inc(measured, 1)
    if t == NT - 1:
        dve.wait_ge(measured, NT)
        for u in range(NT):
            dve.bn_aggr(g.mv[:, u, :], g.stats[:, u, :]).then_inc(measured, 1)


def layernorm_buffers(s, banks):
    b = Graph()
    b.eps = s.sb("eps", [128, 1], F32)
    b.std, b.rstd, b.shift = (s.sb(k, [128, NT], F32) for k in ("std", "rstd", "shift"))
    b.h = s.sb("h", [128, NT, D], F32)
    b.tp = [bank[:, :].rearrange("p (f i) -> p f i", f=2) for bank in banks]
    b.measured, b.v, b.std_ok, b.scale_ok, b.h_ok, b.turned, b.out = (
        s.sem(k) for k in ("ln_measured", "ln_v", "std_ok", "scale_ok", "h_ok", "ln_turned", "ln_out"))
    b.pairs = [(a, min(2, NT - a)) for a in range(0, NT, 2)]
    return b


def layernorm_programs(g, b, block, x_in=None, ident_ok=None):
    @block.vector
    def _(dve):
        c = Chain(dve, b.v)
        c.done(dve.memset(b.eps[:, :], 1e-5))
        if x_in:
            for t in range(NT):
                measure(dve, g, t, *x_in, b.measured)
            dve.wait_ge(b.measured, 2 * NT)
        dve.wait_ge(b.std_ok, 1)
        c.step(dve.reciprocal(b.rstd[:, :], b.std[:, :]))
        dve.scalar_tensor_tensor(out=b.shift[:, :], in0=g.mv[:, :, 0], scalar=-1.0, in1=b.rstd[:, :],
                                 op0=ALU.mult, op1=ALU.mult).then_inc(b.scale_ok, 1)
        for n, (a, k) in enumerate(b.pairs):
            dve.wait_ge(b.turned, n + 1)
            dve.tensor_copy(g.hT[:, :, a * 128:(a + k) * 128], b.tp[n % 3][:, :, 0:k * 128]).then_inc(b.out, 1)

    @block.scalar
    def _(act):
        act.wait_ge(b.v, 1)
        if x_in:
            act.wait_ge(b.measured, 2 * NT)
        act.activation(b.std[:, :], g.mv[:, :, 1], ACT.Sqrt, bias=b.eps[:, 0:1]).then_inc(b.std_ok, 1)
        act.wait_ge(b.scale_ok, 1)
        for t in range(NT):
            act.activation(b.h[:, t, :], g.x[:, t, :], ACT.Relu, bias=b.shift[:, t:t + 1],
                           scale=b.rstd[:, t:t + 1]).then_inc(b.h_ok, 1)

    @block.tensor
    def _(pe):
        if ident_ok:
            pe.wait_ge(*ident_ok)
        for n, (a, k) in enumerate(b.pairs):
            if n >= 3:
                pe.wait_ge(b.out, n - 2)
            pe.wait_ge(b.h_ok, a + k)
            for q in range(k):
                for f in range(2):
                    mm = pe.transpose(b.tp[n % 3][:, f, q * 128:(q + 1) * 128],
                                      b.h[:, a + q, f * 128:(f + 1) * 128], g.ident[:, :])
            mm.then_inc(b.turned, 1)


def cosine_attention(nc, g, wT):
    with ExitStack() as outer:
        so = Scope(nc, outer, "cos")
        wh = so.sb("wh", [128, NT, D + 1], F32)
        nsq = so.sb("nsq", [128, NT], F32)
        with ExitStack() as ctx:
            s = Scope(nc, ctx, "cosp")
            squares = s.sb("squares", [128, 2, D], F32)
            least = s.sb("least", [128, 1], F32)
            least1 = s.sb("least1", [1, 1], F32)
            bank = [s.ps(f"bank{i}", [128, 512], F32) for i in range(4)]
            wh_mm, wh_out, nsq_ok, least_ok, least_mm, v = (
                s.sem(k) for k in ("wh_mm", "wh_out", "nsq_ok", "least_ok", "least_mm", "v"))
            block = s.block()

            @block.gpsimd
            def _(pool):
                pool.memset(wh[:, :, D:D + 1], 1.0).then_inc(v, 1)

            @block.tensor
            def _(pe):
                for t in range(NT):
                    if t >= 3:
                        pe.wait_ge(wh_out, t - 2)
                    for k in range(2):
                        mm = pe.matmul(bank[t % 3][:, 0:D], g.hT[:, k, t * 128:(t + 1) * 128], wT[:, k, :],
                                       start=k == 0, stop=k == 1)
                    mm.then_inc(wh_mm, 1)
                pe.wait_ge(least_ok, 1)
                pe.transpose(bank[3][0:1, 0:128], least[:, :], g.ident[:, :])
                pe.transpose(bank[3][0:1, 128:256], nsq[:, NT - 1:NT], g.ident[:, :]).then_inc(least_mm, 1)

            @block.scalar
            def _(act):
                for t in range(NT):
                    act.wait_ge(wh_out, t + 1)
                    if t >= 2:
                        act.wait_ge(nsq_ok, t - 1)
                    act.activation(squares[:, t % 2, :], wh[:, t, 0:D], ACT.Square,
                                   accum_out=nsq[:, t:t + 1]).then_inc(nsq_ok, 1)

            @block.vector
            def _(dve):
                for t in range(NT):
                    dve.wait_ge(wh_mm, t + 1)
                    dve.tensor_copy(wh[:, t, 0:D], bank[t % 3][:, 0:D]).then_inc(wh_out, 1)
                dve.wait_ge(nsq_ok, NT)
                dve.tensor_reduce(least[:, :], nsq[:, 0:NT - 1], axis=AX.X, op=ALU.min).then_inc(least_ok, 1)
                dve.wait_ge(least_mm, 1)
                dve.tensor_reduce(least1[:, :], bank[3][0:1, 0:128 + TAIL], axis=AX.X, op=ALU.min).then_inc(least_ok, 1)
                dve.wait_ge(least_ok, 2)
                dve.tensor_scalar(g.near[:, :], least1[:, :], 1.0, None, ALU.is_ge).then_inc(least_ok, 1)

        long = nc.values_load(g.near[0:1, 0:1], min_val=0, max_val=1)
        with nc.If(long == 1):
            cosine_long(nc, g, wh, nsq)
        with nc.Else():
            cosine_short(nc, g, wT, wh)


def cosine_long(nc, g, wh, nsq):
    with ExitStack() as ctx:
        s = Scope(nc, ctx, "cosl")
        norm, inv = (s.sb(k, [128, NT], F32) for k in ("norm", "inv"))
        unit = s.sb("unit", [128, 3, D], F32)
        uT = [s.sb(f"uT{p}", [128, 2, NP], F32R) for p in range(2)]
        diag = s.sb("diag", [128, NT, 128], F16)
        pt = [s.sb(f"pt{c}", [128, NT, CH[c][1]], F32) for c in range(3)]
        rsum = s.sb("rsum", [128, NT], F32)
        cosb = [s.ps(f"cosb{i}", [128, 512], F32) for i in range(4)]
        ag = [s.ps(f"ag{i}", [128, 512], F32) for i in range(4)]
        measured = s.sem("measured")
        norm_ok, inv_ok, unit_ok, turned, hi_ok, lo_ok, cos_mm, exp_ok, mask_ok, pt_ok, agg_mm, rsum_ok, agg_out, diag_ok = (
            s.sem(k) for k in ("norm_ok", "inv_ok", "unit_ok", "turned", "hi_ok", "lo_ok", "cos_mm", "exp_ok",
                               "mask_ok", "pt_ok", "agg_mm", "rsum_ok", "agg_out", "diag_ok"))
        block = s.block()

        @block.sync
        def _(sp):
            sp.sem_inc(norm_ok, 1)

        @block.gpsimd
        def _(pool):
            pool.sem_inc(norm_ok, 1)

        @block.tensor
        def _(pe):
            for t in range(NT):
                pe.wait_ge(unit_ok, t + 1)
                if t >= 4:
                    pe.wait_ge(lo_ok, t - 3)
                for f in range(2):
                    mm = pe.transpose(cosb[t % 4][:, f * 128:(f + 1) * 128], unit[:, t % 3, f * 128:(f + 1) * 128],
                                      g.ident[:, :])
                mm.then_inc(turned, 1)
            pe.wait_ge(lo_ok, NT)

            def cosines(c):
                a, w = CH[c]
                for t in range(NT):
                    n = NT * c + t
                    if n >= 4:
                        pe.wait_ge(exp_ok, n - 3)
                    for q, (p, r) in enumerate(((0, 0), (0, 1), (1, 0))):
                        for k in range(2):
                            mm = pe.matmul(cosb[n % 4][:, 0:w], uT[p][:, k, t * 128:(t + 1) * 128],
                                           uT[r][:, k, a:a + w], start=q == 0 and k == 0, stop=q == 2 and k == 1)
                    mm.then_inc(cos_mm, 1)

            def add_up(c):
                for r in range(CH[c][0] // 128, (CH[c][0] + CH[c][1]) // 128):
                    if r >= 4:
                        pe.wait_ge(agg_out, r - 3)
                    off = r * 128 - CH[c][0]
                    for t in range(NT):
                        pe.wait_ge(pt_ok, NT * c + t + 1)
                        mm = pe.matmul(ag[r % 4][:, 0:D + 1], pt[c][:, t, off:off + 128], wh[:, t, :],
                                       start=t == 0, stop=t == NT - 1)
                    mm.then_inc(agg_mm, 1)

            cosines(0)
            cosines(1)
            add_up(0)
            cosines(2)
            add_up(1)
            add_up(2)

        @block.scalar
        def _(act):
            act.activation(norm[:, :], nsq[:, :], ACT.Sqrt).then_inc(norm_ok, 1)
            for t in range(NT):
                act.wait_ge(turned, t + 1)
                act.activation(uT[0][:, :, t * 128:(t + 1) * 128],
                               cosb[t % 4][:, 0:D].rearrange("p (f i) -> p f i", i=128), ACT.Copy).then_inc(hi_ok, 1)
            for c in range(3):
                w = CH[c][1]
                for t in range(NT):
                    n = NT * c + t
                    act.wait_ge(cos_mm, n + 1)
                    act.activation(pt[c][:, t, :], cosb[n % 4][:, 0:w], ACT.Exp).then_inc(exp_ok, 1)

        @block.vector
        def _(dve):
            for t in range(NT):
                dve.tensor_tensor(diag[:, t, :], g.AT[:, t, t * 128:(t + 1) * 128], g.ident16[:, :],
                                  ALU.max).then_inc(diag_ok, 1)
            dve.wait_ge(norm_ok, 3)
            dve.tensor_scalar(inv[:, :], norm[:, :], 1e-20, None, ALU.max).then_inc(inv_ok, 1)
            dve.wait_ge(inv_ok, 1)
            dve.reciprocal(inv[:, :], inv[:, :]).then_inc(inv_ok, 1)
            dve.wait_ge(inv_ok, 2)

            def low(t):
                dve.wait_ge(hi_ok, t + 1)
                dve.tensor_tensor(uT[1][:, :, t * 128:(t + 1) * 128],
                                  cosb[t % 4][:, 0:D].rearrange("p (f i) -> p f i", i=128),
                                  uT[0][:, :, t * 128:(t + 1) * 128].bitcast(F32), ALU.subtract).then_inc(lo_ok, 1)

            for t in range(NT):
                if t >= 3:
                    dve.wait_ge(turned, t - 2)
                dve.tensor_scalar(unit[:, t % 3, :], wh[:, t, 0:D], inv[:, t:t + 1], None, ALU.mult).then_inc(unit_ok, 1)
                if t >= 2:
                    low(t - 2)
            low(NT - 2)
            low(NT - 1)
            dve.wait_ge(diag_ok, NT)

            def finish(r):
                dve.wait_ge(agg_mm, r + 1)
                dve.reciprocal(rsum[:, r:r + 1], ag[r % 4][:, D:D + 1]).then_inc(rsum_ok, 1)
                dve.wait_ge(rsum_ok, r + 1)
                dve.scalar_tensor_tensor(out=g.x[:, r, :], in0=ag[r % 4][:, 0:D], scalar=rsum[:, r:r + 1],
                                         in1=g.x[:, r, :], op0=ALU.mult, op1=ALU.add).then_inc(agg_out, 1)
                if r >= 1:
                    measure(dve, g, r - 1, agg_out, r, measured)
                if r == NT - 1:
                    measure(dve, g, r, agg_out, NT, measured)

            for c, (a, w) in enumerate(CH):
                for t in range(NT):
                    dve.wait_ge(exp_ok, NT * c + t + 1)
                    block_ = pt[c][:, t, :]
                    d = t * 128 - a
                    if 0 <= d < w:
                        pieces = [(0, d, None), (d, d + 128, diag[:, t, :]), (d + 128, w, None)]
                    else:
                        pieces = [(0, w, None)]
                    pieces = [p for p in pieces if p[0] < p[1]]
                    for n, (lo, hi, m) in enumerate(pieces):
                        mask = g.AT[:, t, a + lo:a + hi] if m is None else m
                        ins = dve.tensor_tensor(block_[:, lo:hi], block_[:, lo:hi], mask, ALU.mult)
                        ins.then_inc(pt_ok if n == len(pieces) - 1 else mask_ok, 1)
                if c == 2:
                    for r in range(0, 4):
                        finish(r)
            for r in range(4, NT):
                finish(r)


def cosine_short(nc, g, wT, wh):
    with ExitStack() as ctx:
        s = Scope(nc, ctx, "coss")
        measured = s.sem("measured")
        whT = s.sb("whT", [128, 2, NP], F32)
        nsq = s.sb("nsq", [128, NT], F32)
        norm = s.sb("norm", [128, NT], F32)
        norm_row = s.sb("norm_row", [128, NP], F32)
        diag = s.sb("diag", [128, NT, 128], F16)
        den = s.sb("den", [128, 2, NP], F32)
        sim = s.sb("sim", [128, 2, NP], F32)
        sqT = sim
        probs = s.sb("probs", [128, NT, NP], F32)
        rsum = s.sb("rsum", [128, NT], F32)
        bank = [s.ps(f"bank{i}", [128, 512], F32) for i in range(8)]
        sp_passed, wh_mm, wh_out, whT_mm, whT_out, sq_ok, nb_mm, norm_ok, nsq_ok = (
            s.sem(k) for k in ("sp_passed", "wh_mm", "wh_out", "whT_mm", "whT_out", "sq_ok", "nb_mm", "norm_ok", "nsq_ok"))
        dot_mm, dot_used, exp_ok, probs_ok, agg_mm, agg_out, v = (
            s.sem(k) for k in ("dot_mm", "dot_used", "exp_ok", "probs_ok", "agg_mm", "agg_out", "v"))
        block = s.block()
        blocks = [(m, c) for m in range(2) for c in range(3)]

        @block.sync
        def _(sp):
            sp.sem_inc(sp_passed, 1)

        @block.tensor
        def _(pe):
            for n, (m, c) in enumerate(blocks):
                a, w = CH[c]
                if n >= 3:
                    pe.wait_ge(whT_out, n - 2)
                for k in range(2):
                    mm = pe.matmul(bank[n % 3][:, 0:w], wT[:, k, m * 128:(m + 1) * 128], g.hT[:, k, a:a + w],
                                   start=k == 0, stop=k == 1)
                mm.then_inc(whT_mm, 1)
            for t in range(NT):
                if t >= 3:
                    pe.wait_ge(wh_out, t - 2)
                    pe.wait_ge(nsq_ok, t - 2)
                for k in range(2):
                    mm = pe.matmul(bank[3 + t % 3][:, 0:D], g.hT[:, k, t * 128:(t + 1) * 128], wT[:, k, :],
                                   start=k == 0, stop=k == 1)
                mm.then_inc(wh_mm, 1)
            pe.wait_ge(whT_out, 6)
            pe.wait_ge(sq_ok, 2)
            for c, (a, w) in enumerate(CH):
                for k in range(2):
                    mm = pe.matmul(bank[c][:, 0:w], g.ones[:, :], sqT[:, k, a:a + w], start=k == 0, stop=k == 1)
                mm.then_inc(nb_mm, 1)
            pe.wait_ge(norm_ok, 4)
            pe.wait_ge(wh_out, NT)
            pe.wait_ge(nsq_ok, NT)
            for t in range(NT):
                for c, (a, w) in enumerate(CH):
                    n = 3 * t + c
                    if n >= 6:
                        pe.wait_ge(dot_used, n - 5)
                    for k in range(2):
                        mm = pe.matmul(bank[n % 6][:, 0:w], whT[:, k, t * 128:(t + 1) * 128], whT[:, k, a:a + w],
                                       start=k == 0, stop=k == 1)
                    mm.then_inc(dot_mm, 1)
            pe.wait_ge(dot_used, 3 * NT)
            for r in range(NT):
                if r >= 8:
                    pe.wait_ge(agg_out, r - 7)
                for t in range(NT):
                    pe.wait_ge(probs_ok, t + 1)
                    mm = pe.matmul(bank[r % 8][:, 0:D + 1], probs[:, t, r * 128:(r + 1) * 128], wh[:, t, :],
                                   start=t == 0, stop=t == NT - 1)
                mm.then_inc(agg_mm, 1)

        @block.scalar
        def _(act):
            for n, (m, c) in enumerate(blocks):
                a, w = CH[c]
                act.wait_ge(whT_mm, n + 1)
                act.activation(whT[:, m, a:a + w], bank[n % 3][:, 0:w], ACT.Copy).then_inc(whT_out, 1)
            for t in range(NT):
                act.wait_ge(wh_out, t + 1)
                act.activation(probs[:, t, 0:D], bank[3 + t % 3][:, 0:D], ACT.Square,
                               accum_out=nsq[:, t:t + 1]).then_inc(nsq_ok, 1)
            act.wait_ge(nsq_ok, NT)
            act.activation(norm[:, :], nsq[:, :], ACT.Sqrt).then_inc(norm_ok, 1)
            for c, (a, w) in enumerate(CH):
                act.wait_ge(nb_mm, c + 1)
                act.activation(norm_row[:, a:a + w], bank[c][:, 0:w], ACT.Sqrt).then_inc(norm_ok, 1)
            for t in range(NT):
                act.wait_ge(dot_used, 3 * t + 3)
                act.activation(sim[:, t % 2, :], sim[:, t % 2, :], ACT.Exp).then_inc(exp_ok, 1)

        @block.gpsimd
        def _(pool):
            for m in range(2):
                pool.wait_ge(whT_out, 3 * m + 3)
                pool.tensor_tensor(sqT[:, m, :], whT[:, m, :], whT[:, m, :], ALU.mult).then_inc(sq_ok, 1)

        @block.vector
        def _(dve):
            c_ = Chain(dve, v)
            c_.done(dve.memset(wh[:, :, D:D + 1], 1.0))
            for t in range(NT):
                dve.wait_ge(wh_mm, t + 1)
                dve.tensor_copy(wh[:, t, 0:D], bank[3 + t % 3][:, 0:D]).then_inc(wh_out, 1)
            for t in range(NT):
                c_.done(dve.tensor_tensor(diag[:, t, :], g.AT[:, t, t * 128:(t + 1) * 128], g.ident16[:, :], ALU.max))
            dve.wait_ge(norm_ok, 4)

            def mask(t):
                dve.wait_ge(exp_ok, t + 1)
                c_.wait()
                dve.tensor_tensor(probs[:, t, :], sim[:, t % 2, :], g.AT[:, t, :], ALU.mult).then_inc(v, 1)
                c_.n += 1
                c_.wait()
                dve.tensor_tensor(probs[:, t, t * 128:(t + 1) * 128], sim[:, t % 2, t * 128:(t + 1) * 128],
                                  diag[:, t, :], ALU.mult).then_inc(probs_ok, 1)

            for t in range(NT):
                if t >= 2:
                    dve.wait_ge(dot_used, 3 * (t - 1))
                c_.step(dve.tensor_scalar(den[:, t % 2, :], norm_row[:, :], norm[:, t:t + 1], 1e-8, ALU.mult, ALU.add))
                c_.step(dve.reciprocal(den[:, t % 2, :], den[:, t % 2, :]))
                if t >= 2:
                    dve.wait_ge(probs_ok, t - 1)
                for c, (a, w) in enumerate(CH):
                    n = 3 * t + c
                    dve.wait_ge(dot_mm, n + 1)
                    ins = dve.tensor_tensor(sim[:, t % 2, a:a + w], bank[n % 6][:, 0:w], den[:, t % 2, a:a + w],
                                            ALU.mult)
                    ins.then_inc(dot_used, 1)
                if t >= 1:
                    mask(t - 1)
            mask(NT - 1)
            for r in range(NT):
                dve.wait_ge(agg_mm, r + 1)
                c_.step(dve.reciprocal(rsum[:, r:r + 1], bank[r % 8][:, D:D + 1]))
                dve.scalar_tensor_tensor(out=g.x[:, r, :], in0=bank[r % 8][:, 0:D], scalar=rsum[:, r:r + 1],
                                         in1=g.x[:, r, :], op0=ALU.mult, op1=ALU.add).then_inc(agg_out, 1)
                measure(dve, g, r, agg_out, r + 1, measured)


def gat(nc, g, tag, inT, KT, space, H, O, val):
    w = space[:, 0:KT * H * O].rearrange("p (k o) -> p k o", o=H * O)
    ab = space[:, KT * H * O:(KT + 2) * H * O].rearrange("p (k o) -> p k o", o=H * O)
    with ExitStack() as ctx:
        s = Scope(nc, ctx, tag)
        b = Graph()
        b.wa = s.sb("wa", [128, KT, 2 * H], F32)
        b.sd = s.sb("sd", [128, NT, 2 * H], F32)
        b.hj = s.sb("hj", [128, NT, H], F32)
        b.f = s.sb("f", [128, NT, 2, H], F32)
        b.ri = s.sb("ri", [128, NT, H], F32)
        b.row = s.sb("row", [32 + H, NP], F32R)
        b.val = val
        gat_prelude(nc, g, tag + "p", inT, KT, w, ab, H, O, b)
        near = nc.values_load(g.near[0:1, 0:1], min_val=0, max_val=1)
        with nc.If(near == 1):
            if H > 1:
                gat_heads(nc, g, tag + "h", H, O, b, space)
            else:
                gat_one_head(nc, g, tag + "h", O, b)
        with nc.Else():
            gat_rowwise(nc, g, tag + "r", inT, KT, w, H, O, b)


SPREAD = 60.0
SPREAD16, WH_LOW, WH_HIGH, SCALE16 = 10.0, 0.5, 15.9, 4096.0


def gat_prelude(nc, g, tag, inT, KT, w, ab, H, O, b):
    HO, V1 = H * O, O + 1
    val, wa = b.val, b.wa
    with ExitStack() as ctx:
        s = Scope(nc, ctx, tag)
        prod = s.sb("prod", [128, 2, HO], F32)
        tops = s.sb("tops", [2 * H, 2, 3], F32)
        top = s.sb("top", [2 * H, 2], F32)
        dtop = s.sb("dtop", [2 * H, 2, 2 * H], F32)
        topb = s.sb("topb", [128, 4 * H], F32)
        dt = s.sb("dt", [H, H], F32)
        dcol = s.sb("dcol", [H, 1], F32)
        ok = s.sb("ok", [128, 2], F32)
        dn = s.sb("dn", [128, NT, H], F32)
        sn = s.sb("sn", [128, NT, H], F32)
        whmax = s.sb("whmax", [1, 3], F32)
        peaks = s.sb("peaks", [128, 2, NT], F32)
        absmax = s.sb("absmax", [128, 2], F32)
        rows = s.sb("rows", [2 * H, NP], F32)
        rowf = s.sb("rowf", [H, NP], F32)
        sb_ = [s.ps(f"sb{i}", [128, 512], F32) for i in range(3)]
        ag = [s.ps(f"ag{i}", [128, 512], F32) for i in range(5)]
        v, wa_ok, sd_mm, top_ok, topb_mm, dn_mm, dn_ok, f_ok, wh_mm, val_ok, dcol_ok, relu_ok, exp_ok, hi_ok = (
            s.sem(k) for k in ("v", "wa_ok", "sd_mm", "top_ok", "topb_mm", "dn_mm", "dn_ok", "f_ok",
                               "wh_mm", "val_ok", "dcol_ok", "relu_ok", "exp_ok", "hi_ok"))
        cleared, rows_ok, peak_ok, max_ok, max_mm = (s.sem(k) for k in ("cleared", "rows_ok", "peak_ok", "max_ok", "max_mm"))
        block = s.block()
        early = 6 if H > 1 else 3

        @block.gpsimd
        def _(pool):
            pool.memset(b.row[:, :].bitcast(F32), 0.0).then_inc(cleared, 1)

        @block.tensor
        def _(pe):
            def wh(t):
                if t >= 3:
                    pe.wait_ge(val_ok, t - 2)
                for k in range(KT):
                    mm = pe.matmul(ag[2 + t % 3][:, 0:HO], inT[:, k, t * 128:(t + 1) * 128], w[:, k, :],
                                   start=k == 0, stop=k == KT - 1)
                mm.then_inc(wh_mm, 1)

            for t in range(early):
                wh(t)
            pe.wait_ge(wa_ok, 2 * KT)
            for c, (a, wd) in enumerate(CH):
                for k in range(KT):
                    mm = pe.matmul(sb_[c][0:2 * H, 0:wd], wa[:, k, :], inT[:, k, a:a + wd],
                                   start=k == 0, stop=k == KT - 1)
                mm.then_inc(sd_mm, 1)
            for t in range(NT):
                pe.wait_ge(rows_ok, t // 4 + 1)
                mm = pe.transpose(ag[0][:, t * 2 * H:(t + 1) * 2 * H], rows[:, t * 128:(t + 1) * 128],
                                  g.ident[0:2 * H, 0:2 * H])
            mm.then_inc(dn_mm, 1)
            pe.wait_ge(top_ok, 1)
            pe.matmul(ag[1][:, 0:4 * H], g.ones[0:2 * H, :], dtop[:, :, :], start=True, stop=True).then_inc(topb_mm, 1)
            for t in range(early, NT):
                wh(t)
            if H > 1:
                pe.wait_ge(max_ok, 1)
                pe.transpose(ag[0][0:1, 0:128], absmax[:, 0:1], g.ident[:, :]).then_inc(max_mm, 1)

        @block.scalar
        def _(act):
            def copy(t):
                act.wait_ge(wh_mm, t + 1)
                act.activation(val[:, t, :].rearrange("p (h o) -> p h o", o=V1)[:, :, 0:O],
                               ag[2 + t % 3][:, 0:HO].rearrange("p (h o) -> p h o", o=O), ACT.Copy).then_inc(val_ok, 1)

            if H > 1:
                for t in range(early):
                    copy(t)
            for c, (a, wd) in enumerate(CH):
                act.wait_ge(sd_mm, c + 1)
                act.activation(rows[:, a:a + wd], sb_[c][0:2 * H, 0:wd], ACT.Copy).then_inc(rows_ok, 1)
            act.wait_ge(dn_ok, 2 if H > 1 else 1)
            act.activation(b.f[:, :, 0, :], dn[:, :, :], ACT.Exp, scale=0.2).then_inc(f_ok, 1)
            act.activation(b.hj[:, :, :], dn[:, :, :], ACT.Exp, scale=0.8).then_inc(f_ok, 1)
            if H > 1:
                act.activation(b.f[:, :, 1, :], dn[:, :, :], ACT.Exp).then_inc(f_ok, 1)
                act.activation(b.ri[:, :, :], sn[:, :, :], ACT.Exp, scale=-0.8).then_inc(f_ok, 1)
            act.wait_ge(dcol_ok, 1)
            for c, (a, wd) in enumerate(CH):
                ps = sb_[c][0:H, 0:wd]
                act.activation(ps, ps, ACT.Relu, bias=dcol[:, 0:1]).then_inc(relu_ok, 1)
                if H > 1:
                    copy(early + c)
                act.wait_ge(relu_ok, c + 1)
                act.activation(rowf[:, a:a + wd], ps, ACT.Exp, scale=-0.8).then_inc(exp_ok, 1)
            act.wait_ge(exp_ok, 3)
            act.wait_ge(cleared, 1)
            act.activation(b.row[0:H, :], rowf[:, :], ACT.Copy).then_inc(hi_ok, 1)
            if H > 1:
                for t in range(early + 3, NT):
                    copy(t)

        @block.vector
        def _(dve):
            c_ = Chain(dve, v)

            def peak(t):
                dve.wait_ge(val_ok, t + 1)
                for n, op in enumerate((ALU.max, ALU.min)):
                    dve.tensor_reduce(peaks[:, n, t:t + 1], vals[:, t, :, 0:O], axis=AX.XY, op=op).then_inc(peak_ok, 1)

            for n in range(2):
                for k in range(KT):
                    q = (n * KT + k) % 2
                    if n * KT + k >= 2:
                        dve.wait_ge(wa_ok, n * KT + k - 1)
                    c_.step(dve.tensor_tensor(prod[:, q, :], w[:, k, :], ab[:, n, :], ALU.mult))
                    dve.tensor_reduce(wa[:, k, n * H:(n + 1) * H], prod[:, q, :].rearrange("p (h o) -> p h o", h=H),
                                      axis=AX.X, op=ALU.add).then_inc(wa_ok, 1)
            if H > 1:
                vals = val[:, :, :].rearrange("p t (h o) -> p t h o", o=V1)
                c_.done(dve.memset(vals[:, :, :, O], 1.0))
                for t in range(early - 1):
                    peak(t)
            for c, (a, wd) in enumerate(CHV):
                dve.wait_ge(rows_ok, c + 1)
                for n, op in enumerate((ALU.max, ALU.min)):
                    c_.done(dve.tensor_reduce(tops[:, n, c:c + 1], rows[:, a:a + wd], axis=AX.X, op=op))
            c_.wait()
            c_.done(dve.tensor_reduce(top[:, 0:1], tops[:, 0, :], axis=AX.X, op=ALU.max))
            c_.step(dve.tensor_reduce(top[:, 1:2], tops[:, 1, :], axis=AX.X, op=ALU.min))
            c_.step(dve.tensor_tensor(top[:, 1:2], top[:, 0:1], top[:, 1:2], ALU.subtract))
            c_.step(dve.tensor_scalar(dtop[:, 0, :], g.ident[0:2 * H, 0:2 * H], top[:, 0:1], None, ALU.mult))
            dve.tensor_scalar(dtop[:, 1, :], g.ident[0:2 * H, 0:2 * H], top[:, 1:2], None,
                              ALU.mult).then_inc(top_ok, 1)
            dve.wait_ge(topb_mm, 1)
            dve.wait_ge(dn_mm, 1)
            c_.step(dve.tensor_copy(topb[:, :], ag[1][:, 0:4 * H]))
            c_.step(dve.tensor_copy(b.sd[:, :, :], ag[0][:, 0:NT * 2 * H].rearrange("p (t h) -> p t h", h=2 * H)))
            tb = topb[:, H:2 * H].unsqueeze(1).broadcast_to([128, NT, H])
            if H > 1:
                c_.step(dve.tensor_tensor(sn[:, :, :], b.sd[:, :, 0:H], tb, ALU.add))
                dve.tensor_scalar(sn[:, :, :], sn[:, :, :], 0.0, None, ALU.max).then_inc(dn_ok, 1)
            dve.tensor_tensor(dn[:, :, :], b.sd[:, :, H:2 * H], tb, ALU.subtract).then_inc(dn_ok, 1)
            c_.step(dve.tensor_tensor(dt[:, :], topb[0:H, H:2 * H], g.ident[0:H, 0:H], ALU.mult))
            dve.tensor_reduce(dcol[:, :], dt[:, :], axis=AX.X, op=ALU.add).then_inc(dcol_ok, 1)
            if H == 1:
                dve.wait_ge(f_ok, 2)
                for t in range(NT):
                    dve.wait_ge(wh_mm, t + 1)
                    c_.done(dve.tensor_copy(val[:, t, O:V1], b.f[:, t, 0, :]))
                    dve.tensor_tensor(val[:, t, 0:O], ag[2 + t % 3][:, 0:O], b.f[:, t, 0, :].broadcast_to([128, O]),
                                      ALU.mult).then_inc(val_ok, 1)
            else:
                for t in range(early - 1, NT):
                    peak(t)
                dve.wait_ge(peak_ok, 2 * NT)
                c_.done(dve.tensor_reduce(absmax[:, 0:1], peaks[:, 0, :], axis=AX.X, op=ALU.max))
                c_.step(dve.tensor_reduce(absmax[:, 1:2], peaks[:, 1, :], axis=AX.X, op=ALU.min))
                dve.scalar_tensor_tensor(out=absmax[:, 0:1], in0=absmax[:, 1:2], scalar=-1.0, in1=absmax[:, 0:1],
                                         op0=ALU.mult, op1=ALU.max).then_inc(max_ok, 1)
                dve.wait_ge(f_ok, 4)
                c_.step(dve.tensor_scalar(b.f[:, :, :, :], b.f[:, :, :, :], SCALE16, None, ALU.mult))
                dve.wait_ge(max_mm, 1)
                c_.step(dve.tensor_reduce(whmax[:, 0:1], ag[0][0:1, 0:128], axis=AX.X, op=ALU.max))
                c_.step(dve.tensor_scalar(whmax[:, 1:2], whmax[:, 0:1], WH_LOW, None, ALU.is_ge))
                c_.step(dve.tensor_scalar(whmax[:, 2:3], whmax[:, 0:1], WH_HIGH, None, ALU.is_le))
                c_.step(dve.tensor_tensor(whmax[:, 1:2], whmax[:, 1:2], whmax[:, 2:3], ALU.mult))
            c_.step(dve.tensor_reduce(ok[:, 0:1], topb[:, 3 * H:4 * H], axis=AX.X, op=ALU.max))
            c_.step(dve.tensor_scalar(ok[:, 0:1], ok[:, 0:1], SPREAD16 if H > 1 else SPREAD, None, ALU.is_le))
            c_.step(dve.tensor_scalar(ok[:, 1:2], g.fewest[:, 0:1], 0.5, None, ALU.is_gt))
            if H > 1:
                c_.step(dve.tensor_tensor(ok[0:1, 0:1], ok[0:1, 0:1], whmax[:, 1:2], ALU.mult))
            c_.step(dve.tensor_tensor(g.near[:, :], ok[0:1, 0:1], ok[0:1, 1:2], ALU.mult))
            dve.wait_ge(hi_ok, 1)
            c_.step(dve.tensor_tensor(b.row[32:32 + H, :], rowf[:, :], b.row[0:H, :].bitcast(F32), ALU.subtract))


def hold(eng, sem, value, passed):
    eng.wait_ge(sem, value)
    eng.sem_inc(passed, 1)


def head_pairs(eng, H, body):
    with eng.Fori(0, H // 2 - 1) as pair:
        body(pair * 2, 0, 2)
        body(pair * 2 + 1, 1, 2)
    body(H - 2, 0, 1)
    body(H - 1, 1, 0)


def gat_heads(nc, g, tag, H, O, b, space):
    V1 = O + 1
    G = 2 if 8 * V1 <= 512 else 1
    chunks = HALVES if G == 2 else CH
    C = len(chunks)
    MB = G
    groups = [(a, k) for c in chunks for a in range(c[0] // 128, (c[0] + c[1]) // 128, G)
              for k in (min(G, (c[0] + c[1]) // 128 - a),)]
    NG, NB = len(groups), 4
    in_chunk = [[n for n, (a, k) in enumerate(groups) if c[0] <= a * 128 < c[0] + c[1]] for c in chunks]
    val, hj = b.val, b.hj
    with ExitStack() as ctx:
        s = Scope(nc, ctx, tag)
        sel = [s.sb(f"sel{e}", [32 + H, 128], F32R) for e in range(2)]
        vf = g.hT[:, :, :].rearrange("p f i -> p (f i)")[:, 0:NT * 2 * V1].rearrange("p (t q o) -> p t q o", q=2, o=V1)
        both = space[:, 0:NT * 2 * V1].rearrange("p (t q o) -> p t q o", q=2, o=V1)
        vv = [s.sb(f"vv{e}", [128, NT, 6, V1], F16) for e in range(2)]
        neg = [[s.sb(f"neg{m}{c}", [128, NT, w], F16) for c, (a, w) in enumerate(chunks)] for m in range(MB)]
        parts = [s.sb(f"parts{e}", [128, NT, 4, V1], F32) for e in range(2)]
        row = [s.ps(f"row{c}", [128, (w + 511) // 512, 512], F32) for c, (a, w) in enumerate(chunks)]
        ag = [s.ps(f"ag{i}", [128, 512], F32) for i in range(NB)]
        sel_ok, vf_ok, vhi_ok, vlo_ok, vneg_ok, row_mm, neg_ok, agg_mm, agg_out, sum_ok, val_ok, passed = (
            s.sem(k) for k in ("sel_ok", "vf_ok", "vhi_ok", "vlo_ok", "vneg_ok", "row_mm", "neg_ok", "agg_mm",
                               "agg_out", "sum_ok", "val_ok", "passed"))
        block = s.block()

        @block.sync
        def _(sp):
            sp.sem_inc(passed, 1)

        @block.tensor
        def _(pe):
            def rows(h, e, c):
                a, wd = chunks[c]
                pe.wait_ge(sel_ok, h + 1)
                if not (isinstance(h, int) and h == 0):
                    pe.wait_ge(neg_ok, C * NT * (h - 1) + NT * (c + 1))
                for q in range(0, wd, 512):
                    n = min(512, wd - q)
                    mm = pe.matmul(row[c][:, q // 512, 0:n], sel[e][:, :], b.row[:, a + q:a + q + n],
                                   start=True, stop=True)
                mm.then_inc(row_mm, 1)

            for c in range(C):
                rows(0, 0, c)

            def head(h, e, follow):
                pe.wait_ge(vneg_ok, h + 1)
                for c in range(C):
                    if follow:
                        rows(h + 1, 1 - e, c)
                    for n in in_chunk[c]:
                        a, k = groups[n]
                        last = n - NB if n >= NB else max(m for m in range(NG) if m % NB == n % NB) - NG
                        pe.wait_ge(agg_out, NG * (h + 2) + last + 1)
                        for i in range(k):
                            off = (a + i) * 128 - chunks[c][0]
                            out = ag[n % NB][:, i * 4 * V1:(i + 1) * 4 * V1]
                            for t in range(NT):
                                if n == in_chunk[c][0] and i == 0:
                                    pe.wait_ge(neg_ok, C * NT * h + NT * c + t + 1)
                                pe.matmul(out, neg[e % MB][c][:, t, off:off + 128], vv[e][:, t, 0:4, :],
                                          start=t == 0, stop=False)
                                mm = pe.matmul(out[:, 2 * V1:4 * V1], g.AT[:, t, (a + i) * 128:(a + i + 1) * 128],
                                               vv[e][:, t, 4:6, :], start=False, stop=t == NT - 1)
                        mm.then_inc(agg_mm, 1)

            head_pairs(pe, H, head)

        def total(eng, h, e):
            eng.wait_ge(val_ok, h + 2)
            eng.wait_ge(agg_out, NG * (h + 2) + NG)
            eng.tensor_tensor(both[:, :, :, :], parts[e][:, :, 0:4:2, :], parts[e][:, :, 1:4:2, :],
                              ALU.add).then_inc(sum_ok, 1)
            hold(eng, sum_ok, 2 * h + 1, passed)
            eng.tensor_tensor(both[:, :, 0, :], both[:, :, 0, :],
                              b.ri[:, :, bass.ds(h, 1)].broadcast_to([128, NT, V1]), ALU.mult).then_inc(sum_ok, 1)
            hold(eng, sum_ok, 2 * h + 2, passed)
            eng.tensor_tensor(val[:, :, bass.ds(h * V1, V1)], both[:, :, 0, :], both[:, :, 1, :],
                              ALU.add).then_inc(val_ok, 1)

        @block.gpsimd
        def _(pool):
            pool.sem_inc(agg_out, 2 * NG)
            pool.sem_inc(val_ok, 2)

            def select(h, e):
                high, low = (g.ident[0:32 + H, bass.ds(h + first, 1)].broadcast_to([32 + H, 128]) for first in (0, 32))
                pool.tensor_tensor(sel[e][:, :], high, low, ALU.add).then_inc(sel_ok, 1)

            def values(h, e):
                pool.tensor_tensor(vf[:, :, :, :],
                                   val[:, :, bass.ds(h * V1, V1)].unsqueeze(2).broadcast_to([128, NT, 2, V1]),
                                   b.f[:, :, :, bass.ds(h, 1)].broadcast_to([128, NT, 2, V1]),
                                   ALU.mult).then_inc(vf_ok, 1)
                pool.wait_ge(vhi_ok, h + 1)
                pool.tensor_tensor(vv[e][:, :, 1:6:4, :], vf[:, :, :, :], vv[e][:, :, 0:5:4, :],
                                   ALU.subtract).then_inc(vlo_ok, 1)

            select(0, 0)
            values(0, 0)
            select(1, 1)
            hold(pool, vlo_ok, 1, passed)
            values(1, 1)

            def head(h, e, follow):
                if follow == 2:
                    hold(pool, row_mm, C * (h + 1), passed)
                    select(h + 2, e)
                if follow:
                    total(pool, h, e)
                if follow == 2:
                    hold(pool, vlo_ok, h + 2, passed)
                    hold(pool, val_ok, h + 3, passed)
                    values(h + 2, e)

            head_pairs(pool, H, head)

        @block.scalar
        def _(act):
            def high(h, e):
                act.wait_ge(vf_ok, h + 1)
                act.activation(vv[e][:, :, 0:5:4, :], vf[:, :, :, :], ACT.Copy).then_inc(vhi_ok, 1)

            def negate(h, e):
                act.wait_ge(vlo_ok, h + 1)
                act.activation(vv[e][:, :, 2:4, :], vv[e][:, :, 4:6, :], ACT.Copy, scale=-1.0).then_inc(vneg_ok, 1)

            high(0, 0)
            negate(0, 0)

            def head(h, e, follow):
                act.wait_ge(val_ok, h + 1)
                for c in range(C):
                    for n in in_chunk[c]:
                        a, k = groups[n]
                        act.wait_ge(agg_mm, NG * h + n + 1)
                        act.activation(parts[e][:, a:a + k, :, :],
                                       ag[n % NB][:, 0:k * 4 * V1].rearrange("p (i q o) -> p i q o", q=4, o=V1),
                                       ACT.Copy).then_inc(agg_out, 1)
                        if follow and n == in_chunk[1][1]:
                            negate(h + 1, 1 - e)
                    if follow and c == 0:
                        high(h + 1, 1 - e)

            head_pairs(act, H, head)

        @block.vector
        def _(dve):
            def head(h, e, follow):
                for c in range(C):
                    a, wd = chunks[c]
                    whole_row = row[c][:, :, :].rearrange("p q i -> p (q i)")[:, 0:wd]
                    dve.wait_ge(row_mm, C * h + c + 1)
                    dve.wait_ge(agg_out, NG * (h + 2 - MB) + in_chunk[c][-1] + 1)
                    for t in range(NT):
                        dve.scalar_tensor_tensor(out=neg[e % MB][c][:, t, :], in0=whole_row,
                                                 scalar=hj[:, t, bass.ds(h, 1)], in1=g.AT[:, t, a:a + wd],
                                                 op0=ALU.is_ge, op1=ALU.mult).then_inc(neg_ok, 1)

            head_pairs(dve, H, head)
            total(dve, H - 1, 1)


def gat_one_head(nc, g, tag, O, b):
    V1 = O + 1
    NB = 4
    with ExitStack() as ctx:
        s = Scope(nc, ctx, tag)
        sel = s.sb("sel", [33, 128], F32R)
        row = g.hT[:, :, :].rearrange("p f i -> p (f i)")[:, 0:3 * 512].rearrange("p (c i) -> p c i", i=512)
        pt = [s.sb(f"pt{c}", [128, NT, CH[c][1]], F32) for c in range(3)]
        sb_ = [s.ps(f"sb{i}", [128, 512], F32) for i in range(3)]
        ag = [s.ps(f"ag{i}", [128, 512], F32) for i in range(NB)]
        sel_ok, s_mm, row_ok, pt_ok, agg_mm, agg_out, sp_passed = (
            s.sem(k) for k in ("sel_ok", "s_mm", "row_ok", "pt_ok", "agg_mm", "agg_out", "sp_passed"))
        block = s.block()

        @block.sync
        def _(sp):
            sp.sem_inc(sp_passed, 1)

        @block.gpsimd
        def _(pool):
            pool.tensor_tensor(sel[:, :], g.ident[0:33, 0:1].broadcast_to([33, 128]),
                               g.ident[0:33, 32:33].broadcast_to([33, 128]), ALU.add).then_inc(sel_ok, 1)

        @block.tensor
        def _(pe):
            pe.wait_ge(sel_ok, 1)
            for c, (a, wd) in enumerate(CH):
                pe.matmul(sb_[c][:, 0:wd], sel[:, :], b.row[:, a:a + wd], start=True, stop=True).then_inc(s_mm, 1)
            for r in range(NT):
                c = r // 4
                if r >= NB:
                    pe.wait_ge(agg_out, r - NB + 1)
                for t in range(NT):
                    if r % 4 == 0:
                        pe.wait_ge(pt_ok, NT * c + t + 1)
                    mm = pe.matmul(ag[r % NB][:, 0:V1], pt[c][:, t, (r % 4) * 128:(r % 4 + 1) * 128], b.val[:, t, :],
                                   start=t == 0, stop=t == NT - 1)
                mm.then_inc(agg_mm, 1)

        @block.scalar
        def _(act):
            for c, (a, wd) in enumerate(CH):
                act.wait_ge(s_mm, c + 1)
                act.activation(row[:, c, 0:wd], sb_[c][:, 0:wd], ACT.Copy).then_inc(row_ok, 1)
            for r in range(NT):
                act.wait_ge(agg_mm, r + 1)
                act.activation(g.sums1[:, r, :], ag[r % NB][:, 0:V1], ACT.Copy).then_inc(agg_out, 1)

        @block.vector
        def _(dve):
            for c, (a, wd) in enumerate(CH):
                dve.wait_ge(row_ok, c + 1)
                for t in range(NT):
                    dve.scalar_tensor_tensor(out=pt[c][:, t, :], in0=row[:, c, 0:wd], scalar=b.hj[:, t, 0:1],
                                             in1=g.AT[:, t, a:a + wd], op0=ALU.max, op1=ALU.mult).then_inc(pt_ok, 1)


NEG = -9e15


def gat_rowwise(nc, g, tag, inT, KT, w, H, O, b):
    V1, HO = O + 1, H * O
    val = b.val
    with ExitStack() as ctx:
        s = Scope(nc, ctx, tag)
        wab = s.sb("wab", [128, KT, 128], F32)
        vh = s.sb("vh", [128, NT, V1], F32)
        drow = s.sb("drow", [128, NP], F32)
        e = s.sb("e", [128, NP], F32)
        bias = s.sb("bias", [128, NP], F32)
        p = s.sb("p", [128, NP], F32)
        pT = s.sb("pT", [128, NT, 128], F32)
        neg, total, inv = (s.sb(k, [128, 1], F32) for k in ("neg", "total", "inv"))
        bank = [s.ps(f"bank{i}", [128, 512], F32) for i in range(8)]
        wh_mm, val_ok, copied, d_mm, d_ok, v, sc_ok, p_ok, pn_ok, t_mm, t_ok, a_mm, a_ok, passed = (
            s.sem(k) for k in ("wh_mm", "val_ok", "copied", "d_mm", "d_ok", "v", "sc_ok", "p_ok", "pn_ok",
                               "t_mm", "t_ok", "a_mm", "a_ok", "passed"))
        block = s.block()

        @block.sync
        def _(sp):
            sp.sem_inc(passed, 1)

        @block.gpsimd
        def _(pool):
            pool.memset(p[:, N:NP], 0.0).then_inc(copied, 1)
            pool.wait_ge(copied, 1)
            pool.wait_ge(val_ok, NT)
            pool.sem_inc(a_ok, 1)
            with pool.Fori(0, H) as h:
                pool.wait_ge(a_ok, NT * h + 1)
                pool.sem_inc(passed, 1)
                pool.tensor_copy(wab[:, :, :],
                                 b.wa[:, :, bass.ds(h + H, 1)].broadcast_to([128, KT, 128])).then_inc(copied, 1)
                pool.tensor_copy(vh[:, :, :], val[:, :, bass.ds(h * V1, V1)]).then_inc(copied, 1)

        @block.tensor
        def _(pe):
            for t in range(NT):
                if t >= 2:
                    pe.wait_ge(val_ok, t - 1)
                for k in range(KT):
                    mm = pe.matmul(bank[t % 2][:, 0:HO], inT[:, k, t * 128:(t + 1) * 128], w[:, k, :],
                                   start=k == 0, stop=k == KT - 1)
                mm.then_inc(wh_mm, 1)
            with pe.Fori(0, H) as h:
                pe.wait_ge(copied, 2 * h + 3)
                for c, (a, wd) in enumerate(CH):
                    for k in range(KT):
                        mm = pe.matmul(bank[2 + c][:, 0:wd], wab[:, k, :], inT[:, k, a:a + wd],
                                       start=k == 0, stop=k == KT - 1)
                    mm.then_inc(d_mm, 1)
                for r in range(NT):
                    pe.wait_ge(pn_ok, NT * h + r + 1)
                    for t in range(NT):
                        mm = pe.transpose(bank[5 + t // 4][:, (t % 4) * 128:(t % 4 + 1) * 128],
                                          p[:, t * 128:(t + 1) * 128], g.ident[:, :])
                    mm.then_inc(t_mm, 1)
                    pe.wait_ge(t_ok, 3 * (NT * h + r) + 3)
                    for t in range(NT):
                        mm = pe.matmul(bank[0][:, 0:V1], pT[:, t, :], vh[:, t, :], start=t == 0, stop=t == NT - 1)
                    mm.then_inc(a_mm, 1)

        @block.scalar
        def _(act):
            with act.Fori(0, H) as h:
                for r in range(NT):
                    act.wait_ge(sc_ok, NT * h + r + 1)
                    act.activation(p[:, 0:N], e[:, 0:N], ACT.Exp, bias=neg[:, 0:1],
                                   accum_out=total[:, 0:1]).then_inc(p_ok, 1)
                    act.wait_ge(a_mm, NT * h + r + 1)
                    act.sem_inc(passed, 1)
                    dst = val[:, r, bass.ds(h * V1, V1)] if H > 1 else g.sums1[:, r, :]
                    act.activation(dst, bank[0][:, 0:V1], ACT.Copy).then_inc(a_ok, 1)

        @block.vector
        def _(dve):
            dve.sem_inc(v, 1)
            for t in range(NT):
                dve.wait_ge(wh_mm, t + 1)
                vv = val[:, t, :].rearrange("p (h o) -> p h o", o=V1)
                dve.memset(vv[:, :, O:V1], 1.0).then_inc(v, 1)
                dve.tensor_copy(vv[:, :, 0:O], bank[t % 2][:, 0:HO].rearrange("p (h o) -> p h o", o=O)).then_inc(val_ok, 1)
            dve.wait_ge(v, 1 + NT)
            first = 1 + NT
            S = 6
            with dve.Fori(0, H) as h:
                for c, (a, wd) in enumerate(CH):
                    dve.wait_ge(d_mm, 3 * h + c + 1)
                    dve.tensor_copy(drow[:, a:a + wd], bank[2 + c][:, 0:wd]).then_inc(d_ok, 1)
                dve.wait_ge(d_ok, 3 * h + 3)
                for r in range(NT):
                    base = first + S * (NT * h + r)
                    dve.wait_ge(a_ok, NT * h + r + 1)
                    dve.tensor_scalar(e[:, 0:N], drow[:, 0:N], b.sd[:, r, bass.ds(h, 1)], None, ALU.add).then_inc(v, 1)
                    dve.tensor_scalar(bias[:, 0:N], g.A[:, r, 0:N], -1.0, -NEG, ALU.add, ALU.mult).then_inc(v, 1)
                    dve.wait_ge(v, base + 2)
                    dve.scalar_tensor_tensor(out=e[:, 0:N], in0=e[:, 0:N], scalar=0.2, in1=e[:, 0:N],
                                             op0=ALU.mult, op1=ALU.max).then_inc(v, 1)
                    dve.wait_ge(v, base + 3)
                    dve.tensor_tensor(e[:, 0:N], e[:, 0:N], bias[:, 0:N], ALU.add).then_inc(v, 1)
                    dve.wait_ge(v, base + 4)
                    dve.tensor_reduce(neg[:, :], e[:, 0:N], axis=AX.X, op=ALU.max).then_inc(v, 1)
                    dve.wait_ge(v, base + 5)
                    dve.tensor_scalar(neg[:, :], neg[:, :], -1.0, None, ALU.mult).then_inc(sc_ok, 1)
                    dve.wait_ge(p_ok, NT * h + r + 1)
                    dve.reciprocal(inv[:, :], total[:, :]).then_inc(v, 1)
                    dve.wait_ge(v, base + 6)
                    dve.tensor_scalar(p[:, 0:N], p[:, 0:N], inv[:, 0:1], None, ALU.mult).then_inc(pn_ok, 1)
                    dve.wait_ge(t_mm, NT * h + r + 1)
                    for q in range(3):
                        k = min(4, NT - 4 * q)
                        dve.tensor_copy(pT[:, 4 * q:4 * q + k, :],
                                        bank[5 + q][:, 0:k * 128].rearrange("p (t i) -> p t i", i=128)).then_inc(t_ok, 1)


def normalise_elu(nc, g, tag, raw, H, O, outT, loads=()):
    HO, V1 = H * O, O + 1
    F = HO // 128
    with ExitStack() as ctx:
        s = Scope(nc, ctx, tag)
        inv = s.sb("inv", [128, NT, H], F32)
        B = 3
        xn, e, y = (s.sb(k, [128, B, HO], F32) for k in ("xn", "e", "y"))
        tp = [s.ps(f"tp{i}", [128, F, 128], F32) for i in range(3)]
        minus1 = s.sb("minus1", [128, 1], F32)
        v, xn_ok, neg_ok, exp_ok, y_ok, turned, out = (
            s.sem(k) for k in ("v", "xn_ok", "neg_ok", "exp_ok", "y_ok", "turned", "out"))
        block = s.block()
        fetch(block, s, loads)

        @block.vector
        def _(dve):
            c = Chain(dve, v)
            r4 = raw[:, :, :].rearrange("p t (h o) -> p t h o", o=V1)
            c.done(dve.memset(minus1[:, :], -1.0))
            c.step(dve.reciprocal(inv[:, :, :], r4[:, :, :, O]))

            def finish(t):
                b = t % B
                dve.wait_ge(exp_ok, t + 1)
                if t >= B:
                    dve.wait_ge(turned, t - B + 1)
                dve.scalar_tensor_tensor(out=y[:, b, :], in0=xn[:, b, :], scalar=0.0, in1=e[:, b, :],
                                         op0=ALU.max, op1=ALU.add).then_inc(y_ok, 1)

            for t in range(NT):
                b = t % B
                if t >= B:
                    dve.wait_ge(y_ok, t - B + 1)
                dve.tensor_tensor(xn[:, b, :].rearrange("p (h o) -> p h o", o=O), r4[:, t, :, 0:O],
                                  inv[:, t, :].unsqueeze(2).broadcast_to([128, H, O]), ALU.mult).then_inc(xn_ok, 1)
                if t >= 2:
                    finish(t - 2)
            finish(NT - 2)
            finish(NT - 1)

        @block.scalar
        def _(act):
            for t in range(NT + 2):
                if t < NT:
                    b = t % B
                    act.wait_ge(xn_ok, t + 1)
                    if t >= B:
                        act.wait_ge(y_ok, t - B + 1)
                    act.activation(e[:, b, :], xn[:, b, :], ACT.Relu, scale=-1.0).then_inc(neg_ok, 1)
                    act.wait_ge(neg_ok, t + 1)
                    act.activation(e[:, b, :], e[:, b, :], ACT.Exp, scale=-1.0).then_inc(exp_ok, 1)
                if t >= 2:
                    act.wait_ge(turned, t - 1)
                    act.activation(outT[:, :, (t - 2) * 128:(t - 1) * 128], tp[(t - 2) % 3][:, :, :],
                                   ACT.Identity, bias=minus1[:, 0:1]).then_inc(out, 1)

        @block.tensor
        def _(pe):
            for t in range(NT):
                pe.wait_ge(y_ok, t + 1)
                if t >= 3:
                    pe.wait_ge(out, t - 2)
                for f in range(F):
                    mm = pe.transpose(tp[t % 3][:, f, :], y[:, t % B, f * 128:(f + 1) * 128], g.ident[:, :])
                mm.then_inc(turned, 1)


def mlp(nc, g, tag, inT, weights, func, check_symmetry=False):
    w1, b1, w2, b2 = weights
    F = w2.shape[1]
    with ExitStack() as ctx:
        s = Scope(nc, ctx, tag)
        z = s.sb("z", [128, F, NP], F32)
        bank = [s.ps(f"bank{i}", [128, 512], F32) for i in range(8)]
        z_mm, z_ok, y_mm, y_ok, xb_ok, measured = (
            s.sem(k) for k in ("z_mm", "z_ok", "y_mm", "y_ok", "xb_ok", "measured"))
        block = s.block()
        blocks = [(c, m) for c in range(3) for m in range(F)]
        if check_symmetry:
            diff = s.sb("diff", [128, NT, N], F16)
            most = s.sb("most", [128, 4], F32)
            v, most_ok, all_ok = s.sem("v"), s.sem("most_ok"), s.sem("all_ok")

        @block.gpsimd
        def _(pool):
            for t in range(NT):
                pool.tensor_tensor(g.x[:, t, :], g.x[:, t, :], b2[:, :], ALU.add).then_inc(xb_ok, 1)

        if check_symmetry:
            @block.gpsimd
            def _(pool):
                pool.wait_ge(most_ok, 1)
                pool.partition_all_reduce(most[:, 1:2], most[:, 0:1], 128, RMAX).then_inc(all_ok, 1)

        @block.tensor
        def _(pe):
            for n, (c, m) in enumerate(blocks):
                a, w = CH[c]
                if n >= 4:
                    pe.wait_ge(z_ok, n - 3)
                for k in range(2):
                    mm = pe.matmul(bank[n % 4][:, 0:w], w1[:, k, m * 128:(m + 1) * 128], inT[:, k, a:a + w],
                                   start=k == 0, stop=k == 1)
                mm.then_inc(z_mm, 1)
            for t in range(NT):
                pe.wait_ge(z_ok, F * (t // 4 + 1))
                if t >= 4:
                    pe.wait_ge(y_ok, t - 3)
                for k in range(F):
                    mm = pe.matmul(bank[4 + t % 4][:, 0:D], z[:, k, t * 128:(t + 1) * 128], w2[:, k, :],
                                   start=k == 0, stop=k == F - 1)
                mm.then_inc(y_mm, 1)

        @block.scalar
        def _(act):
            for n, (c, m) in enumerate(blocks):
                a, w = CH[c]
                act.wait_ge(z_mm, n + 1)
                act.activation(z[:, m, a:a + w], bank[n % 4][:, 0:w], func, bias=b1[:, m:m + 1]).then_inc(z_ok, 1)

        @block.vector
        def _(dve):
            if check_symmetry:
                c = Chain(dve, v)
                c.step(dve.tensor_tensor(diff[:, :, :], g.A[:, :, 0:N], g.AT[:, :, 0:N], ALU.subtract))
                dve.tensor_reduce(most[:, 0:1], diff[:, :, :], axis=AX.XY, op=ALU.max).then_inc(most_ok, 1)
                dve.wait_ge(all_ok, 1)
                c.step(dve.tensor_scalar(g.symmetric[:, :], most[0:1, 1:2], 0.0, None, ALU.is_le))
            for t in range(NT):
                dve.wait_ge(y_mm, t + 1)
                dve.wait_ge(xb_ok, t + 1)
                dve.tensor_tensor(g.x[:, t, :], bank[4 + t % 4][:, 0:D], g.x[:, t, :], ALU.add).then_inc(y_ok, 1)
                if t >= 1:
                    measure(dve, g, t - 1, y_ok, t, measured)
            measure(dve, g, NT - 1, y_ok, NT, measured)


STATE_SCALE = 1024.0


def gated_graph(nc, g, d):
    symmetric = nc.values_load(g.symmetric[0:1, 0:1], min_val=0, max_val=1)
    with nc.If(symmetric == 1):
        gated_network(nc, g, d, "s", 1)
    with nc.Else():
        gated_network(nc, g, d, "a", 2)


def gated_network(nc, g, d, tag, sides):
    with ExitStack() as ctx:
        s = Scope(nc, ctx, "ggnn" + tag)
        gw = [s.sb(f"gw{i}", [128, 2 * sides + 2, 3 * D], F32R) for i in range(2)]
        bw = s.sb("bw", [6, 3 * D], F32R)
        deg = s.sb("deg", [6, N], F32R)
        nm = [s.sb(f"nm{i}", [128, NT, D], F16) for i in range(2)]
        gate_weights(nc, g, d, tag, sides, gw, bw, deg, nm)
        gated_steps(nc, g, tag, sides, gw, bw, deg, nm)


def gate_weights(nc, g, d, tag, sides, gw, bw, deg, nm):
    with ExitStack() as ctx:
        s = Scope(nc, ctx, "gate" + tag)
        win = s.sb("win", [128, 2, 2, D], F32)
        wst = s.sb("wst", [128, 6, 3 * D], F32)
        bcol = s.sb("bcol", [128, 2, 2], F32)
        brow = s.sb("brow", [1, 3 * D], F32)
        blhs = s.sb("blhs", [128, 2, 2, 6], F32)
        elhs = s.sb("elhs", [1, 6], F32)
        dlhs = s.sb("dlhs", [128, 2, 6], F16)
        dl1 = s.sb("dl1", [1, 6], F16)
        one16 = s.sb("one16", [1, 512], F16)
        first3 = s.sb("first3", [6, 1], F32)
        last3 = s.sb("last3", [6, 1], F32)
        bhi = s.sb("bhi", [6, 3 * D], F32R)
        blo = s.sb("blo", [6, 3 * D], F32)
        bank = [s.ps(f"bank{i}", [128, 512], F32) for i in range(8)]
        w_in, v, lhs_ok, g_mm, hi_ok, lo_ok, own_ok, b_mm, d_mm, d_ok, turned, nhi, nlo = (
            s.sem(k) for k in ("w_in", "v", "lhs_ok", "g_mm", "hi_ok", "lo_ok", "own_ok", "b_mm", "d_mm", "d_ok",
                               "turned", "nhi", "nlo"))
        block = s.block()
        HALF = 3 * D // 2
        prods = [(side, k, n) for side in range(sides) for k in range(2) for n in range(2)]
        own = 2 * sides
        n_in = 16 * 10

        @block.sync
        def _(sp):
            for i, name in enumerate(("in_W", "out_W")):
                sp.dma_start(win[:, i, :, :], d[name].rearrange("(k p) o -> p k o", p=128)).then_inc(w_in, 16)
            for i, name in enumerate(("r_WT", "z_WT", "h_WT")):
                sp.dma_start(wst[:, :, i * D:(i + 1) * D],
                             d[name].rearrange("(k p) o -> p k o", p=128)).then_inc(w_in, 16)
            for i, name in enumerate(("in_b", "out_b")):
                sp.dma_start(bcol[:, i, :], d[name]).then_inc(w_in, 16)
            for i, name in enumerate(("r_b", "z_b", "h_b")):
                sp.dma_start(brow[:, i * D:(i + 1) * D], d[name].unsqueeze(0)).then_inc(w_in, 16)

        @block.gpsimd
        def _(pool):
            n = 0
            for m in (blhs, elhs, dlhs, dl1):
                ap = m[:, :, :, :] if m is blhs else m[:, :, :] if m is dlhs else m[:, :]
                n += 1
                pool.memset(ap, 0.0).then_inc(lhs_ok, 1)
                pool.wait_ge(lhs_ok, n)
            pool.memset(one16[:, :], 1.0).then_inc(lhs_ok, 1)
            pool.wait_ge(lhs_ok, 5)
            for q in range(2):
                for side in range(2):
                    pool.memset(dlhs[:, side if sides == 2 else 0, side + 3 * q:side + 3 * q + 1], 1.0).then_inc(lhs_ok, 1)
                pool.memset(elhs[:, 2 + 3 * q:3 + 3 * q], 1.0).then_inc(lhs_ok, 1)
                pool.memset(dl1[:, 2 + 3 * q:3 + 3 * q], 1.0).then_inc(lhs_ok, 1)
            pool.wait_ge(w_in, n_in)
            for q in range(2):
                for side in range(2):
                    pool.tensor_copy(blhs[:, side, :, side + 3 * q], bcol[:, side, :]).then_inc(lhs_ok, 1)

        @block.tensor
        def _(pe):
            pe.wait_ge(lhs_ok, 13)
            for c, (a, w) in enumerate(CHV):
                if c == 2:
                    pe.wait_ge(d_ok, 1)
                for t in range(NT):
                    pe.matmul(bank[6 + c % 2][0:6, 0:w], dlhs[:, 0, :], g.AT[:, t, a:a + w], start=t == 0, stop=False)
                    if sides == 2:
                        pe.matmul(bank[6 + c % 2][0:6, 0:w], dlhs[:, 1, :], g.A[:, t, a:a + w], start=False, stop=False)
                pe.matmul(bank[6 + c % 2][0:6, 0:w], dl1[:, :], one16[:, 0:w], start=False, stop=True).then_inc(d_mm, 1)
            for t in range(NT):
                if t >= 4:
                    pe.wait_ge(nlo, t - 3)
                for f in range(2):
                    mm = pe.transpose(bank[t % 4][:, f * 128:(f + 1) * 128], g.hT[:, f, t * 128:(t + 1) * 128],
                                      g.ident[:, :])
                mm.then_inc(turned, 1)
            pe.wait_ge(w_in, n_in)
            pe.wait_ge(lhs_ok, 17)
            for half in range(2):
                cols = slice(half * HALF, (half + 1) * HALF)
                for side in range(2):
                    for o in range(2):
                        pe.matmul(bank[4 + half][0:6, 0:HALF], blhs[:, side, o, :], wst[:, 2 * side + o, cols],
                                  start=side + o == 0, stop=False)
                pe.matmul(bank[4 + half][0:6, 0:HALF], elhs[:, :], brow[:, cols], start=False, stop=True).then_inc(b_mm, 1)
            pe.wait_ge(nlo, NT)
            for n, (side, k, half) in enumerate(prods):
                if n >= 4:
                    pe.wait_ge(lo_ok, n - 3)
                terms = [(sd, o) for sd in ((side,) if sides == 2 else (0, 1)) for o in range(2)]
                for i, (sd, o) in enumerate(terms):
                    mm = pe.matmul(bank[n % 4][:, 0:HALF], win[:, sd, o, k * 128:(k + 1) * 128],
                                   wst[:, 2 * sd + o, half * HALF:(half + 1) * HALF],
                                   start=i == 0, stop=i == len(terms) - 1)
                mm.then_inc(g_mm, 1)

        @block.scalar
        def _(act):
            for t in range(NT):
                act.wait_ge(turned, t + 1)
                act.activation(nm[0][:, t, :], bank[t % 4][:, 0:D], ACT.Copy, scale=STATE_SCALE).then_inc(nhi, 1)
            act.wait_ge(w_in, n_in)
            for k in range(2):
                act.activation(gw[0][:, own + k, :], wst[:, 4 + k, :], ACT.Copy).then_inc(hi_ok, 1)
            for n, (side, k, half) in enumerate(prods):
                act.wait_ge(g_mm, n + 1)
                act.activation(gw[0][:, 2 * side + k, half * HALF:(half + 1) * HALF], bank[n % 4][:, 0:HALF],
                               ACT.Copy).then_inc(hi_ok, 1)

        @block.vector
        def _(dve):
            c = Chain(dve, v)
            c.done(dve.reduce_sum(first3[:, :], g.ident[0:6, 0:3], AX.X))
            c.step(dve.reduce_sum(last3[:, :], g.ident[0:6, 3:6], AX.X))
            for q, (a, w) in enumerate(CHV):
                dve.wait_ge(d_mm, q + 1)
                dve.tensor_copy(deg[:, a:a + w], bank[6 + q % 2][0:6, 0:w]).then_inc(d_ok, 1)
            for t in range(NT):
                dve.wait_ge(nhi, t + 1)
                dve.scalar_tensor_tensor(out=nm[1][:, t, :], in0=bank[t % 4][:, 0:D], scalar=STATE_SCALE,
                                         in1=nm[0][:, t, :], op0=ALU.mult, op1=ALU.subtract).then_inc(nlo, 1)
            for k in range(2):
                dve.wait_ge(hi_ok, k + 1)
                dve.tensor_tensor(gw[1][:, own + k, :], wst[:, 4 + k, :], gw[0][:, own + k, :].bitcast(F32),
                                  ALU.subtract).then_inc(own_ok, 1)
            for half in range(2):
                cols = slice(half * HALF, (half + 1) * HALF)
                ps = bank[4 + half][0:6, 0:HALF]
                dve.wait_ge(b_mm, half + 1)
                c.step(dve.tensor_copy(bhi[:, cols], ps))
                c.step(dve.tensor_tensor(blo[:, cols], ps, bhi[:, cols].bitcast(F32), ALU.subtract))
                c.step(dve.tensor_scalar(blo[:, cols], blo[:, cols], last3[:, 0:1], None, ALU.mult))
                c.done(dve.scalar_tensor_tensor(out=bw[:, cols], in0=bhi[:, cols].bitcast(F32), scalar=first3[:, 0:1],
                                                in1=blo[:, cols], op0=ALU.mult, op1=ALU.add))
            for n, (side, k, half) in enumerate(prods):
                dve.wait_ge(hi_ok, n + 3)
                cols = slice(half * HALF, (half + 1) * HALF)
                dve.tensor_tensor(gw[1][:, 2 * side + k, cols], bank[n % 4][:, 0:HALF],
                                  gw[0][:, 2 * side + k, cols].bitcast(F32), ALU.subtract).then_inc(lo_ok, 1)


def gated_steps(nc, g, tag, sides, gw, bw, deg, nm):
    M = 2 * sides
    STEPS = 5
    CW = 512
    FT = [t for c in range(3) for t in [(4 * c, min(4, NT - 4 * c))]]
    with ExitStack() as ctx:
        s = Scope(nc, ctx, "step" + tag)
        uv = [[s.sb(f"uv{b}{p}", [128, M, CW], F32R) for p in range(2)] for b in range(2)]
        st = [s.sb(f"st{p}", [128, 2, CW], F32R) for p in range(2)]
        rs = [s.sb(f"rs{p}", [128, 2, CW], F32R) for p in range(2)]
        rsf, r, z = (s.sb(k, [128, 2, CW], F32) for k in ("rsf", "r", "z"))
        ht = rsf
        sums = [s.ps(f"sums{i}", [128, 512], F32) for i in range(2)]
        gate = [s.ps(f"gate{i}", [128, 512], F32) for i in range(6)]
        sums_mm, sums_hi, sums_lo = s.sem("sums_mm"), s.sem("sums_hi"), s.sem("sums_lo")
        sp_passed = s.sem("sp_passed")
        st_hi, st_lo, rz_mm, h_mm, gate_out = (s.sem(k) for k in ("st_hi", "st_lo", "rz_mm", "h_mm", "gate_out"))
        rs_ok, rs_hi, rs_lo, upd, new_ok = (s.sem(k) for k in ("rs_ok", "rs_hi", "rs_lo", "upd", "new_ok"))
        last_mm, last_hi, last_lo = (s.sem(k) for k in ("last_mm", "last_hi", "last_lo"))
        block = s.block()

        uses = [("sum", c, m) for c in range(3) for m in range(M)]
        uses += [("turn", c, q) for c in range(2) for q in range(2)]
        U = len(uses)
        number = {u: n for n, u in enumerate(uses)}

        def turn_bank(c, q):
            return (sums[number[("turn", c, q)] % 2], sums_mm) if c < 2 else (gate[q], last_mm)

        def each_step(eng, whole):
            with eng.Fori(0, STEPS - 1) as step:
                whole(step, False)
            whole(STEPS - 1, True)

        @block.gpsimd
        def _(pool):
            pool.sem_inc(sums_lo, 2)
            pool.sem_inc(gate_out, 6)
            pool.sem_inc(rz_mm, 4)
            pool.sem_inc(h_mm, 2)
            pool.sem_inc(last_lo, 2)

        @block.tensor
        def _(pe):
            def sum_tiles(c, m, tiles):
                a, w = CHV[c]
                adj, f = (g.AT if m < 2 else g.A), m % 2
                for t in tiles:
                    for p in range(2):
                        mm = pe.matmul(sums[number[("sum", c, m)] % 2][:, 0:w], nm[p][:, t, f * 128:(f + 1) * 128],
                                       adj[:, t, a:a + w], start=t + p == 0, stop=t == NT - 1 and p == 1)
                return mm

            def begin(step, m):
                pe.wait_ge(sums_lo, U * step + 2)
                sum_tiles(0, m, range(8))

            def add_up(step, c):
                for m in range(M):
                    n = number[("sum", c, m)]
                    if n < 2:
                        pe.wait_ge(last_lo, 2 * step + 2)
                        mm = sum_tiles(c, m, range(8, NT))
                    else:
                        pe.wait_ge(sums_lo, U * step + n + 1)
                        mm = sum_tiles(c, m, range(NT))
                    mm.then_inc(sums_mm, 1)

            def products(out, m, ks, parts, w, start, stop):
                n = 0
                for k, (hi, lo) in zip(ks, parts):
                    col = slice(m * 128, (m + 1) * 128)
                    for wp, x in ((gw[0], hi), (gw[0], lo), (gw[1], hi)):
                        n += 1
                        mm = pe.matmul(out[:, 0:w], wp[:, k, col], x, start=start and n == 1,
                                       stop=stop and n == 3 * len(ks))
                return mm

            def gates(step, c, turn_last_chunk):
                a, w = CHV[c]
                G = 3 * step + c
                b = c % 2
                pair = [(uv[b][0][:, k, 0:w], uv[b][1][:, k, 0:w]) for k in range(M)]
                spair = [(st[0][:, k, 0:w], st[1][:, k, 0:w]) for k in range(2)]
                rpair = [(rs[0][:, k, 0:w], rs[1][:, k, 0:w]) for k in range(2)]
                pe.wait_ge(sums_lo, U * step + number[("sum", c, M - 1)] + 3)
                pe.wait_ge(st_lo, G + 1)
                for m in range(6):
                    pe.wait_ge(gate_out, 6 * G + m + 1)
                    pe.matmul(gate[m][:, 0:w], bw[:, m * 128:(m + 1) * 128], deg[:, a:a + w], start=True, stop=False)
                    mm = products(gate[m], m, range(M), pair, w, False, False)
                    if m < 4:
                        mm = products(gate[m], m, (M, M + 1), spair, w, False, True)
                        mm.then_inc(rz_mm, 1)
                    if m == 3 and turn_last_chunk:
                        turn(step, c - 1)
                pe.wait_ge(rs_lo, G + 1)
                for m in (4, 5):
                    products(gate[m], m, (M, M + 1), rpair, w, False, True).then_inc(h_mm, 1)

            def turn(step, c):
                t0, k = FT[c]
                pe.wait_ge(new_ok, 3 * step + c + 1)
                for q in range(2):
                    bank, ok = turn_bank(c, q)
                    if c < 2:
                        pe.wait_ge(sums_lo, U * step + number[("turn", c, q)] + 1)
                    for e in range(min(2, k - 2 * q)):
                        for f in range(2):
                            t = t0 + 2 * q + e
                            mm = pe.transpose(bank[:, (2 * e + f) * 128:(2 * e + f + 1) * 128],
                                              g.hT[:, f, t * 128:(t + 1) * 128], g.ident[:, :])
                    mm.then_inc(ok, 1)

            def whole(step, last):
                add_up(step, 0)
                add_up(step, 1)
                gates(step, 0, False)
                add_up(step, 2)
                gates(step, 1, not last)
                gates(step, 2, not last)
                if not last:
                    begin(step + 1, 0)
                    turn(step, 2)
                    begin(step + 1, 1)

            begin(0, 0)
            begin(0, 1)
            each_step(pe, whole)

        @block.sync
        def _(sp):
            sp.sem_inc(sp_passed, 1)

        @block.scalar
        def _(act):
            def sums_high(step, c):
                w = CHV[c][1]
                for m in range(M):
                    n = number[("sum", c, m)]
                    act.wait_ge(sums_mm, U * step + n + 1)
                    if m == 0:
                        last = {0: 3 * step * 2, 1: (3 * step) * 2, 2: (3 * step + 1) * 2}[c]
                        act.wait_ge(h_mm, last + 2)
                    act.activation(uv[c % 2][0][:, m, 0:w], sums[n % 2][:, 0:w], ACT.Copy,
                                   scale=1.0 / STATE_SCALE).then_inc(sums_hi, 1)

            def state_high(step, c):
                a, w = CHV[c]
                G = 3 * step + c
                act.wait_ge(rz_mm, 4 * G + 4)
                act.activation(st[0][:, :, 0:w], g.hT[:, :, a:a + w], ACT.Copy).then_inc(st_hi, 1)

            def gates(step, c, turn_last_chunk):
                w = CHV[c][1]
                G = 3 * step + c
                for m in range(4):
                    act.wait_ge(rz_mm, 4 * G + m + 5)
                    if m == 2:
                        act.wait_ge(upd, 3 * G + 1)
                    act.activation((r, z)[m // 2][:, m % 2, 0:w], gate[m][:, 0:w], ACT.Sigmoid).then_inc(gate_out, 1)
                    if m == 1:
                        act.wait_ge(rs_ok, G + 1)
                        act.activation(rs[0][:, :, 0:w], rsf[:, :, 0:w], ACT.Copy).then_inc(rs_hi, 1)
                if c < 2:
                    state_high(step, c + 1)
                if turn_last_chunk:
                    turned_high(step, c - 1)
                for m in range(2):
                    act.wait_ge(h_mm, 2 * G + m + 3)
                    act.activation(ht[:, m, 0:w], gate[4 + m][:, 0:w], ACT.Tanh).then_inc(gate_out, 1)

            def turned_high(step, c):
                t0, k = FT[c]
                for q in range(2):
                    kk = min(2, k - 2 * q)
                    bank, ok = turn_bank(c, q)
                    if c < 2:
                        act.wait_ge(ok, U * step + number[("turn", c, q)] + 1)
                    else:
                        act.wait_ge(ok, 2 * step + q + 1)
                    act.activation(nm[0][:, t0 + 2 * q:t0 + 2 * q + kk, :],
                                   bank[:, 0:kk * D].rearrange("p (t f) -> p t f", f=D), ACT.Copy,
                                   scale=STATE_SCALE).then_inc(sums_hi if c < 2 else last_hi, 1)

            def whole(step, last):
                gates(step, 0, False)
                sums_high(step, 2)
                gates(step, 1, not last)
                gates(step, 2, not last)
                if not last:
                    turned_high(step, 2)
                    state_high(step + 1, 0)
                    sums_high(step + 1, 0)
                    sums_high(step + 1, 1)

            state_high(0, 0)
            sums_high(0, 0)
            sums_high(0, 1)
            each_step(act, whole)

        @block.vector
        def _(dve):
            dve.sem_inc(upd, 1)

            def sums_low(step, c):
                w = CHV[c][1]
                for m in range(M):
                    n = number[("sum", c, m)]
                    dve.wait_ge(sums_hi, U * step + n + 1)
                    dve.scalar_tensor_tensor(out=uv[c % 2][1][:, m, 0:w], in0=sums[n % 2][:, 0:w],
                                             scalar=1.0 / STATE_SCALE, in1=uv[c % 2][0][:, m, 0:w].bitcast(F32),
                                             op0=ALU.mult, op1=ALU.subtract).then_inc(sums_lo, 1)

            def state_low(step, c):
                a, w = CHV[c]
                dve.wait_ge(st_hi, 3 * step + c + 1)
                dve.tensor_tensor(st[1][:, :, 0:w], g.hT[:, :, a:a + w], st[0][:, :, 0:w].bitcast(F32),
                                  ALU.subtract).then_inc(st_lo, 1)

            def reset(step, c):
                a, w = CHV[c]
                G = 3 * step + c
                dve.wait_ge(gate_out, 6 * G + 2 + 6)
                dve.tensor_tensor(rsf[:, :, 0:w], r[:, :, 0:w], g.hT[:, :, a:a + w], ALU.mult).then_inc(rs_ok, 1)
                dve.wait_ge(rs_hi, G + 1)
                dve.tensor_tensor(rs[1][:, :, 0:w], rsf[:, :, 0:w], rs[0][:, :, 0:w].bitcast(F32),
                                  ALU.subtract).then_inc(rs_lo, 1)

            def update(step, c):
                a, w = CHV[c]
                G = 3 * step + c
                dve.wait_ge(gate_out, 6 * G + 6 + 6)
                old = g.hT[:, :, a:a + w]
                dve.tensor_tensor(ht[:, :, 0:w], ht[:, :, 0:w], old, ALU.subtract).then_inc(upd, 1)
                dve.wait_ge(upd, 3 * G + 2)
                dve.tensor_tensor(ht[:, :, 0:w], ht[:, :, 0:w], z[:, :, 0:w], ALU.mult).then_inc(upd, 1)
                dve.wait_ge(upd, 3 * G + 3)
                dve.tensor_tensor(old, old, ht[:, :, 0:w], ALU.add).then_inc(new_ok, 1)
                dve.wait_ge(new_ok, G + 1)
                dve.sem_inc(upd, 1)

            def turned_low(step, c):
                t0, k = FT[c]
                for q in range(2):
                    kk = min(2, k - 2 * q)
                    tiles = slice(t0 + 2 * q, t0 + 2 * q + kk)
                    if c < 2:
                        dve.wait_ge(sums_hi, U * step + number[("turn", c, q)] + 1)
                    else:
                        dve.wait_ge(last_hi, 2 * step + q + 1)
                    dve.scalar_tensor_tensor(out=nm[1][:, tiles, :],
                                             in0=turn_bank(c, q)[0][:, 0:kk * D].rearrange("p (t f) -> p t f", f=D),
                                             scalar=STATE_SCALE, in1=nm[0][:, tiles, :],
                                             op0=ALU.mult, op1=ALU.subtract).then_inc(sums_lo if c < 2 else last_lo, 1)

            def whole(step, last):
                sums_low(step, 0)
                sums_low(step, 1)
                reset(step, 0)
                state_low(step, 1)
                update(step, 0)
                sums_low(step, 2)
                reset(step, 1)
                state_low(step, 2)
                if not last:
                    turned_low(step, 0)
                update(step, 1)
                reset(step, 2)
                if not last:
                    turned_low(step, 1)
                update(step, 2)
                if not last:
                    turned_low(step, 2)
                    state_low(step + 1, 0)

            state_low(0, 0)
            each_step(dve, whole)


def batchnorm_out(nc, g, raw, H, O, gamma_dram, beta_dram, out_dram):
    V1 = O + 1
    with ExitStack() as ctx:
        s = Scope(nc, ctx, "bn")
        inv = s.sb("inv", [128, NT, H], F32)
        hp = s.sb("hp", [128, NT, D], F32)
        sq = s.sb("sq", [128, NT, D], F32)
        gb = s.sb("gb", [128, 2, D], F32)
        mean, scale, tmp = (s.sb(k, [128, D], F32) for k in ("mean", "scale", "tmp"))
        eps = s.sb("eps", [128, 1], F32)
        bank = [s.ps(f"bank{i}", [128, 512], F32) for i in range(2)]
        v, w_in, hp_ok, sum_mm, sq_ok, var_ok, std_ok, cen_ok, scaled, beta_ok, x_ok, stored = (
            s.sem(k) for k in ("v", "w_in", "hp_ok", "sum_mm", "sq_ok", "var_ok", "std_ok", "cen_ok", "scaled",
                               "beta_ok", "x_ok", "stored"))
        block = s.block()

        @block.sync
        def _(sp):
            sp.dma_start(gb[:, 0, :], gamma_dram.partition_broadcast(128)).then_inc(w_in, 16)
            sp.dma_start(gb[:, 1, :], beta_dram.partition_broadcast(128)).then_inc(w_in, 16)
            for t in range(NT):
                k = 128 if t < NT - 1 else TAIL
                sp.wait_ge(x_ok, t + 1)
                sp.dma_start(out_dram[t * 128:t * 128 + k, :], g.x[0:k, t, :]).then_inc(stored, 16)
            sp.wait_ge(stored, 16 * NT)

        @block.tensor
        def _(pe):
            for b, (src, ok) in enumerate(((hp, hp_ok), (sq, sq_ok))):
                for t in range(NT):
                    k = 128 if t < NT - 1 else TAIL
                    pe.wait_ge(ok, t + 1)
                    mm = pe.matmul(bank[b][:, 0:D], g.ones[0:k, :], src[0:k, t, :], start=t == 0, stop=t == NT - 1)
                mm.then_inc(sum_mm, 1)

        @block.scalar
        def _(act):
            for t in range(NT):
                act.wait_ge(cen_ok, t + 1)
                act.activation(sq[:, t, :], hp[:, t, :], ACT.Square).then_inc(sq_ok, 1)
            act.wait_ge(var_ok, 1)
            act.activation(tmp[:, :], tmp[:, :], ACT.Sqrt, bias=eps[:, 0:1]).then_inc(std_ok, 1)

        @block.vector
        def _(dve):
            c = Chain(dve, v)
            r4 = raw[:, :, :].rearrange("p t (h o) -> p t h o", o=V1)
            c.done(dve.memset(eps[:, :], 1e-5))
            c.step(dve.reciprocal(inv[:, :, :], r4[:, :, :, O]))
            for t in range(NT):
                dve.tensor_tensor(hp[:, t, :].rearrange("p (h o) -> p h o", o=O), r4[:, t, :, 0:O],
                                  inv[:, t, :].unsqueeze(2).broadcast_to([128, H, O]), ALU.mult).then_inc(hp_ok, 1)
            dve.wait_ge(sum_mm, 1)
            c.step(dve.tensor_scalar(mean[:, :], bank[0][:, 0:D], 1.0 / N, None, ALU.mult))
            for t in range(NT):
                dve.tensor_tensor(hp[:, t, :], hp[:, t, :], mean[:, :], ALU.subtract).then_inc(cen_ok, 1)
            dve.wait_ge(sum_mm, 2)
            dve.tensor_scalar(tmp[:, :], bank[1][:, 0:D], 1.0 / N, None, ALU.mult).then_inc(var_ok, 1)
            dve.wait_ge(std_ok, 1)
            dve.wait_ge(w_in, 32)
            c.step(dve.reciprocal(scale[:, :], tmp[:, :]))
            c.step(dve.tensor_tensor(scale[:, :], scale[:, :], gb[:, 0, :], ALU.mult))
            dve.wait_ge(cen_ok, NT)

            def finish(t):
                dve.wait_ge(beta_ok, t + 1)
                dve.scalar_tensor_tensor(out=g.x[:, t, :], in0=hp[:, t, :], scalar=0.0, in1=g.x[:, t, :],
                                         op0=ALU.max, op1=ALU.add).then_inc(x_ok, 1)

            for t in range(NT):
                dve.tensor_tensor(hp[:, t, :], hp[:, t, :], scale[:, :], ALU.mult).then_inc(scaled, 1)
                if t >= 2:
                    finish(t - 2)
            finish(NT - 2)
            finish(NT - 1)

        @block.gpsimd
        def _(pool):
            for t in range(NT):
                pool.wait_ge(scaled, t + 1)
                pool.tensor_tensor(hp[:, t, :], hp[:, t, :], gb[:, 1, :], ALU.add).then_inc(beta_ok, 1)


def program(nc, d, out):
    with ExitStack() as ctx:
        s = Scope(nc, ctx, "g")
        g = Graph()
        g.A = s.sb("A", [128, NT, NP], F16)
        g.AT = s.sb("AT", [128, NT, NP], F16)
        g.x = s.sb("x", [128, NT, D], F32)
        g.hT = s.sb("hT", [128, 2, NP], F32)
        g.ident = s.sb("ident", [128, 128], F32)
        g.ident16 = s.sb("ident16", [128, 128], F16)
        g.ones = s.sb("ones", [128, 128], F32)
        g.stats = s.sb("stats", [128, NT, 6], F32)
        g.mv = s.sb("mv", [128, NT, 2], F32)
        g.fewest = s.sb("fewest", [128, 1], F32)
        g.near = s.sb("near", [1, 1], I32)
        g.symmetric = s.sb("symmetric", [1, 1], I32)

        def attention_weights(scope, name, KT, H, O, w_dram, ai_dram, aj_dram):
            HO = H * O
            space = scope.sb(name + "w", [128, (KT + 2) * HO], F32)
            loads = [(space[:, 0:KT * HO].rearrange("p (k o) -> p k o", o=HO), by_partition(w_dram))]
            for n, a in enumerate((ai_dram, aj_dram)):
                k = a.shape[0]
                loads += [(space[:, i:i + k], a.partition_broadcast(128))
                          for i in range((KT + n) * HO, (KT + n + 1) * HO, k)]
            return space, loads

        def mlp_weights(scope, name, w1_dram, b1_dram, w2_dram, b2_dram):
            F = w2_dram.shape[0] // 128
            w1 = scope.sb(name + "w1", [128, 2, F * 128], F32)
            b1 = scope.sb(name + "b1", [128, F], F32)
            w2 = scope.sb(name + "w2", [128, F, D], F32)
            b2 = scope.sb(name + "b2", [128, D], F32)
            return (w1, b1, w2, b2), [(w1[:, :, :], by_partition(w1_dram)), (b1[:, :], b1_dram),
                                      (w2[:, :, :], by_partition(w2_dram)), (b2[:, :], b2_dram.partition_broadcast(128))]

        with ExitStack() as c0:
            wT = Scope(nc, c0, "l0").sb("wT", [128, 2, D], F32)
            load_graph(nc, g, d["x"], d["adj"], [(wT[:, :, :], by_partition(d["L0_WT"]))])
            cosine_attention(nc, g, wT)
        with ExitStack() as c1:
            s1 = Scope(nc, c1, "l1")
            val8 = s1.sb("val8", [128, NT, 8 * 65], F32)
            with ExitStack() as c2:
                space, loads = attention_weights(Scope(nc, c2, "l1"), "a", 2, 8, 64, d["L1_W1"], d["L1_ai"], d["L1_aj"])
                layernorm_relu(nc, g, "ln1", loads)
                gat(nc, g, "gat8", g.hT, 2, space, 8, 64, val8)
            x1T = s1.sb("x1T", [128, 4, NP], F32)
            space, loads = attention_weights(s1, "b", 4, 1, 256, d["L1_Wo"], d["L1_aoi"], d["L1_aoj"])
            normalise_elu(nc, g, "elu8", val8, 8, 64, x1T, loads)
            g.sums1 = val8[:, :, 0:257]
            gat(nc, g, "gat1", x1T, 4, space, 1, 256, val8[:, :, 257:514])
            weights, loads = mlp_weights(s1, "m", d["L1_lin1"], d["L1_b1"], d["L1_lin2"], d["L1_b2"])
            normalise_elu(nc, g, "elu1", g.sums1, 1, 256, g.hT, loads)
            mlp(nc, g, "mlp1", g.hT, weights, ACT.Relu, check_symmetry=True)
        with ExitStack() as c3:
            weights, loads = mlp_weights(Scope(nc, c3, "l2"), "m", d["o1_WT"], d["o1_b"], d["o2_WT"], d["o2_b"])
            layernorm_relu(nc, g, "ln2", loads)
            gated_graph(nc, g, d)
            mlp(nc, g, "mlp2", g.hT, weights, ACT.Tanh)
        with ExitStack() as c4:
            s3 = Scope(nc, c4, "l3")
            val3 = s3.sb("val3", [128, NT, 8 * 33], F32)
            space, loads = attention_weights(s3, "a", 2, 8, 32, d["L3_WT"], d["L3_ai"], d["L3_aj"])
            layernorm_relu(nc, g, "ln3", loads)
            gat(nc, g, "gat3", g.hT, 2, space, 8, 32, val3)
            batchnorm_out(nc, g, val3, 8, 32, d["L3_gamma"], d["L3_beta"], out)


def kernel(**inputs):
    import numpy as _np
    import concourse.bacc as _bacc
    from concourse import mybir as _mybir
    from concourse.bass_utils import run_bass_kernel_spmd as _run

    i = {k: _np.asarray(v) for k, v in inputs.items()}
    laid = {
        "x": i["x"], "adj": i["adj"], "L0_WT": i["L0_gnn_W"].T,
        "L1_W1": i["L1_gnn_W1"].transpose(1, 0, 2).reshape(256, 512),
        "L1_ai": i["L1_gnn_a1"][:, :64].reshape(512), "L1_aj": i["L1_gnn_a1"][:, 64:].reshape(512),
        "L1_Wo": i["L1_gnn_Wo"], "L1_aoi": i["L1_gnn_ao"][:256], "L1_aoj": i["L1_gnn_ao"][256:],
        "L1_lin1": i["L1_gnn_lin1_w"], "L1_b1": i["L1_gnn_lin1_b"].reshape(4, 128).T,
        "L1_lin2": i["L1_gnn_lin2_w"], "L1_b2": i["L1_gnn_lin2_b"],
        "in_W": i["L2_gnn_in_W"], "out_W": i["L2_gnn_out_W"],
        "in_b": i["L2_gnn_in_b"].reshape(2, 128).T, "out_b": i["L2_gnn_out_b"].reshape(2, 128).T,
        "r_WT": i["L2_gnn_r_W"].T, "z_WT": i["L2_gnn_z_W"].T, "h_WT": i["L2_gnn_h_W"].T,
        "r_b": i["L2_gnn_r_b"], "z_b": i["L2_gnn_z_b"], "h_b": i["L2_gnn_h_b"],
        "o1_WT": i["L2_gnn_o1_W"].T, "o1_b": i["L2_gnn_o1_b"].reshape(2, 128).T,
        "o2_WT": i["L2_gnn_o2_W"].T, "o2_b": i["L2_gnn_o2_b"],
        "L3_WT": i["L3_gnn_W"].T, "L3_ai": i["L3_gnn_a"][32:], "L3_aj": i["L3_gnn_a"][:32],
        "L3_gamma": i["L3_gnn_gamma"], "L3_beta": i["L3_gnn_beta"],
    }
    nc = _bacc.Bacc("TRN2", target_bir_lowering=False, num_devices=1)
    arrays, d = {}, {}
    for name, a in laid.items():
        a = _np.ascontiguousarray(a)
        arrays[f"in_{name}_dram"] = a
        d[name] = nc.dram_tensor(f"in_{name}_dram", a.shape, _mybir.dt.from_np(a.dtype), kind="ExternalInput").ap()
    out = nc.dram_tensor("out_dram", (1354, 256), _mybir.dt.float32, kind="ExternalOutput").ap()
    program(nc, d, out)
    r = _run(nc, [arrays], core_ids=[0])
    return r.results[0]["out_dram"]
```
